# Optimizing a Trainium2 kernel written in Bass

```python
import numpy as np
import jax
import jax.numpy as jnp

def _softmax(x, axis=-1):
    return jax.nn.softmax(x, axis=axis)

def _gelu(x):
    return jax.nn.gelu(x, approximate=True)

def _silu(x):
    return jax.nn.silu(x)

def _sigmoid(x):
    return jax.nn.sigmoid(x)

def _layernorm(x, axis=-1, eps=1e-05):
    m = jnp.mean(x, axis=axis, keepdims=True)
    v = jnp.var(x, axis=axis, keepdims=True)
    return (x - m) / jnp.sqrt(v + eps)

def _scatter_add(tgt, idx, src, axis=0):
    return tgt.at[idx].add(src)

def _segment_sum(src, seg, n):
    return jax.ops.segment_sum(src, seg, n)
kernel_name = 'mk_vit_tower_cls_d1_tok_img768_r4_0d0290'

def setup_inputs(seed: int=0):
    np.random.seed(seed)
    _w = jnp.asarray

    def _rec_inputs():
        import jax
        import jax.numpy as jnp
        _rk = jax.random.key(seed)
        x = -0.000125008 + 0.999885 * jax.random.normal(jax.random.fold_in(_rk, 1), (32, 1, 256, 256), jnp.float32)
        cls_tok = 0.02 * jax.random.normal(jax.random.fold_in(_rk, 5), (1, 1, 192), jnp.float32)
        return (x, cls_tok)
    x, cls_tok = _rec_inputs()

    def _L0_tok_setup():
        import jax, jax.numpy as jnp
        import numpy as np
        C, H, W = (1, 256, 256)
        P = 32
        D_TOK = 192
        B = 32
        D_PATCH = C * P * P

        def _patchify(x):
            Bx = x.shape[0]
            x = x.reshape(Bx, C, H // P, P, W // P, P)
            x = x.transpose(0, 2, 4, 1, 3, 5)
            return x.reshape(Bx, H // P * (W // P), D_PATCH)
        key = jax.random.key(seed)
        k_x, k_w, k_b = jax.random.split(key, 3)
        x = jax.random.normal(k_x, (B, C, H, W), dtype=jnp.float32)
        bound = 1.0 / np.sqrt(D_PATCH)
        w = jax.random.uniform(k_w, (D_TOK, D_PATCH), jnp.float32, -bound, bound)
        b = jax.random.uniform(k_b, (D_TOK,), jnp.float32, -bound, bound)
        return {'x': x, 'w': w, 'b': b}
    _L0_tok_all = _L0_tok_setup()
    _L0_tok_in = {k: v for k, v in _L0_tok_all.items() if k in ('w', 'b')}
    del _L0_tok_all

    def _L0_attn_setup():
        import jax, jax.numpy as jnp
        import numpy as np
        EMBED_DIM = 192
        NUM_HEADS = 12
        HEAD_DIM = EMBED_DIM // NUM_HEADS
        key = jax.random.key(seed)
        ks = jax.random.split(key, 9)
        d = EMBED_DIM
        s = 1.0 / np.sqrt(d)
        x = jax.random.normal(ks[0], (1, 1024, d), dtype=jnp.float32)
        wq = jax.random.uniform(ks[1], (d, d), jnp.float32, -s, s)
        bq = jax.random.uniform(ks[2], (d,), jnp.float32, -s, s)
        wk = jax.random.uniform(ks[3], (d, d), jnp.float32, -s, s)
        bk = jax.random.uniform(ks[4], (d,), jnp.float32, -s, s)
        wv = jax.random.uniform(ks[5], (d, d), jnp.float32, -s, s)
        bv = jax.random.uniform(ks[6], (d,), jnp.float32, -s, s)
        ww = jax.random.uniform(ks[7], (d, d), jnp.float32, -s, s)
        bw = jax.random.uniform(ks[8], (d,), jnp.float32, -s, s)
        return {'x': x, 'wq': wq, 'bq': bq, 'wk': wk, 'bk': bk, 'wv': wv, 'bv': bv, 'ww': ww, 'bw': bw}
    _L0_attn_all = _L0_attn_setup()
    _L0_attn_in = {k: v for k, v in _L0_attn_all.items() if k in ('wq', 'bq', 'wk', 'bk', 'wv', 'bv', 'ww', 'bw')}
    del _L0_attn_all

    def _L0_ffn_setup():
        import math
        import jax, jax.numpy as jnp
        import numpy as np
        B, L, D = (8, 1024, 192)
        E = 16
        TOP_K = 2
        F_EXP = 4 * D
        F_SH = F_EXP * 2 // 4
        key = jax.random.key(seed)
        ks = jax.random.split(key, 8)
        s = lambda fan_in: 1.0 / math.sqrt(fan_in)
        return {'hidden_states': jax.random.normal(ks[0], (B, L, D), jnp.float32), 'gate_weight': jax.random.uniform(ks[1], (E, D), jnp.float32, -s(D), s(D)), 'Wg': jax.random.uniform(ks[2], (E, F_EXP, D), jnp.float32, -s(D), s(D)), 'Wu': jax.random.uniform(ks[3], (E, F_EXP, D), jnp.float32, -s(D), s(D)), 'Wd': jax.random.uniform(ks[4], (E, D, F_EXP), jnp.float32, -s(F_EXP), s(F_EXP)), 'Ws_g': jax.random.uniform(ks[5], (F_SH, D), jnp.float32, -s(D), s(D)), 'Ws_u': jax.random.uniform(ks[6], (F_SH, D), jnp.float32, -s(D), s(D)), 'Ws_d': jax.random.uniform(ks[7], (D, F_SH), jnp.float32, -s(F_SH), s(F_SH))}
    _L0_ffn_all = _L0_ffn_setup()
    _L0_ffn_in = {k: v for k, v in _L0_ffn_all.items() if k in ('gate_weight', 'Wg', 'Wu', 'Wd', 'Ws_g', 'Ws_u', 'Ws_d')}
    del _L0_ffn_all
    return {'x': x, 'cls_tok': cls_tok, 'L0_tok_w': _L0_tok_in['w'], 'L0_tok_b': _L0_tok_in['b'], 'L0_attn_wq': _L0_attn_in['wq'], 'L0_attn_bq': _L0_attn_in['bq'], 'L0_attn_wk': _L0_attn_in['wk'], 'L0_attn_bk': _L0_attn_in['bk'], 'L0_attn_wv': _L0_attn_in['wv'], 'L0_attn_bv': _L0_attn_in['bv'], 'L0_attn_ww': _L0_attn_in['ww'], 'L0_attn_bw': _L0_attn_in['bw'], 'L0_ffn_gate_weight': _L0_ffn_in['gate_weight'], 'L0_ffn_Wg': _L0_ffn_in['Wg'], 'L0_ffn_Wu': _L0_ffn_in['Wu'], 'L0_ffn_Wd': _L0_ffn_in['Wd'], 'L0_ffn_Ws_g': _L0_ffn_in['Ws_g'], 'L0_ffn_Ws_u': _L0_ffn_in['Ws_u'], 'L0_ffn_Ws_d': _L0_ffn_in['Ws_d']}

def reference(x, cls_tok, L0_tok_w, L0_tok_b, L0_attn_wq, L0_attn_bq, L0_attn_wk, L0_attn_bk, L0_attn_wv, L0_attn_bv, L0_attn_ww, L0_attn_bw, L0_ffn_gate_weight, L0_ffn_Wg, L0_ffn_Wu, L0_ffn_Wd, L0_ffn_Ws_g, L0_ffn_Ws_u, L0_ffn_Ws_d):
    import jax
    import jax.numpy as jnp

    def _L0_tok_ref(x, w, b):
        import jax, jax.numpy as jnp
        import numpy as np
        C, H, W = (1, 256, 256)
        P = 32
        D_TOK = 192
        B = 32
        D_PATCH = C * P * P

        def _patchify(x):
            Bx = x.shape[0]
            x = x.reshape(Bx, C, H // P, P, W // P, P)
            x = x.transpose(0, 2, 4, 1, 3, 5)
            return x.reshape(Bx, H // P * (W // P), D_PATCH)
        patches = _patchify(x)
        return jnp.einsum('bld,td->blt', patches, w) + b

    def _L0_attn_ref(x, wq, bq, wk, bk, wv, bv, ww, bw):
        import jax, jax.numpy as jnp
        import numpy as np
        EMBED_DIM = 192
        NUM_HEADS = 12
        HEAD_DIM = EMBED_DIM // NUM_HEADS
        B, S, D = x.shape
        H, Hd = (NUM_HEADS, HEAD_DIM)

        def proj(w, b):
            y = x @ w.T + b
            return y.reshape(B, S, H, Hd).transpose(0, 2, 1, 3)
        q = proj(wq, bq)
        k = proj(wk, bk)
        v = proj(wv, bv)
        scores = jnp.einsum('bhqd,bhkd->bhqk', q, k) / jnp.sqrt(jnp.float32(Hd))
        attn = jax.nn.softmax(scores, axis=-1)
        out = jnp.einsum('bhqk,bhkd->bhqd', attn, v)
        out = out.transpose(0, 2, 1, 3).reshape(B, S, D)
        return out @ ww.T + bw

    def _L0_ffn_ref(hidden_states, gate_weight, Wg, Wu, Wd, Ws_g, Ws_u, Ws_d):
        import math
        import jax, jax.numpy as jnp
        import numpy as np
        B, L, D = (8, 1024, 192)
        E = 16
        TOP_K = 2
        F_EXP = 4 * D
        F_SH = F_EXP * 2 // 4
        b, l, d = hidden_states.shape
        n = b * l
        x = hidden_states.reshape(n, d)
        scores = jax.nn.sigmoid(x @ gate_weight.T)
        capacity = math.ceil(n / E * TOP_K)
        topk_score, topk_ids = jax.lax.top_k(scores.T, capacity)
        xg = x[topk_ids]
        gate = jax.nn.silu(jnp.einsum('ecd,efd->ecf', xg, Wg))
        up = jnp.einsum('ecd,efd->ecf', xg, Wu)
        out = jnp.einsum('ecf,edf->ecd', gate * up, Wd)
        out = out * topk_score[..., None]
        y = jnp.zeros((n, d), x.dtype).at[topk_ids.reshape(-1)].add(out.reshape(-1, d))
        y = y.reshape(b, l, d)
        shared = jax.nn.silu(hidden_states @ Ws_g.T) * (hidden_states @ Ws_u.T) @ Ws_d.T
        return y + shared
    h = _L0_tok_ref(x, L0_tok_w, L0_tok_b)
    h = jnp.concatenate([jnp.broadcast_to(cls_tok, (h.shape[0], 1, h.shape[2])), h], axis=1)
    h = h + _L0_attn_ref(_layernorm(h, axis=-1), L0_attn_wq, L0_attn_bq, L0_attn_wk, L0_attn_bk, L0_attn_wv, L0_attn_bv, L0_attn_ww, L0_attn_bw)
    h = h + _L0_ffn_ref(_layernorm(h, axis=-1), L0_ffn_gate_weight, L0_ffn_Wg, L0_ffn_Wu, L0_ffn_Wd, L0_ffn_Ws_g, L0_ffn_Ws_u, L0_ffn_Ws_d)
    return h

_drawn_inputs = setup_inputs


def setup_inputs(seed=0):
    import zlib

    import numpy as np

    out = dict(_drawn_inputs(seed))
    spreads = {}
    factors = {'L0_attn_bq': 6.747, 'L0_attn_bk': 8.0}
    for name, (base, spread) in spreads.items():
        noise = np.random.default_rng([zlib.crc32(name.encode()), seed]).standard_normal(out[name].shape)
        drawn = base * np.exp(spread * noise) if base else spread * noise
        out[name] = jnp.asarray(drawn.astype(out[name].dtype))
    for name, factor in factors.items():
        out[name] = (out[name] * factor).astype(out[name].dtype)
    return out
```

```python
import concourse.bass as bass
from concourse import mybir
from contextlib import ExitStack

FP32 = mybir.dt.float32
FP16 = mybir.dt.float16
U32 = mybir.dt.uint32
ALU = mybir.AluOpType
ACT = mybir.ActivationFunctionType
AX = mybir.AxisListType

IMGS = 32
PATCHES = 64
SEQ = PATCHES + 1
D = 192
DP = 96
DK = D // DP
PIX = 1024
PK = PIX // 128
TOK = IMGS * SEQ
HEADS = 12
HD = D // HEADS
HH = HEADS // DK
PAIRS = HEADS // 2
GI = 4
CHUNKS = IMGS // GI
CT = GI * SEQ
CP = GI * PATCHES
TT = 104
TILES = TOK // TT
WJ = 4
WT = WJ * TT
WIDE = TOK // WT
E = 16
TOPK = 2
CAP = -(-TOK * TOPK // E)
SLOTP = -(-CAP // 3)
THIRDS = [SLOTP, SLOTP, CAP - 2 * SLOTP]
FE = 768
FET = FE // 128
FS = 384
FST = FS // 128
ROW = D + E
BITS = 30
STEPS = BITS // WIDE
IDMID = 1040
EPS = 1e-5
VW = 2 * (HD + 1)


class Sems:

    def __init__(self, nc, ctx, stage):
        self.made, self.nc, self.ctx, self.stage = {}, nc, ctx, stage

    def __call__(self, name):
        if name not in self.made:
            self.made[name] = self.ctx.enter_context(self.nc.semaphore(f"{self.stage}_{name}"))
        return self.made[name]


def embed_stage(nc, t, a):
    with ExitStack() as ctx:
        def sb(name, shape, dt=FP32):
            return ctx.enter_context(nc.sbuf_tensor("a_" + name, shape, dt))

        s = Sems(nc, ctx, "a")
        hT, xnT, bank, bias = t["hT"], t["xnT"], t["bank"], t["bias"]
        patches = sb("patches", [128, CHUNKS, PK, CP])
        tok_w = sb("tok_w", [128, PK, D])
        xc = sb("xc", [DP, DK, CT])
        sq = sb("sq", [DP, DK, CT])
        std = sb("std", [DP, CT])
        rstd = sb("rstd", [DP, CT])
        loaded = [s(f"patches_loaded{c}") for c in range(CHUNKS)]
        emb = [bank[2 * p:2 * p + 2] for p in range(2)]
        mean_b, var_b = bank[4], bank[5]
        block = ctx.enter_context(nc.Block())

        def cols(x, c):
            return x[:, :, bass.ds(c * CT, CT)]

        @block.sync
        def _(sp):
            sp.dma_start(tok_w[:, :, :], a["tok_w"]).then_inc(s("tok_w"), 16)
            for c in range(CHUNKS):
                sp.dma_start(patches[:, c], a["patches"][c]).then_inc(loaded[c], 16)
                if c == 0:
                    sp.dma_start(bias[:, :, :], a["bias"]).then_inc(s("consts"), 16)
                    sp.dma_start(t["avg"][:, :], a["avg"]).then_inc(s("consts"), 16)
            later = ("ident", "headmask", "clsmask", "attn_w", "gate_w", "shared_gu", "shared_d", "ones", "before",
                     "iota", "ids", "restart", "bitf", "bitu")
            for name in later:
                sp.dma_start(t[name], a[name]).then_inc(s("later"), 16)
            sp.wait_ge(s("later"), 16 * len(later))

        @block.tensor
        def _(pe):
            pe.wait_ge(s("tok_w"), 16)
            pe.wait_ge(s("consts"), 32)

            def embed(c, par, m):
                if m == 0:
                    pe.wait_ge(s("chunk_go"), c + 1)
                for k in range(PK):
                    last = nc.tensor.matmul(emb[par][m][0:DP, 0:CP], tok_w[:, k, m * DP:(m + 1) * DP],
                                            patches[:, c, k, :], start=(k == 0), stop=(k == PK - 1))
                last.then_inc(s("emb_done"), 1)

            def mean(c):
                pe.wait_ge(s("h_ready"), 2 * c + 2)
                if not isinstance(c, int) or c > 0:
                    pe.wait_ge(s("xc_ready"), c)
                for m in range(DK):
                    last = nc.tensor.matmul(mean_b[0:DP, 0:CT], t["avg"][:, :], hT[:, m, bass.ds(c * CT, CT)],
                                            start=(m == 0), stop=(m == DK - 1))
                last.then_inc(s("mean_done"), 1)

            def var(c):
                pe.wait_ge(s("sq_ready"), c + 1)
                for m in range(DK):
                    last = nc.tensor.matmul(var_b[0:DP, 0:CT], t["avg"][:, :], sq[:, m, :],
                                            start=(m == 0), stop=(m == DK - 1))
                last.then_inc(s("var_done"), 1)

            def step(c, par):
                embed(c + 1, 1 - par, 0)
                mean(c)
                embed(c + 1, 1 - par, 1)
                var(c)

            embed(0, 0, 0)
            embed(0, 0, 1)
            with pe.Fori(0, (CHUNKS - 2) // 2) as it:
                for p in range(2):
                    step(it * 2 + p, p)
            step(CHUNKS - 2, 0)
            mean(CHUNKS - 1)
            var(CHUNKS - 1)

        @block.scalar
        def _(act):
            act.wait_ge(s("consts"), 32)

            def embedded(c, par):
                for m in range(DK):
                    act.wait_ge(s("emb_done"), 2 * c + m + 1)
                    dst = hT[:, m, bass.ds(c * CT, CT)].rearrange("p (b i) -> p b i", i=SEQ)[:, :, 1:SEQ]
                    src = emb[par][m][0:DP, 0:CP].rearrange("p (b i) -> p b i", i=PATCHES)
                    nc.scalar.activation(dst, src, ACT.Identity, bias=bias[:, m, 0:1]).then_inc(s("h_ready"), 1)

            def squares(c):
                act.wait_ge(s("xc_ready"), c + 1)
                nc.scalar.activation(sq[:, :, :], xc[:, :, :], ACT.Square).then_inc(s("sq_ready"), 1)

            def deviation(c):
                act.wait_ge(s("var_done"), c + 1)
                if not isinstance(c, int) or c > 0:
                    act.wait_ge(s("rstd_ready"), c)
                nc.scalar.activation(std[:, :], var_b[0:DP, 0:CT], ACT.Sqrt,
                                     bias=bias[:, 0, 6:7]).then_inc(s("std_ready"), 1)

            embedded(0, 0)
            with act.Fori(0, (CHUNKS - 2) // 2) as it:
                for p in range(2):
                    squares(it * 2 + p)
                    embedded(it * 2 + p + 1, 1 - p)
                    deviation(it * 2 + p)
            squares(CHUNKS - 2)
            embedded(CHUNKS - 1, 1)
            deviation(CHUNKS - 2)
            squares(CHUNKS - 1)
            deviation(CHUNKS - 1)

        @block.vector
        def _(dve):
            dve.wait_ge(s("consts"), 32)

            def centre(c):
                dve.wait_ge(s("mean_done"), c + 1)
                if not isinstance(c, int) or c > 0:
                    dve.wait_ge(s("xn_ready"), c)
                nc.vector.tensor_tensor(xc[:, :, :], cols(hT, c),
                                        mean_b[0:DP, 0:CT].unsqueeze(1).broadcast_to([DP, DK, CT]),
                                        ALU.subtract).then_inc(s("xc_ready"), 1)

            def normalise(c):
                dve.wait_ge(s("std_ready"), c + 1)
                nc.vector.reciprocal(rstd[:, :], std[:, :]).then_inc(s("rstd_ready"), 1)
                dve.wait_ge(s("rstd_ready"), c + 1)
                nc.vector.tensor_tensor(cols(xnT, c), xc[:, :, :],
                                        rstd[:, :].unsqueeze(1).broadcast_to([DP, DK, CT]),
                                        ALU.mult).then_inc(s("xn_ready"), 1)

            with dve.Fori(0, CHUNKS) as c:
                centre(c)
                normalise(c)

        @block.gpsimd
        def _(pool):
            pool.wait_ge(s("consts"), 32)
            for m in range(DK):
                dst = hT[:, m, :].rearrange("p (b i) -> p b i", i=SEQ)[:, :, 0]
                last = nc.gpsimd.tensor_copy(dst, bias[:, m, 5:6].broadcast_to([DP, IMGS]))
                last.then_inc(s("cls_written"), 1)
            pool.wait_ge(s("cls_written"), 2)
            for c in range(CHUNKS):
                pool.wait_ge(loaded[c], 16)
                if c >= 2:
                    pool.wait_ge(s("h_ready"), 2 * c - 2)
                pool.sem_inc(s("chunk_go"), 1)


def attention_stage(nc, t, a):
    with ExitStack() as ctx:
        def sb(name, shape, dt=FP32):
            return ctx.enter_context(nc.sbuf_tensor("b_" + name, shape, dt))

        s = Sems(nc, ctx, "b")
        hT, xnT, bank, bias, ident, w = t["hT"], t["xnT"], t["bank"], t["bias"], t["ident"], t["attn_w"]
        WQ, WK, WV, WO = range(4)
        xs = [sb(f"xs{p}", [DP, DK, GI, 2, PATCHES]) for p in range(2)]
        qT = [sb(f"qT{p}", [DP, DK, CT]) for p in range(2)]
        kT = sb("kT", [DP, DK, GI, SEQ])
        kblk = [sb(f"kblk{p}", [DP, DK, GI, HH * SEQ]) for p in range(2)]
        vblk = [[sb(f"vblk{p}{i}", [128, PAIRS, VW]) for i in range(GI)] for p in range(2)]
        vcls = sb("vcls", [HEADS, PAIRS * VW])
        prob = [sb(f"prob{p}", [SEQ, HEADS * SEQ]) for p in range(2)]
        top = sb("top", [SEQ, DK, HH])
        probT = sb("probT", [128, PAIRS, SEQ])
        probclsT = sb("probclsT", [HEADS, SEQ])
        rsum = sb("rsum", [SEQ, HEADS])
        attn = sb("attn", [SEQ, HEADS, HD])
        attnT = sb("attnT", [DP, DK, CT])
        proj_b = bank[0:2]
        score_b = t["psum"][0:SEQ, 2 * 512:4 * 512].rearrange("p (m n) -> p m n", m=2)[:, :, 0:HH * SEQ]
        pT_b = bank[4]
        av_b = bank[5][0:SEQ, 0:PAIRS * VW]
        v_b = bank[6][:, 0:D]
        aT_b = bank[7][0:DP, 0:DK * SEQ].rearrange("p (m i) -> p m i", m=DK)
        VALUES_AT = [[], [], [0, 1], [2, 3]]
        block = ctx.enter_context(nc.Block())

        def span(x, m, c):
            return x[:, m, bass.ds(c * CT, CT)]

        @block.tensor
        def _(pe):
            def keys(c, par):
                for m in range(DK):
                    if m == 0 and not (isinstance(c, int) and c == 0):
                        pe.wait_ge(s("q_ready"), 2 * c)
                    for k in range(DK):
                        last = nc.tensor.matmul(proj_b[m][0:DP, 0:CT], w[:, WK, k, m * DP:(m + 1) * DP],
                                                span(xnT, k, c), start=(k == 0), stop=(k == DK - 1))
                    last.then_inc(s("k_done"), 1)

            def queries(c, par):
                for m in range(DK):
                    if isinstance(c, int) and c < 2:
                        pe.wait_ge(s("k_ready"), 2 * c + m + 1)
                    else:
                        pe.wait_ge(s("bank_clear"), 2 * c - 3 + m)
                    for k in range(DK):
                        last = nc.tensor.matmul(proj_b[m][0:DP, 0:CT], w[:, WQ, k, m * DP:(m + 1) * DP],
                                                span(xnT, k, c), start=(k == 0), stop=(k == DK - 1))
                    last.then_inc(s("q_done"), 1)

            def values(c, par, i):
                if i == 0:
                    pe.wait_ge(s("xs_ready"), c + 1)
                if not (isinstance(c, int) and c == 0 and i == 0):
                    pe.wait_ge(s("v_ready_lo"), 4 * c + i)
                    pe.wait_ge(s("v_ready_hi"), 4 * c + i)
                for k in range(DK):
                    tok = xs[par][:, k, i].rearrange("p e n -> p (e n)")
                    last = nc.tensor.matmul(v_b, tok, w[:, WV, k, :], start=(k == 0), stop=(k == DK - 1))
                last.then_inc(s("v_done"), 1)

            def scores(c, par, i):
                if i == 0:
                    pe.wait_ge(s("q_ready"), 2 * c + 2)
                    pe.wait_ge(s("kblk_ready"), c + 1)
                if not (isinstance(c, int) and c == 0 and i == 0):
                    pe.wait_ge(s("shifted"), 4 * c + i)
                for m in range(DK):
                    last = nc.tensor.matmul(score_b[:, m, :], qT[par][:, m, i * SEQ:(i + 1) * SEQ],
                                            kblk[par][:, m, i, :], start=True, stop=True)
                last.then_inc(s("scores_done"), 1)

            def flip_probs(c, i, pi):
                pe.wait_ge(s("exp_ready"), 4 * c + i + 1)
                if not (isinstance(c, int) and c == 0 and i == 0):
                    pe.wait_ge(s("probT_ready"), 4 * c + i)
                for g in range(PAIRS):
                    nc.tensor.transpose(pT_b[:, g * SEQ:(g + 1) * SEQ], prob[pi][:, g * 128:(g + 1) * 128],
                                        ident[0:SEQ, 0:SEQ])
                nc.tensor.transpose(pT_b[0:HEADS, PAIRS * SEQ:(PAIRS + 1) * SEQ], prob[pi][:, PAIRS * 128:],
                                    ident[0:SEQ, 0:SEQ]).then_inc(s("pT_done"), 1)

            def weigh(c, par, i):
                pe.wait_ge(s("probT_ready"), 4 * c + i + 1)
                pe.wait_ge(s("v_ready_lo"), 4 * c + i + 1)
                pe.wait_ge(s("v_ready_hi"), 4 * c + i + 1)
                if not (isinstance(c, int) and c == 0 and i == 0):
                    pe.wait_ge(s("attn_ready"), 4 * c + i)
                for g in range(PAIRS):
                    nc.tensor.matmul(av_b[:, g * VW:(g + 1) * VW], probT[:, g, :], vblk[par][i][:, g, :],
                                     start=(g == 0), stop=False, skip_group_check=True)
                nc.tensor.matmul(av_b, probclsT[:, :], vcls[:, :], start=False, stop=True,
                                 skip_group_check=True).then_inc(s("av_done"), 1)

            def flip_attn(n, i, c):
                pe.wait_ge(s("attn_ready"), n + 1)
                if not (isinstance(n, int) and n == 0):
                    pe.wait_ge(s("attnT_ready"), n)
                rows = attn[:, :, :].rearrange("p h d -> p (h d)")
                for m in range(DK):
                    last = nc.tensor.transpose(aT_b[:, m, :], rows[:, m * DP:(m + 1) * DP],
                                               ident[0:SEQ, 0:SEQ])
                last.then_inc(s("aT_done"), 1)

            def output(c, last_use, value):
                pe.wait_ge(s("attnT_ready"), 4 * c + 4)
                pe.wait_ge(s(last_use), value)
                for m in range(DK):
                    for k in range(DK):
                        last = nc.tensor.matmul(proj_b[m][0:DP, 0:CT], w[:, WO, k, m * DP:(m + 1) * DP],
                                                attnT[:, k, :], start=(k == 0), stop=(k == DK - 1))
                    last.then_inc(s("o_done"), 1)

            def step(c, par, prev=True, more=True):
                for i in range(GI):
                    if i < GI - 1:
                        scores(c, par, i + 1)
                    elif more:
                        scores(c + 1, 1 - par, 0)
                    flip_probs(c, i, i % 2)
                    if i > 0:
                        flip_attn(4 * c + i - 1, i - 1, c)
                    elif prev:
                        flip_attn(4 * c - 1, GI - 1, c - 1)
                    if more:
                        if i == 0:
                            keys(c + 1, 1 - par)
                        elif i == 2:
                            queries(c + 1, 1 - par)
                        for v in VALUES_AT[i]:
                            values(c + 1, 1 - par, v)
                    if i == 1 and prev:
                        if more:
                            output(c - 1, "k_ready", 2 * c + 4)
                        else:
                            output(c - 1, "q_ready", 2 * c + 2)
                    weigh(c, par, i)

            for k in range(DK):
                last = nc.tensor.matmul(v_b[0:HEADS, :], xnT[:, k, 0:1].broadcast_to([DP, HEADS]),
                                        w[:, WV, k, :], start=(k == 0), stop=(k == DK - 1))
            last.then_inc(s("vcls_done"), 1)
            pe.wait_ge(s("vcls_ready"), 1)
            keys(0, 0)
            queries(0, 0)
            for i in range(GI):
                values(0, 0, i)
            scores(0, 0, 0)
            step(0, 0, prev=False)
            with pe.Fori(0, (CHUNKS - 2) // 2) as it:
                for p in range(2):
                    step(it * 2 + 1 + p, (1 + p) % 2)
            step(CHUNKS - 1, 1, more=False)
            flip_attn(IMGS - 1, GI - 1, CHUNKS - 1)
            output(CHUNKS - 1, "bank_clear", 2 * CHUNKS - 2)

        @block.scalar
        def _(act):
            def exponent(n, pi):
                act.wait_ge(s("shifted"), n + 1)
                nc.scalar.activation(prob[pi][:, :], prob[pi][:, :], ACT.Exp).then_inc(s("exp_ready"), 1)

            def probs_out(n):
                act.wait_ge(s("pT_done"), n + 1)
                nc.scalar.activation(probT[:, :, :].rearrange("p g q -> p (g q)"), pT_b[:, 0:PAIRS * SEQ], ACT.Identity)
                nc.scalar.activation(probclsT[:, :], pT_b[0:HEADS, PAIRS * SEQ:(PAIRS + 1) * SEQ],
                                     ACT.Identity).then_inc(s("probT_ready"), 1)

            def keys_out(c):
                for m in range(DK):
                    act.wait_ge(s("k_done"), 2 * c + m + 1)
                    if m == 0 and not (isinstance(c, int) and c == 0):
                        act.wait_ge(s("kblk_ready"), c)
                    nc.scalar.activation(kT[:, m].rearrange("p b k -> p (b k)"), proj_b[m][0:DP, 0:CT], ACT.Identity,
                                         bias=bias[:, m, 2:3]).then_inc(s("k_ready"), 1)

            def values_lo(c, par, i, first):
                act.wait_ge(s("v_done"), 4 * c + i + 1)
                if not first:
                    act.wait_ge(s("av_done"), 4 * c + i - 7)
                src = v_b[0:64, :].rearrange("p (g e d) -> p g e d", g=PAIRS, e=2)[:, :, 0, :]
                nc.scalar.activation(vblk[par][i][0:64, :, 0:HD], src, ACT.Identity).then_inc(s("v_ready_lo"), 1)

            def attn_out(n, i, c):
                act.wait_ge(s("aT_done"), n + 1)
                if i == 0 and not (isinstance(c, int) and c == 0):
                    act.wait_ge(s("o_done"), 2 * c)
                for m in range(DK):
                    last = nc.scalar.activation(attnT[:, m, i * SEQ:(i + 1) * SEQ], aT_b[:, m, :], ACT.Identity,
                                                bias=bias[:, m, 3:4])
                last.then_inc(s("attnT_ready"), 1)

            def step(c, par, prev=True, more=True, fresh=False):
                for i in range(GI):
                    exponent(4 * c + i, i % 2)
                    probs_out(4 * c + i)
                    if i > 0:
                        attn_out(4 * c + i - 1, i - 1, c)
                    elif prev:
                        attn_out(4 * c - 1, GI - 1, c - 1)
                    if more:
                        if i == 0:
                            keys_out(c + 1)
                        for v in VALUES_AT[i]:
                            values_lo(c + 1, 1 - par, v, fresh)

            keys_out(0)
            act.wait_ge(s("blocks_clear"), 1)
            for i in range(GI):
                values_lo(0, 0, i, True)
            step(0, 0, prev=False, fresh=True)
            with act.Fori(0, (CHUNKS - 2) // 2) as it:
                for p in range(2):
                    step(it * 2 + 1 + p, (1 + p) % 2)
            step(CHUNKS - 1, 1, more=False)
            attn_out(IMGS - 1, GI - 1, CHUNKS - 1)

        @block.vector
        def _(dve):
            def shift(c, i, pi):
                n = 4 * c + i
                dve.wait_ge(s("scores_done"), n + 1)
                patch = score_b[:, :, 0:HH * PATCHES].rearrange("p m (h k) -> p m h k", h=HH)
                cls = score_b[:, :, HH * PATCHES:]
                nc.vector.tensor_reduce(top[:, :, :], patch, AX.X, ALU.max).then_inc(s("patch_top"), 1)
                dve.wait_ge(s("patch_top"), n + 1)
                nc.vector.tensor_tensor(top[:, :, :], top[:, :, :], cls, ALU.max).then_inc(s("top_ready"), 1)
                dve.wait_ge(s("top_ready"), n + 1)
                if not (isinstance(c, int) and 4 * c + i < 2):
                    dve.wait_ge(s("pT_done"), n - 1)
                nc.vector.tensor_tensor(prob[pi][:, PAIRS * 128:].rearrange("p (m h) -> p m h", m=DK), cls,
                                        top[:, :, :], ALU.subtract)
                nc.vector.tensor_tensor(
                    prob[pi][:, 0:PAIRS * 128].rearrange("p (m h k) -> p m h k", m=DK, h=HH), patch,
                    top[:, :, :].unsqueeze(3).broadcast_to([SEQ, DK, HH, PATCHES]),
                    ALU.subtract).then_inc(s("shifted"), 1)

            def queries_out(c, par):
                for m in range(DK):
                    dve.wait_ge(s("q_done"), 2 * c + m + 1)
                    if m == 0 and not (isinstance(c, int) and c < 2):
                        dve.wait_ge(s("scores_done"), 4 * c - 4)
                    nc.vector.tensor_scalar(qT[par][:, m, :], proj_b[m][0:DP, 0:CT], bias[:, m, 1:2], HD ** -0.5,
                                            ALU.add, ALU.mult).then_inc(s("q_ready"), 1)

            def values_hi(c, par, i, first):
                dve.wait_ge(s("v_done"), 4 * c + i + 1)
                if not first:
                    dve.wait_ge(s("av_done"), 4 * c + i - 7)
                src = v_b[64:128, :].rearrange("p (g e d) -> p g e d", g=PAIRS, e=2)[:, :, 1, :]
                nc.vector.tensor_copy(vblk[par][i][64:128, :, HD + 1:VW - 1], src).then_inc(s("v_ready_hi"), 1)

            def attend(n):
                dve.wait_ge(s("av_done"), n + 1)
                av = av_b.rearrange("p (h d) -> p h d", h=HEADS)
                nc.vector.reciprocal(rsum[:, :], av[:, :, HD]).then_inc(s("rsum_ready"), 1)
                dve.wait_ge(s("rsum_ready"), n + 1)
                nc.vector.tensor_tensor(attn[:, :, :], av[:, :, 0:HD],
                                        rsum[:, :].unsqueeze(2).broadcast_to([SEQ, HEADS, HD]),
                                        ALU.mult).then_inc(s("attn_ready"), 1)

            def residual(c):
                for m in range(DK):
                    dve.wait_ge(s("o_done"), 2 * c + m + 1)
                    nc.vector.scalar_tensor_tensor(span(hT, m, c), proj_b[m][0:DP, 0:CT], bias[:, m, 4:5],
                                                   span(hT, m, c), ALU.add, ALU.add).then_inc(s("bank_clear"), 1)

            def step(c, par, prev=True, more=True, fresh=False):
                for i in range(GI):
                    if i < GI - 1:
                        shift(c, i + 1, (i + 1) % 2)
                    elif more:
                        shift(c + 1, 0, 0)
                    if more:
                        if i == 2:
                            queries_out(c + 1, 1 - par)
                        for v in VALUES_AT[i]:
                            values_hi(c + 1, 1 - par, v, fresh)
                    if i == 1 and prev:
                        residual(c - 1)
                    attend(4 * c + i)

            nc.vector.memset(vcls[:, :], 0.0).then_inc(s("vcls_zero"), 1)
            dve.wait_ge(s("vcls_done"), 1)
            dve.wait_ge(s("vcls_zero"), 1)
            vc = vcls[:, :].rearrange("p (h d) -> p h d", h=HEADS)
            nc.vector.tensor_tensor(vc[:, :, 0:HD], v_b[0:HEADS, :].rearrange("p (h d) -> p h d", h=HEADS),
                                    t["clsmask"][:, :].unsqueeze(2).broadcast_to([HEADS, HEADS, HD]), ALU.mult)
            nc.vector.tensor_copy(vc[:, :, HD], t["clsmask"][:, :]).then_inc(s("vcls_ready"), 1)
            queries_out(0, 0)
            dve.wait_ge(s("blocks_clear"), 1)
            for i in range(GI):
                values_hi(0, 0, i, True)
            shift(0, 0, 0)
            step(0, 0, prev=False, fresh=True)
            with dve.Fori(0, (CHUNKS - 2) // 2) as it:
                for p in range(2):
                    step(it * 2 + 1 + p, (1 + p) % 2)
            step(CHUNKS - 1, 1, more=False)
            residual(CHUNKS - 1)

        @block.gpsimd
        def _(pool):
            def copy_chunk(c, par):
                if not (isinstance(c, int) and c < 2):
                    pool.wait_ge(s("v_done"), 4 * c - 4)
                for m in range(DK):
                    src = xnT[:, m, bass.ds(c * CT, CT)].rearrange("p (b i) -> p b i", i=SEQ)[:, :, 1:SEQ]
                    last = nc.gpsimd.tensor_copy(xs[par][:, m],
                                                 src.unsqueeze(2).broadcast_to([DP, GI, 2, PATCHES]))
                last.then_inc(s("xs_ready"), 1)

            def key_blocks(c, par):
                pool.wait_ge(s("k_ready"), 2 * c + 2)
                if not (isinstance(c, int) and c < 2):
                    pool.wait_ge(s("scores_done"), 4 * c - 4)
                for m in range(DK):
                    nc.gpsimd.tensor_tensor(
                        kblk[par][:, m, :, 0:HH * PATCHES].rearrange("p b (h k) -> p b h k", h=HH),
                        kT[:, m, :, 1:SEQ].unsqueeze(2).broadcast_to([DP, GI, HH, PATCHES]),
                        t["headmask"].unsqueeze(1).unsqueeze(3).broadcast_to([DP, GI, HH, PATCHES]), ALU.mult)
                    last = nc.gpsimd.tensor_tensor(
                        kblk[par][:, m, :, HH * PATCHES:], kT[:, m, :, 0].unsqueeze(2).broadcast_to([DP, GI, HH]),
                        t["headmask"].unsqueeze(1).broadcast_to([DP, GI, HH]), ALU.mult)
                last.then_inc(s("kblk_ready"), 1)

            copy_chunk(0, 0)
            for row in vblk:
                for v in row:
                    v4 = v[:, :, :].rearrange("p g (e d) -> p g e d", e=2)
                    last = nc.gpsimd.memset(v[:, :, :], 0.0)
            last.then_inc(s("zeroed"), 1)
            pool.wait_ge(s("zeroed"), 1)
            for row in vblk:
                for v in row:
                    nc.gpsimd.memset(v[0:64, :, HD:HD + 1], 1.0)
                    last = nc.gpsimd.memset(v[64:128, :, VW - 1:VW], 1.0)
            last.then_inc(s("blocks_clear"), 1)
            pool.wait_ge(s("blocks_clear"), 1)
            key_blocks(0, 0)
            copy_chunk(1, 1)
            key_blocks(1, 1)
            with pool.Fori(0, (CHUNKS - 2) // 2) as it:
                for p in range(2):
                    copy_chunk(it * 2 + 2 + p, p)
                    key_blocks(it * 2 + 2 + p, p)


def table_stage(nc, t, a, table):
    with ExitStack() as ctx:
        def sb(name, shape, dt=FP32):
            return ctx.enter_context(nc.sbuf_tensor("c_" + name, shape, dt))

        s = Sems(nc, ctx, "c")
        hT, xnT, bank, bias, ident, rows = t["hT"], t["xnT"], t["bank"], t["bias"], t["ident"], t["rows"]
        xc = sb("xc", [DP, DK, WT])
        sq = sb("sq", [DP, DK, WT])
        std = sb("std", [DP, WT])
        rstd = sb("rstd", [DP, WT])
        xn = [sb(f"xn{p}", [DP, DK, WT]) for p in range(2)]
        mean_b, var_b = bank[0], bank[1]
        row_b = bank[2:2 + WJ]
        block = ctx.enter_context(nc.Block())

        def first(c):
            return isinstance(c, int) and c == 0

        @block.tensor
        def _(pe):
            def mean(c):
                if not first(c):
                    pe.wait_ge(s("xc_ready"), c)
                for m in range(DK):
                    last = nc.tensor.matmul(mean_b[0:DP, 0:WT], t["avg"], hT[:, m, bass.ds(c * WT, WT)],
                                            start=(m == 0), stop=(m == DK - 1))
                last.then_inc(s("mean_done"), 1)

            def var(c):
                pe.wait_ge(s("sq_ready"), c + 1)
                if not first(c):
                    pe.wait_ge(s("std_ready"), c)
                for m in range(DK):
                    last = nc.tensor.matmul(var_b[0:DP, 0:WT], t["avg"], sq[:, m, :], start=(m == 0), stop=(m == DK - 1))
                last.then_inc(s("var_done"), 1)

            def tiles(c, par, js):
                for j in js:
                    if j == 0:
                        pe.wait_ge(s("xn_ready"), c + 1)
                        if not first(c):
                            pe.wait_ge(s("row_ready"), 4 * c)
                    for k in range(DK):
                        nc.tensor.matmul(row_b[j][0:TT, D:ROW], xn[par][:, k, j * TT:(j + 1) * TT], t["gate_w"][:, k, :],
                                         start=(k == 0), stop=(k == DK - 1))
                    for k in range(DK):
                        last = nc.tensor.transpose(row_b[j][0:TT, k * DP:(k + 1) * DP],
                                                   xn[par][:, k, j * TT:(j + 1) * TT], ident[0:DP, 0:DP])
                    last.then_inc(s("tile_done"), 1)

            mean(0)
            var(0)
            with pe.Fori(0, (WIDE - 1) // 2) as it:
                for p in range(2):
                    mean(it * 2 + p + 1)
                    tiles(it * 2 + p, p, [0, 1])
                    var(it * 2 + p + 1)
                    tiles(it * 2 + p, p, [2, 3])
            tiles(WIDE - 1, 0, [0, 1, 2, 3])

        @block.scalar
        def _(act):
            def spread(c):
                act.wait_ge(s("xc_ready"), c + 1)
                nc.scalar.activation(sq[:, :, :], xc[:, :, :], ACT.Square).then_inc(s("sq_ready"), 1)
                act.wait_ge(s("var_done"), c + 1)
                if not first(c):
                    act.wait_ge(s("rstd_ready"), c)
                nc.scalar.activation(std[:, :], var_b[0:DP, 0:WT], ACT.Sqrt,
                                     bias=bias[:, 0, 6:7]).then_inc(s("std_ready"), 1)

            spread(0)
            with act.Fori(1, WIDE) as c:
                spread(c)
            act.wait_ge(s("row_ready"), TILES)
            nc.scalar.activation(rows[:, :, D:ROW], rows[:, :, D:ROW], ACT.Sigmoid).then_inc(s("score_ready"), 1)

        @block.vector
        def _(dve):
            def normalise(c, par):
                dve.wait_ge(s("mean_done"), c + 1)
                if not first(c):
                    dve.wait_ge(s("xn_ready"), c)
                nc.vector.tensor_tensor(xc[:, :, :], hT[:, :, bass.ds(c * WT, WT)],
                                        mean_b[0:DP, 0:WT].unsqueeze(1).broadcast_to([DP, DK, WT]),
                                        ALU.subtract).then_inc(s("xc_ready"), 1)
                dve.wait_ge(s("std_ready"), c + 1)
                nc.vector.reciprocal(rstd[:, :], std[:, :]).then_inc(s("rstd_ready"), 1)
                dve.wait_ge(s("rstd_ready"), c + 1)
                if not (isinstance(c, int) and c < 2):
                    dve.wait_ge(s("tile_done"), 4 * c - 4)
                    dve.wait_ge(s("kept"), c - 1)
                nc.vector.tensor_tensor(xn[par][:, :, :], xc[:, :, :],
                                        rstd[:, :].unsqueeze(1).broadcast_to([DP, DK, WT]),
                                        ALU.mult).then_inc(s("xn_ready"), 1)

            def copy_rows(c):
                for j in range(WJ):
                    dve.wait_ge(s("tile_done"), 4 * c + j + 1)
                    nc.vector.tensor_copy(rows[:, c * WJ + j, :], row_b[j][0:TT, 0:ROW]).then_inc(s("row_ready"), 1)

            normalise(0, 0)
            normalise(1, 1)
            copy_rows(0)
            normalise(2, 0)
            copy_rows(1)
            with dve.Fori(1, (WIDE - 1) // 2) as it:
                for p in range(2):
                    normalise(it * 2 + p + 1, 1 - p)
                    copy_rows(it * 2 + p)
            copy_rows(WIDE - 1)

        @block.gpsimd
        def _(pool):
            def keep(c, par):
                pool.wait_ge(s("xn_ready"), c + 1)
                nc.gpsimd.tensor_copy(xnT[:, :, bass.ds(c * WT, WT)], xn[par][:, :, :]).then_inc(s("kept"), 1)

            with pool.Fori(0, (WIDE - 1) // 2) as it:
                for p in range(2):
                    keep(it * 2 + p, p)
            keep(WIDE - 1, 0)

        @block.sync
        def _(sp):
            sp.wait_ge(s("score_ready"), 1)
            sp.dma_start(table.rearrange("(i t) r -> t i r", t=TT), rows).then_inc(s("table_out"), 16)
            sp.wait_ge(s("table_out"), 16)


def shared_stage(nc, t, a, out):
    with ExitStack() as ctx:
        def sb(name, shape, dt=FP32):
            return ctx.enter_context(nc.sbuf_tensor("d_" + name, shape, dt))

        s = Sems(nc, ctx, "d")
        hT, xnT, bank, ident, rows, limit = t["hT"], t["xnT"], t["bank"], t["ident"], t["rows"], t["limit"]
        wgu, wd = t["shared_gu"], t["shared_d"]
        hc = [sb(f"hc{p}", [DP, DK, WT]) for p in range(2)]
        gate = [sb(f"gate{p}", [128, WT]) for p in range(2)]
        hid = sb("hid", [128, FST, WT])
        base = [sb(f"base{p}", [TT, D]) for p in range(2)]
        reach = sb("reach", [TT, TILES, E], FP16)
        part = sb("part", [TT, E], FP16)
        back = sb("back", [TT, E], U32)
        gate_b, up_b = bank[0:2], bank[2:4]
        down_b = bank[4:6]
        count_b = bank[6][0:TT, 0:E]
        score = rows[:, :, D:ROW]
        block = ctx.enter_context(nc.Block())

        def first(c):
            return isinstance(c, int) and c == 0

        @block.sync
        def _(sp):
            def store(c, js):
                for j in js:
                    sp.wait_ge(s("base_ready"), 4 * c + j + 1)
                    sp.dma_start(out[bass.ds((c * WJ + j) * TT, TT), :], base[j % 2][:, :]).then_inc(s(f"base_out{j % 2}"), 16)

            store(0, range(WJ))
            with sp.Fori(1, WIDE) as c:
                store(c, range(WJ))
            for p in range(2):
                sp.wait_ge(s(f"base_out{p}"), 16 * TILES // 2)

        @block.tensor
        def _(pe):
            def gate_up(c, f, n):
                for g, b, read in ((0, gate_b, "gate_ready"), (1, up_b, "hid_ready")):
                    if not (isinstance(n, int) and n < 2):
                        pe.wait_ge(s(read), n - 1)
                    for k in range(DK):
                        last = nc.tensor.matmul(b[f % 2][:, 0:WT], wgu[:, g, k, f * 128:(f + 1) * 128],
                                                xnT[:, k, bass.ds(c * WT, WT)], start=(k == 0), stop=(k == DK - 1))
                    last.then_inc(s("gate_done" if g == 0 else "up_done"), 1)

            def down(c, par, j):
                if j == 0:
                    pe.wait_ge(s("hid_ready"), 3 * c + 3)
                    pe.wait_ge(s("hc_ready"), c + 1)
                if not (first(c) and j < 2):
                    pe.wait_ge(s("base_ready"), 4 * c + j - 1)
                b = down_b[j % 2][0:TT, 0:D]
                for f in range(FST):
                    nc.tensor.matmul(b, hid[:, f, j * TT:(j + 1) * TT], wd[:, f, :], start=(f == 0), stop=False,
                                     skip_group_check=True)
                for k in range(DK):
                    last = nc.tensor.matmul(b[:, k * DP:(k + 1) * DP], hc[par][:, k, j * TT:(j + 1) * TT],
                                            ident[0:DP, 0:DP], start=False, stop=(k == DK - 1), skip_group_check=True)
                last.then_inc(s("down_done"), 1)

            def count(n):
                pe.wait_ge(s("part_ready"), n + 1)
                nc.tensor.matmul(count_b, t["ones"][0:TT, 0:TT], part[:, :], start=True,
                                 stop=True).then_inc(s("counted"), 1)

            def chunk(c, par):
                for q in range(STEPS):
                    if q < FST:
                        gate_up(c, q, c * FST + q)
                    elif q < STEPS - 1:
                        down(c, par, q - FST)
                    else:
                        for j in range(STEPS - 1 - FST, WJ):
                            down(c, par, j)
                    count(c * STEPS + q)

            chunk(0, 0)
            with pe.Fori(0, (WIDE - 1) // 2) as it:
                for p in range(2):
                    chunk(it * 2 + 1 + p, 1 - p)

        @block.scalar
        def _(act):
            def chunk(c):
                for f in range(FST):
                    n = c * FST + f
                    act.wait_ge(s("gate_done"), n + 1)
                    if not (isinstance(n, int) and n < 2):
                        act.wait_ge(s("hid_ready"), n - 1)
                    nc.scalar.activation(gate[f % 2][:, :], gate_b[f % 2][:, 0:WT], ACT.Silu).then_inc(s("gate_ready"), 1)
                for j in range(WJ):
                    act.wait_ge(s("down_done"), 4 * c + j + 1)
                    if not (first(c) and j < 2):
                        act.wait_ge(s(f"base_out{j % 2}"), 16 * (2 * c + j // 2))
                    nc.scalar.activation(base[j % 2][:, :], down_b[j % 2][0:TT, 0:D],
                                         ACT.Identity).then_inc(s("base_ready"), 1)

            chunk(0)
            with act.Fori(1, WIDE) as c:
                chunk(c)

        @block.vector
        def _(dve):
            def reached(n):
                nc.vector.tensor_tensor(reach[:, :, :], score, limit.bitcast(FP32).unsqueeze(1).broadcast_to([TT, TILES, E]),
                                        ALU.is_ge).then_inc(s("reach_ready"), 1)
                dve.wait_ge(s("reach_ready"), n + 1)
                if not (isinstance(n, int) and n == 0):
                    dve.wait_ge(s("counted"), n)
                with nc.allow_low_precision(reason="counts up to TILES are exact"):
                    nc.vector.tensor_reduce(part[:, :], reach[:, :, :].rearrange("p i e -> p e i"), AX.X,
                                            ALU.add).then_inc(s("part_ready"), 1)

            def settle(n):
                dve.wait_ge(s("counted"), n + 1)
                nc.vector.tensor_scalar(back[:, :], count_b, float(CAP), t["bitf"][:, bass.ds(n, 1)], ALU.is_lt,
                                        ALU.mult).then_inc(s("back_ready"), 1)
                dve.wait_ge(s("back_ready"), n + 1)
                nc.vector.scalar_tensor_tensor(limit, back[:, :], t["bitu"][:, bass.ds(n, 1)], limit, ALU.bitwise_or,
                                               ALU.bitwise_xor).then_inc(s("limit_ready"), 1)
                dve.wait_ge(s("limit_ready"), n + 2)

            def hidden(c, f):
                n = c * FST + f
                dve.wait_ge(s("gate_ready"), n + 1)
                dve.wait_ge(s("up_done"), n + 1)
                if f == 0 and not first(c):
                    dve.wait_ge(s("down_done"), 4 * c)
                nc.vector.tensor_tensor(hid[:, f, :], gate[f % 2][:, :], up_b[f % 2][:, 0:WT],
                                        ALU.mult).then_inc(s("hid_ready"), 1)

            def chunk(c):
                for q in range(STEPS):
                    reached(c * STEPS + q)
                    if q < FST:
                        hidden(c, q)
                    settle(c * STEPS + q)

            nc.vector.memset(limit, 1 << (BITS - 1)).then_inc(s("limit_ready"), 1)
            dve.wait_ge(s("limit_ready"), 1)
            chunk(0)
            with dve.Fori(1, WIDE) as c:
                chunk(c)

        @block.gpsimd
        def _(pool):
            def chunk(c, par):
                if not (isinstance(c, int) and c < 2):
                    pool.wait_ge(s("down_done"), 4 * c - 4)
                nc.gpsimd.tensor_copy(hc[par][:, :, :], hT[:, :, bass.ds(c * WT, WT)]).then_inc(s("hc_ready"), 1)

            chunk(0, 0)
            chunk(1, 1)
            chunk(2, 0)
            with pool.Fori(1, (WIDE - 1) // 2) as it:
                for p in range(2):
                    chunk(it * 2 + 1 + p, 1 - p)


def slot_stage(nc, t, a):
    with ExitStack() as ctx:
        def sb(name, shape, dt=FP32):
            return ctx.enter_context(nc.sbuf_tensor("e_" + name, shape, dt))

        s = Sems(nc, ctx, "e")
        bank, rows, limit = t["bank"], t["rows"], t["limit"]
        N = E * TILES
        above = sb("above", [TT, N], FP16)
        equal = sb("equal", [TT, N], FP16)
        run = [sb(f"run{i}", [TT, N], FP16) for i in range(2)]
        room = sb("room", [TT, E])
        rank = sb("rank", [TT, N])
        fits = sb("fits", [TT, N])
        slot = sb("slot", [TT, N])
        third = sb("third", [TT, N])
        third2 = sb("third2", [TT, N])
        above_b, equal_b, total_b = bank[0][0:TT, 0:N], bank[1][0:TT, 0:N], bank[2][0:TT, 0:E]
        score = rows[:, :, D:ROW].rearrange("p i e -> p e i")
        lim = limit.bitcast(FP32).unsqueeze(2).broadcast_to([TT, E, TILES])
        block = ctx.enter_context(nc.Block())

        def by_expert(x):
            return x.rearrange("p (e i) -> p e i", e=E)

        @block.vector
        def _(dve):
            done = [0]

            def then(ins):
                done[0] += 1
                ins.then_inc(s("step"), 1)
                dve.wait_ge(s("step"), done[0])

            nc.vector.tensor_tensor(by_expert(above[:, :]), score, lim, ALU.is_gt)
            then(nc.vector.tensor_tensor(by_expert(equal[:, :]), score, lim, ALU.is_equal))
            for m, r in ((above, run[0]), (equal, run[1])):
                last = nc.vector.tensor_tensor_scan(r[:, :], t["restart"], m[:, :], 0.0, ALU.mult, ALU.add)
            last.then_inc(s("run_ready"), 1)
            dve.wait_ge(s("ranked"), 1)
            then(nc.vector.tensor_scalar(room[:, :], total_b, -1.0, float(CAP), ALU.mult, ALU.add))
            then(nc.vector.tensor_copy(rank[:, :], equal_b))
            room_bc = room[:, :].unsqueeze(2).broadcast_to([TT, E, TILES])
            then(nc.vector.tensor_tensor(by_expert(fits[:, :]), by_expert(rank[:, :]), room_bc, ALU.is_lt))
            then(nc.vector.tensor_tensor(fits[:, :], fits[:, :], equal[:, :], ALU.mult))
            then(nc.vector.tensor_tensor(fits[:, :], fits[:, :], above[:, :], ALU.add))
            then(nc.vector.tensor_tensor(by_expert(rank[:, :]), by_expert(rank[:, :]), room_bc, ALU.min))
            then(nc.vector.tensor_tensor(slot[:, :], above_b, rank[:, :], ALU.add))
            then(nc.vector.scalar_tensor_tensor(slot[:, :], slot[:, :], 1.0, fits[:, :], ALU.add, ALU.mult))
            then(nc.vector.tensor_scalar(slot[:, :], slot[:, :], -1.0, None, ALU.add))
            then(nc.vector.tensor_scalar(third[:, :], slot[:, :], float(SLOTP), None, ALU.is_ge))
            then(nc.vector.tensor_scalar(third2[:, :], slot[:, :], float(2 * SLOTP), None, ALU.is_ge))
            then(nc.vector.tensor_tensor(third[:, :], third[:, :], third2[:, :], ALU.add))
            then(nc.vector.scalar_tensor_tensor(t["slotp"], third[:, :], -float(SLOTP), slot[:, :], ALU.mult, ALU.add))
            for b in range(3):
                last = nc.vector.scalar_tensor_tensor(
                    t["slotid"][:, :, :, b], by_expert(third[:, :]), float(b),
                    t["ids"].unsqueeze(1).broadcast_to([TT, E, TILES]), ALU.is_equal, ALU.mult)
            then(last)

        @block.tensor
        def _(pe):
            pe.wait_ge(s("run_ready"), 1)
            for m, r, b in ((above, run[0], above_b), (equal, run[1], equal_b)):
                nc.tensor.matmul(b, t["ones"][0:TT, 0:TT], r[:, :], start=True, stop=False)
                nc.tensor.matmul(b, t["before"], m[:, :], start=False, stop=True)
            nc.tensor.matmul(total_b, t["ones"][0:TT, 0:TT], by_expert(run[0][:, :])[:, :, TILES - 1], start=True,
                             stop=True).then_inc(s("ranked"), 1)


def expert_stage(nc, t, a, table, out):
    with ExitStack() as ctx:
        def sb(name, shape, dt=FP32):
            return ctx.enter_context(nc.sbuf_tensor("f_" + name, shape, dt))

        s = Sems(nc, ctx, "f")
        bank, ident = t["bank"], t["ident"]
        wgu = [sb(f"wgu{p}", [DP, 2, DK, FE]) for p in range(2)]
        wd = [sb(f"wd{p}", [128, FET, D]) for p in range(2)]
        hot = [sb(f"hot{p}", [TT, TILES, SLOTP], FP16) for p in range(2)]
        ids = [sb(f"ids{p}", [SLOTP, 3], U32) for p in range(2)]
        ids_out = [sb(f"ids_out{p}", [SLOTP, 3], U32) for p in range(2)]
        got = [sb(f"got{p}", [SLOTP, 3, ROW]) for p in range(2)]
        score = [sb(f"score{p}", [SLOTP, 3]) for p in range(2)]
        xT = sb("xT", [DP, DK, CAP])
        gate = [sb(f"gate{p}", [128, CAP]) for p in range(2)]
        hid = sb("hid", [128, FET, CAP])
        y = [sb(f"y{p}", [SLOTP, 3, D]) for p in range(2)]
        gate_b, up_b = bank[0:2], bank[2:4]
        x_b = bank[4:6]
        down_b = [bank[6][:, 0:D], bank[7][:, 0:D], bank[4][:, 0:D]]
        ids_b = bank[7][0:SLOTP, 256:259]
        block = ctx.enter_context(nc.Block())

        def least(e, n):
            return isinstance(e, int) and e < n

        def loads_of(e, p):
            return 8 * (e - p) + 16

        def experts(eng, body):
            for e in range(2):
                body(e, e, True, True)
            with eng.Fori(1, E // 2 - 1) as it:
                for p in range(2):
                    body(it * 2 + p, p, True, True)
            body(E - 2, 0, True, False)
            body(E - 1, 1, False, False)

        @block.sync
        def _(sp):
            def load(e, p):
                if not least(e, 2):
                    sp.wait_ge(s("up_done"), FET * (e - 1))
                sp.dma_start(wgu[p][:, :, :, :], a["expert_gu"][e]).then_inc(s(f"gu_loaded{p}"), 16)
                if not least(e, 2):
                    sp.wait_ge(s("down_done"), 3 * (e - 1))
                sp.dma_start(wd[p][:, :, :], a["expert_d"][e]).then_inc(s(f"d_loaded{p}"), 16)

            load(0, 0)
            load(1, 1)
            with sp.Fori(1, E // 2) as it:
                for p in range(2):
                    load(it * 2 + p, p)

        @block.tensor
        def _(pe):
            def list_tokens(e, p):
                pe.wait_ge(s("hot_ready"), e + 1)
                if not least(e, 1):
                    pe.wait_ge(s("ids_ready"), e)
                if not least(e, 2):
                    pe.wait_ge(s("y_ready"), 3 * (e - 1) - 3)
                for i in range(TILES):
                    last = nc.tensor.matmul(ids_b, hot[p][:, i, :], t["slotid"][:, e, i, :], start=(i == 0),
                                            stop=(i == TILES - 1))
                last.then_inc(s("ids_done"), 1)

            def flip_rows(e, p):
                for b in range(3):
                    pe.wait_ge(s(f"got{b}{p}"), loads_of(e, p))
                if not least(e, 1):
                    pe.wait_ge(s("xT_ready"), 2 * e)
                if not least(e, 2):
                    pe.wait_ge(s("y_ready"), 3 * e - 3)
                for k in range(DK):
                    for b in range(3):
                        n = THIRDS[b]
                        last = nc.tensor.transpose(x_b[k][0:DP, b * SLOTP:b * SLOTP + n],
                                                   got[p][0:n, b, k * DP:(k + 1) * DP], ident[0:n, 0:n])
                    last.then_inc(s("x_done"), 1)

            def gate_up(e, p):
                pe.wait_ge(s("xT_ready"), 2 * e + 2)
                pe.wait_ge(s(f"gu_loaded{p}"), loads_of(e, p))
                for f in range(FET):
                    n = e * FET + f
                    for g, b, read in ((0, gate_b, "gate_ready"), (1, up_b, "hid_ready")):
                        if not least(n, 2):
                            pe.wait_ge(s(read), n - 1)
                        for k in range(DK):
                            last = nc.tensor.matmul(b[f % 2][:, 0:CAP], wgu[p][:, g, k, f * 128:(f + 1) * 128],
                                                    xT[:, k, :], start=(k == 0), stop=(k == DK - 1))
                        last.then_inc(s("gate_done" if g == 0 else "up_done"), 1)

            def down(e, p, one, two):
                pe.wait_ge(s("hid_ready"), FET * e + FET)
                pe.wait_ge(s(f"d_loaded{p}"), loads_of(e, p))
                for b in range(3):
                    if b == 1 and two:
                        pe.wait_ge(s("ids_ready"), e + 3)
                    if b == 2 and one:
                        pe.wait_ge(s("xT_ready"), 2 * e + 4)
                    if not least(e, 1):
                        pe.wait_ge(s("y_ready"), 3 * e - 2 + b)
                    n = THIRDS[b]
                    for f in range(FET):
                        last = nc.tensor.matmul(down_b[b][0:n, :], hid[:, f, b * SLOTP:b * SLOTP + n], wd[p][:, f, :],
                                                start=(f == 0), stop=(f == FET - 1))
                    last.then_inc(s("down_done"), 1)

            def body(e, p, one, two):
                gate_up(e, p)
                if one:
                    flip_rows(e + 1, 1 - p)
                if two:
                    list_tokens(e + 2, p)
                down(e, p, one, two)

            list_tokens(0, 0)
            list_tokens(1, 1)
            flip_rows(0, 0)
            experts(pe, body)

        @block.scalar
        def _(act):
            def body(e, p, one, two):
                for f in range(FET):
                    n = e * FET + f
                    act.wait_ge(s("gate_done"), n + 1)
                    if not least(n, 2):
                        act.wait_ge(s("hid_ready"), n - 1)
                    nc.scalar.activation(gate[f % 2][:, :], gate_b[f % 2][:, 0:CAP], ACT.Silu).then_inc(s("gate_ready"), 1)
                if one:
                    rows_in(e + 1)

            def rows_in(e):
                for k in range(DK):
                    act.wait_ge(s("x_done"), 2 * e + k + 1)
                    if k == 0 and not least(e, 1):
                        act.wait_ge(s("up_done"), FET * e)
                    nc.scalar.activation(xT[:, k, :], x_b[k][0:DP, 0:CAP], ACT.Identity).then_inc(s("xT_ready"), 1)

            rows_in(0)
            experts(act, body)

        @block.vector
        def _(dve):
            def one_hot(e, p):
                if not least(e, 2):
                    dve.wait_ge(s("ids_done"), e - 1)
                col = t["slotp"][:, bass.ds(e * TILES, TILES)]
                nc.vector.tensor_tensor(hot[p][:, :, :], t["iota"].unsqueeze(1).broadcast_to([TT, TILES, SLOTP]),
                                        col.unsqueeze(2).broadcast_to([TT, TILES, SLOTP]),
                                        ALU.is_equal).then_inc(s("hot_ready"), 1)

            def token_ids(e, p):
                dve.wait_ge(s("ids_done"), e + 1)
                if not least(e, 2):
                    for b in range(3):
                        dve.wait_ge(s(f"got{b}{p}"), loads_of(e, p) - 16)
                nc.vector.tensor_scalar(ids[p][:, :], ids_b, float(IDMID), None, ALU.add).then_inc(s("ids_ready"), 1)

            def keep_score(e, p):
                for b in range(3):
                    dve.wait_ge(s(f"got{b}{p}"), loads_of(e, p))
                if not least(e, 2):
                    dve.wait_ge(s("y_ready"), 3 * e - 3)
                    dve.wait_ge(s(f"added{p}"), 24 * (e - p))
                nc.vector.tensor_copy(ids_out[p][:, :], ids[p][:, :])
                nc.vector.tensor_copy(score[p][:, 0:2], got[p][:, 0:2, bass.ds(e + D, 1)].rearrange("p b o -> p (b o)"))
                nc.vector.tensor_copy(score[p][0:THIRDS[2], 2:3],
                                      got[p][0:THIRDS[2], 2, bass.ds(e + D, 1)]).then_inc(s("score_kept"), 1)

            def body(e, p, one, two):
                for f in range(FET):
                    n = e * FET + f
                    dve.wait_ge(s("gate_ready"), n + 1)
                    dve.wait_ge(s("up_done"), n + 1)
                    if f == 0 and not least(e, 1):
                        dve.wait_ge(s("down_done"), 3 * e)
                    nc.vector.tensor_tensor(hid[:, f, :], gate[f % 2][:, :], up_b[f % 2][:, 0:CAP],
                                            ALU.mult).then_inc(s("hid_ready"), 1)
                    if f == 1 and two:
                        one_hot(e + 2, p)
                if two:
                    token_ids(e + 2, p)
                if not least(e, 2):
                    dve.wait_ge(s(f"added{p}"), 24 * (e - p))
                dve.wait_ge(s("score_kept"), e + 1)
                for b in range(3):
                    dve.wait_ge(s("down_done"), 3 * e + b + 1)
                    n = THIRDS[b]
                    nc.vector.tensor_scalar(y[p][0:n, b, :], down_b[b][0:n, :], score[p][0:n, b:b + 1], None,
                                            ALU.mult).then_inc(s("y_ready"), 1)
                if one:
                    keep_score(e + 1, 1 - p)

            for e in range(2):
                one_hot(e, e)
                token_ids(e, e)
            keep_score(0, 0)
            experts(dve, body)

        @block.gpsimd
        def _(pool):
            def gather(e, p):
                pool.wait_ge(s("ids_ready"), e + 1)
                if not least(e, 2):
                    pool.wait_ge(s("score_kept"), e - 1)
                    pool.wait_ge(s("x_done"), 2 * (e - 1))
                pool.sem_inc(s("gathers"), 1)
                for b in range(3):
                    n = THIRDS[b]
                    nc.gpsimd.indirect_dma_start(
                        out=got[p][0:n, b, :], out_offset=None, in_=table,
                        in_offset=bass.IndirectOffsetOnAxis(ap=ids[p][0:n, b:b + 1], axis=0)).then_inc(s(f"got{b}{p}"), 16)

            def add(e, p):
                pool.wait_ge(s("y_ready"), 3 * e + 3)
                if not least(e, 1):
                    pool.wait_ge(s(f"added{1 - p}"), 24 * (e - p) + (0 if p == 0 else 48))
                pool.sem_inc(s("adds"), 1)
                for b in range(3):
                    n = THIRDS[b]
                    nc.gpsimd.indirect_dma_start(
                        out=out, out_offset=bass.IndirectOffsetOnAxis(ap=ids_out[p][0:n, b:b + 1], axis=0),
                        in_=y[p][0:n, b, :], in_offset=None, compute_op=ALU.add).then_inc(s(f"added{p}"), 16)

            def body(e, p, one, two):
                if two:
                    gather(e + 2, p)
                add(e, p)

            gather(0, 0)
            gather(1, 1)
            experts(pool, body)
            for p in range(2):
                pool.wait_ge(s(f"added{p}"), 16 * 3 * E // 2)


def tower(nc, a, table, out):
    with ExitStack() as ctx:
        def sb(name, shape, dt=FP32):
            return ctx.enter_context(nc.sbuf_tensor(name, shape, dt))[tuple(slice(None) for _ in shape)]

        psum = ctx.enter_context(nc.psum_tensor("psum", [128, 8 * 512], FP32))
        t = {
            "psum": psum,
            "bank": [psum[:, 512 * i:512 * (i + 1)] for i in range(8)],
            "hT": sb("hT", [DP, DK, TOK]),
            "xnT": sb("xnT", [DP, DK, TOK]),
            "rows": sb("rows", [TT, TILES, ROW]),
            "limit": sb("limit", [TT, E], U32),
            "slotp": sb("slotp", [TT, E * TILES]),
            "slotid": sb("slotid", [TT, E, TILES, 3], FP16),
        }
        for name in ("bias", "avg", "ident", "headmask", "clsmask", "attn_w", "gate_w", "shared_gu", "shared_d", "ones",
                     "before", "iota", "ids", "restart", "bitf", "bitu"):
            t[name] = sb("s_" + name, list(a[name].shape), a[name].dtype)
        embed_stage(nc, t, a)
        attention_stage(nc, t, a)
        table_stage(nc, t, a, table)
        shared_stage(nc, t, a, out)
        slot_stage(nc, t, a)
        expert_stage(nc, t, a, table, out)


def layouts(x, cls_tok, L0_tok_w, L0_tok_b, L0_attn_wq, L0_attn_bq, L0_attn_wk, L0_attn_bk, L0_attn_wv, L0_attn_bv,
            L0_attn_ww, L0_attn_bw, L0_ffn_gate_weight, L0_ffn_Wg, L0_ffn_Wu, L0_ffn_Wd, L0_ffn_Ws_g, L0_ffn_Ws_u,
            L0_ffn_Ws_d):
    import numpy as np

    def halves(m):
        return np.asarray(m).T.reshape(DK, DP, -1).transpose(1, 0, 2)

    def blocks(m):
        return np.asarray(m).T.reshape(-1, 128, D).transpose(1, 0, 2)

    P = 32
    patches = np.asarray(x).reshape(CHUNKS, GI, 8, P, 8, P).transpose(0, 3, 5, 1, 2, 4)
    patches = patches.reshape(CHUNKS, PK, 128, CP).transpose(0, 2, 1, 3)
    bias = np.zeros((DP, DK, 8), np.float32)
    for n, v in enumerate((L0_tok_b, L0_attn_bq, L0_attn_bk, L0_attn_bv, L0_attn_bw, cls_tok)):
        bias[:, :, n] = np.asarray(v).reshape(DK, DP).T
    bias[:, :, 6] = EPS
    at = np.arange(128)
    bits = [1 << (BITS - 1 - n) for n in range(BITS)] + [0]
    restart = np.ones((TT, E, TILES), np.float32)
    restart[:, :, 0] = 0
    tt = np.arange(TT)
    return {
        "patches": patches,
        "tok_w": np.asarray(L0_tok_w).T.reshape(PK, 128, D).transpose(1, 0, 2),
        "bias": bias,
        "attn_w": np.stack([halves(m) for m in (L0_attn_wq, L0_attn_wk, L0_attn_wv, L0_attn_ww)], 1),
        "gate_w": halves(L0_ffn_gate_weight),
        "shared_gu": np.stack([halves(L0_ffn_Ws_g), halves(L0_ffn_Ws_u)], 1),
        "shared_d": blocks(L0_ffn_Ws_d),
        "expert_gu": np.stack([np.asarray(m).transpose(0, 2, 1).reshape(E, DK, DP, FE).transpose(0, 2, 1, 3)
                               for m in (L0_ffn_Wg, L0_ffn_Wu)], 2),
        "expert_d": np.asarray(L0_ffn_Wd).transpose(0, 2, 1).reshape(E, FET, 128, D).transpose(0, 2, 1, 3),
        "avg": np.full((DP, DP), 1 / D, np.float32),
        "ident": np.eye(128, dtype=np.float32),
        "headmask": (np.arange(DP)[:, None] // HD == np.arange(HH)).astype(np.float32),
        "clsmask": np.eye(HEADS, dtype=np.float32),
        "ones": np.ones((128, 128), np.float16),
        "before": -(tt[:, None] >= tt[None, :]).astype(np.float16),
        "iota": np.tile(np.arange(SLOTP, dtype=np.float16), (TT, 1)),
        "ids": (np.arange(TILES)[None, :] * TT + tt[:, None] - IDMID).astype(np.float16),
        "restart": restart.reshape(TT, -1),
        "bitf": np.tile(np.array(bits[:-1], np.float32), (TT, 1)),
        "bitu": np.tile(np.array(bits[1:], np.uint32), (TT, 1)),
    }


def kernel(**inputs):
    import numpy as np
    import concourse.bacc as bacc
    from concourse.bass_utils import run_bass_kernel_spmd

    nc = bacc.Bacc("TRN2", target_bir_lowering=False, num_devices=1)
    arrays, a = {}, {}
    for name, v in layouts(**inputs).items():
        arrays[name + "_in"] = v = np.ascontiguousarray(v)
        a[name] = nc.dram_tensor(name + "_in", v.shape, mybir.dt.from_np(v.dtype), kind="ExternalInput").ap()
    table = nc.dram_tensor("table", (TOK, ROW), FP32, kind="Internal").ap()
    out = nc.dram_tensor("y_out", (TOK, D), FP32, kind="ExternalOutput").ap()
    tower(nc, a, table, out)
    r = run_bass_kernel_spmd(nc, [arrays], core_ids=[0])
    return r.results[0]["y_out"].reshape(IMGS, SEQ, D)
```

```python
import concourse.bass as bass
from concourse import mybir
from contextlib import ExitStack

FP32 = mybir.dt.float32
FP32R = mybir.dt.float32r
FP16 = mybir.dt.float16
U32 = mybir.dt.uint32
ALU = mybir.AluOpType
ACT = mybir.ActivationFunctionType
AX = mybir.AxisListType

IMGS = 32
PATCHES = 64
SEQ = PATCHES + 1
D = 192
DP = 96
DK = D // DP
PIX = 1024
PK = PIX // 128
TOK = IMGS * SEQ
HEADS = 12
HD = D // HEADS
HH = HEADS // DK
PAIRS = HEADS // 2
GI = 4
CHUNKS = IMGS // GI
CT = GI * SEQ
CP = GI * PATCHES
TT = 104
TILES = TOK // TT
WJ = 4
WT = WJ * TT
WIDE = TOK // WT
NJ = 2
NT = NJ * TT
NARROW = TOK // NT
E = 16
TOPK = 2
CAP = -(-TOK * TOPK // E)
SLOTP = -(-CAP // 3)
THIRDS = [SLOTP, SLOTP, CAP - 2 * SLOTP]
FE = 768
FET = FE // 128
FS = 384
FST = FS // 128
MAIN = 128
TAIL = D - MAIN
TURN = MAIN + 2 * TAIL
ROW = TURN + E
BITS = 30
STEPS = BITS // WIDE
IDMID = 1040
EPS = 1e-5
VW = 2 * (HD + 1)


class Sems:

    def __init__(self, nc, ctx, stage):
        self.made, self.nc, self.ctx, self.stage = {}, nc, ctx, stage

    def __call__(self, name):
        if name not in self.made:
            self.made[name] = self.ctx.enter_context(self.nc.semaphore(f"{self.stage}_{name}"))
        return self.made[name]


def stay_awake(nc, t, bank, n):
    for _ in range(n):
        nc.tensor.matmul(bank[:, 0:512], t["ones"], t["ones"].unsqueeze(1).broadcast_to([128, 4, 128]), start=True,
                         stop=True)


def embed_stage(nc, t, a):
    with ExitStack() as ctx:
        def sb(name, shape, dt=FP32):
            return ctx.enter_context(nc.sbuf_tensor("a_" + name, shape, dt))

        s = Sems(nc, ctx, "a")
        hT, xnT, bank, bias = t["hT"], t["xnT"], t["bank"], t["bias"]
        patches = sb("patches", [128, CHUNKS, PK, CP])
        tok_w = sb("tok_w", [128, PK, D])
        xc = sb("xc", [DP, DK, CT])
        sq = sb("sq", [DP, DK, CT])
        std = sb("std", [DP, CT])
        rstd = sb("rstd", [DP, CT])
        loaded = [s(f"patches_loaded{c}") for c in range(CHUNKS)]
        emb = [bank[2 * p:2 * p + 2] for p in range(2)]
        mean_b, var_b = bank[4], bank[5]
        block = ctx.enter_context(nc.Block())

        def cols(x, c):
            return x[:, :, bass.ds(c * CT, CT)]

        @block.sync
        def _(sp):
            sp.dma_start(tok_w[:, :, :], a["tok_w"]).then_inc(s("tok_w"), 16)
            for c in range(CHUNKS):
                sp.dma_start(patches[:, c], a["patches"][c]).then_inc(loaded[c], 16)
                if c == 0:
                    sp.dma_start(bias[:, :, :], a["bias"]).then_inc(s("consts"), 16)
                    sp.dma_start(t["avg"][:, :], a["avg"]).then_inc(s("consts"), 16)
                    sp.dma_start(t["ones"], a["ones"]).then_inc(s("consts"), 16)
            later = ("ident", "headmask", "clsmask", "attn_w", "gate_w", "shared_gu", "shared_d", "before",
                     "iota", "ids", "restart", "bitf", "bitu")
            for name in later:
                sp.dma_start(t[name], a[name]).then_inc(s("later"), 16)
            for e in range(2):
                sp.dma_start(t[f"gu_raw{e}"], a["expert_gu"][e]).then_inc(s("experts"), 16)
                sp.dma_start(t[f"d_raw{e}"], a["expert_d"][e]).then_inc(s("experts"), 16)
            sp.wait_ge(s("later"), 16 * len(later))
            sp.wait_ge(s("experts"), 16 * 4)

        @block.tensor
        def _(pe):
            pe.wait_ge(s("tok_w"), 16)
            pe.wait_ge(s("consts"), 48)

            def embed(c, par, m):
                if m == 0:
                    pe.wait_ge(s("chunk_go"), c + 1)
                for k in range(PK):
                    last = nc.tensor.matmul(emb[par][m][0:DP, 0:CP], tok_w[:, k, m * DP:(m + 1) * DP],
                                            patches[:, c, k, :], start=(k == 0), stop=(k == PK - 1))
                last.then_inc(s("emb_done"), 1)

            def mean(c):
                pe.wait_ge(s("h_ready"), 2 * c + 2)
                if not isinstance(c, int) or c > 0:
                    pe.wait_ge(s("xc_ready"), c)
                for m in range(DK):
                    last = nc.tensor.matmul(mean_b[0:DP, 0:CT], t["avg"][:, :], hT[:, m, bass.ds(c * CT, CT)],
                                            start=(m == 0), stop=(m == DK - 1))
                last.then_inc(s("mean_done"), 1)

            def var(c):
                pe.wait_ge(s("sq_ready"), c + 1)
                for m in range(DK):
                    last = nc.tensor.matmul(var_b[0:DP, 0:CT], t["avg"][:, :], sq[:, m, :],
                                            start=(m == 0), stop=(m == DK - 1))
                last.then_inc(s("var_done"), 1)

            def step(c, par):
                embed(c + 1, 1 - par, 0)
                mean(c)
                embed(c + 1, 1 - par, 1)
                var(c)

            embed(0, 0, 0)
            embed(0, 0, 1)
            with pe.Fori(0, (CHUNKS - 2) // 2) as it:
                for p in range(2):
                    step(it * 2 + p, p)
            step(CHUNKS - 2, 0)
            mean(CHUNKS - 1)
            stay_awake(nc, t, bank[6], 8)
            var(CHUNKS - 1)
            stay_awake(nc, t, bank[6], 22)

        @block.scalar
        def _(act):
            act.wait_ge(s("consts"), 48)

            def embedded(c, par):
                for m in range(DK):
                    act.wait_ge(s("emb_done"), 2 * c + m + 1)
                    dst = hT[:, m, bass.ds(c * CT, CT)].rearrange("p (b i) -> p b i", i=SEQ)[:, :, 1:SEQ]
                    src = emb[par][m][0:DP, 0:CP].rearrange("p (b i) -> p b i", i=PATCHES)
                    nc.scalar.activation(dst, src, ACT.Identity, bias=bias[:, m, 0:1]).then_inc(s("h_ready"), 1)

            def squares(c):
                act.wait_ge(s("xc_ready"), c + 1)
                nc.scalar.activation(sq[:, :, :], xc[:, :, :], ACT.Square).then_inc(s("sq_ready"), 1)

            def deviation(c):
                act.wait_ge(s("var_done"), c + 1)
                if not isinstance(c, int) or c > 0:
                    act.wait_ge(s("rstd_ready"), c)
                nc.scalar.activation(std[:, :], var_b[0:DP, 0:CT], ACT.Sqrt,
                                     bias=bias[:, 0, 6:7]).then_inc(s("std_ready"), 1)

            embedded(0, 0)
            with act.Fori(0, (CHUNKS - 2) // 2) as it:
                for p in range(2):
                    squares(it * 2 + p)
                    embedded(it * 2 + p + 1, 1 - p)
                    deviation(it * 2 + p)
            squares(CHUNKS - 2)
            embedded(CHUNKS - 1, 1)
            deviation(CHUNKS - 2)
            squares(CHUNKS - 1)
            deviation(CHUNKS - 1)

        @block.vector
        def _(dve):
            dve.wait_ge(s("consts"), 48)

            def centre(c):
                dve.wait_ge(s("mean_done"), c + 1)
                if not isinstance(c, int) or c > 0:
                    dve.wait_ge(s("xn_ready"), c)
                nc.vector.tensor_tensor(xc[:, :, :], cols(hT, c),
                                        mean_b[0:DP, 0:CT].unsqueeze(1).broadcast_to([DP, DK, CT]),
                                        ALU.subtract).then_inc(s("xc_ready"), 1)

            def normalise(c):
                dve.wait_ge(s("std_ready"), c + 1)
                nc.vector.reciprocal(rstd[:, :], std[:, :]).then_inc(s("rstd_ready"), 1)
                dve.wait_ge(s("rstd_ready"), c + 1)
                nc.vector.tensor_tensor(cols(xnT, c), xc[:, :, :],
                                        rstd[:, :].unsqueeze(1).broadcast_to([DP, DK, CT]),
                                        ALU.mult).then_inc(s("xn_ready"), 1)

            with dve.Fori(0, CHUNKS) as c:
                centre(c)
                normalise(c)

        @block.gpsimd
        def _(pool):
            pool.wait_ge(s("consts"), 48)
            for m in range(DK):
                dst = hT[:, m, :].rearrange("p (b i) -> p b i", i=SEQ)[:, :, 0]
                last = nc.gpsimd.tensor_copy(dst, bias[:, m, 5:6].broadcast_to([DP, IMGS]))
                last.then_inc(s("cls_written"), 1)
            pool.wait_ge(s("cls_written"), 2)
            for c in range(CHUNKS):
                pool.wait_ge(loaded[c], 16)
                if c >= 2:
                    pool.wait_ge(s("h_ready"), 2 * c - 2)
                pool.sem_inc(s("chunk_go"), 1)


def attention_stage(nc, t, a):
    with ExitStack() as ctx:
        def sb(name, shape, dt=FP32):
            return ctx.enter_context(nc.sbuf_tensor("b_" + name, shape, dt))

        s = Sems(nc, ctx, "b")
        hT, xnT, bank, bias, ident, w = t["hT"], t["xnT"], t["bank"], t["bias"], t["ident"], t["attn_w"]
        WQ, WK, WV, WO = range(4)
        xs = [sb(f"xs{p}", [DP, DK, GI, 2, PATCHES]) for p in range(2)]
        qT = [sb(f"qT{p}", [DP, DK, CT]) for p in range(2)]
        kT = sb("kT", [DP, DK, GI, SEQ])
        kblk = [sb(f"kblk{p}", [DP, DK, GI, HH * SEQ]) for p in range(2)]
        vblk = [sb(f"vblk{p}", [128, GI, PAIRS, VW]) for p in range(2)]
        vcls = sb("vcls", [HEADS, PAIRS * VW])
        prob = [sb(f"prob{p}", [SEQ, HEADS * SEQ]) for p in range(2)]
        top = sb("top", [SEQ, DK, HH])
        probT = sb("probT", [128, PAIRS, SEQ])
        probclsT = sb("probclsT", [HEADS, SEQ])
        rsum = sb("rsum", [SEQ, HEADS])
        attn = sb("attn", [SEQ, HEADS, HD])
        attnT = sb("attnT", [DP, DK, CT])
        proj_b = bank[0:2]
        score_b = t["psum"][0:SEQ, 2 * 512:4 * 512].rearrange("p (m n) -> p m n", m=2)[:, :, 0:HH * SEQ]
        pT_b = bank[4]
        av_b = bank[5][0:SEQ, 0:PAIRS * VW]
        v_b = bank[6][:, 0:2 * D].rearrange("p (i d) -> p i d", i=2)
        aT_b = bank[7][0:DP, 0:DK * SEQ].rearrange("p (m i) -> p m i", m=DK)
        VALUES_AT = [[], [], [0], [1]]
        block = ctx.enter_context(nc.Block())

        def span(x, m, c):
            return x[:, m, bass.ds(c * CT, CT)]

        def key_block(eng, par, m):
            eng.tensor_tensor(
                kblk[par][:, m, :, 0:HH * PATCHES].rearrange("p b (h k) -> p b h k", h=HH),
                kT[:, m, :, 1:SEQ].unsqueeze(2).broadcast_to([DP, GI, HH, PATCHES]),
                t["headmask"].unsqueeze(1).unsqueeze(3).broadcast_to([DP, GI, HH, PATCHES]), ALU.mult)
            return eng.tensor_tensor(
                kblk[par][:, m, :, HH * PATCHES:], kT[:, m, :, 0].unsqueeze(2).broadcast_to([DP, GI, HH]),
                t["headmask"].unsqueeze(1).broadcast_to([DP, GI, HH]), ALU.mult)

        @block.tensor
        def _(pe):
            def keys(c, par):
                for m in range(DK):
                    if m == 0 and not (isinstance(c, int) and c == 0):
                        pe.wait_ge(s("q_ready"), 2 * c)
                    for k in range(DK):
                        last = nc.tensor.matmul(proj_b[m][0:DP, 0:CT], w[:, WK, k, m * DP:(m + 1) * DP],
                                                span(xnT, k, c), start=(k == 0), stop=(k == DK - 1))
                    last.then_inc(s("k_done"), 1)

            def queries(c, par):
                for m in range(DK):
                    if isinstance(c, int) and c < 2:
                        pe.wait_ge(s("k_ready"), 2 * c + m + 1)
                    else:
                        pe.wait_ge(s("bank_clear"), 2 * c - 3 + m)
                    for k in range(DK):
                        last = nc.tensor.matmul(proj_b[m][0:DP, 0:CT], w[:, WQ, k, m * DP:(m + 1) * DP],
                                                span(xnT, k, c), start=(k == 0), stop=(k == DK - 1))
                    last.then_inc(s("q_done"), 1)

            def values(c, par, q):
                if q == 0:
                    pe.wait_ge(s("xs_ready"), c + 1)
                if not (isinstance(c, int) and c == 0 and q == 0):
                    pe.wait_ge(s("v_ready_lo"), 2 * c + q)
                    pe.wait_ge(s("v_ready_hi"), 2 * c + q)
                for i in range(2):
                    for k in range(DK):
                        tok = xs[par][:, k, 2 * q + i].rearrange("p e n -> p (e n)")
                        last = nc.tensor.matmul(v_b[:, i, :], tok, w[:, WV, k, :], start=(k == 0), stop=(k == DK - 1))
                last.then_inc(s("v_done"), 1)

            def scores(c, par, i):
                if i == 0:
                    pe.wait_ge(s("q_ready"), 2 * c + 2)
                    if isinstance(c, int) and c == 0:
                        pe.wait_ge(s("kblk_first"), 2)
                    else:
                        pe.wait_ge(s("kblk_ready"), c)
                if not (isinstance(c, int) and c == 0 and i == 0):
                    pe.wait_ge(s("shifted"), 4 * c + i)
                for m in range(DK):
                    last = nc.tensor.matmul(score_b[:, m, :], qT[par][:, m, i * SEQ:(i + 1) * SEQ],
                                            kblk[par][:, m, i, :], start=True, stop=True)
                last.then_inc(s("scores_done"), 1)

            def flip_probs(c, i, pi):
                pe.wait_ge(s("exp_ready"), 4 * c + i + 1)
                if not (isinstance(c, int) and c == 0 and i == 0):
                    pe.wait_ge(s("probT_ready"), 4 * c + i)
                for g in range(PAIRS):
                    nc.tensor.transpose(pT_b[:, g * SEQ:(g + 1) * SEQ], prob[pi][:, g * 128:(g + 1) * 128],
                                        ident[0:SEQ, 0:SEQ])
                nc.tensor.transpose(pT_b[0:HEADS, PAIRS * SEQ:(PAIRS + 1) * SEQ], prob[pi][:, PAIRS * 128:],
                                    ident[0:SEQ, 0:SEQ]).then_inc(s("pT_done"), 1)

            def weigh(c, par, i):
                pe.wait_ge(s("probT_ready"), 4 * c + i + 1)
                if i % 2 == 0:
                    pe.wait_ge(s("v_ready_lo"), 2 * c + i // 2 + 1)
                    pe.wait_ge(s("v_ready_hi"), 2 * c + i // 2 + 1)
                if not (isinstance(c, int) and c == 0 and i == 0):
                    pe.wait_ge(s("attn_ready"), 4 * c + i)
                for g in range(PAIRS):
                    nc.tensor.matmul(av_b[:, g * VW:(g + 1) * VW], probT[:, g, :], vblk[par][:, i, g, :],
                                     start=(g == 0), stop=False, skip_group_check=True)
                nc.tensor.matmul(av_b, probclsT[:, :], vcls[:, :], start=False, stop=True,
                                 skip_group_check=True).then_inc(s("av_done"), 1)

            def flip_attn(n, i, c):
                pe.wait_ge(s("attn_ready"), n + 1)
                if not (isinstance(n, int) and n == 0):
                    pe.wait_ge(s("attnT_ready"), n)
                rows = attn[:, :, :].rearrange("p h d -> p (h d)")
                for m in range(DK):
                    last = nc.tensor.transpose(aT_b[:, m, :], rows[:, m * DP:(m + 1) * DP],
                                               ident[0:SEQ, 0:SEQ])
                last.then_inc(s("aT_done"), 1)

            def output(c, last_use, value):
                pe.wait_ge(s("attnT_ready"), 4 * c + 4)
                pe.wait_ge(s(last_use), value)
                for m in range(DK):
                    for k in range(DK):
                        last = nc.tensor.matmul(proj_b[m][0:DP, 0:CT], w[:, WO, k, m * DP:(m + 1) * DP],
                                                attnT[:, k, :], start=(k == 0), stop=(k == DK - 1))
                    last.then_inc(s("o_done"), 1)

            def step(c, par, prev=True, more=True):
                for i in range(GI):
                    if i < GI - 1:
                        scores(c, par, i + 1)
                    elif more:
                        scores(c + 1, 1 - par, 0)
                    flip_probs(c, i, i % 2)
                    if i > 0:
                        flip_attn(4 * c + i - 1, i - 1, c)
                    elif prev:
                        flip_attn(4 * c - 1, GI - 1, c - 1)
                    if more:
                        if i == 0:
                            keys(c + 1, 1 - par)
                        elif i == 2:
                            queries(c + 1, 1 - par)
                        for v in VALUES_AT[i]:
                            values(c + 1, 1 - par, v)
                    if i == 1 and prev:
                        if more:
                            output(c - 1, "k_ready", 2 * c + 4)
                        else:
                            output(c - 1, "q_ready", 2 * c + 2)
                    if i >= 2 and not more:
                        stay_awake(nc, t, bank[6], 5)
                    weigh(c, par, i)

            for k in range(DK):
                last = nc.tensor.matmul(v_b[0:HEADS, 0, :], xnT[:, k, 0:1].broadcast_to([DP, HEADS]),
                                        w[:, WV, k, :], start=(k == 0), stop=(k == DK - 1))
            last.then_inc(s("vcls_done"), 1)
            pe.wait_ge(s("vcls_ready"), 1)
            keys(0, 0)
            queries(0, 0)
            for q in range(2):
                values(0, 0, q)
            scores(0, 0, 0)
            step(0, 0, prev=False)
            with pe.Fori(0, (CHUNKS - 2) // 2) as it:
                for p in range(2):
                    step(it * 2 + 1 + p, (1 + p) % 2)
            step(CHUNKS - 1, 1, more=False)
            stay_awake(nc, t, bank[6], 4)
            flip_attn(IMGS - 1, GI - 1, CHUNKS - 1)
            stay_awake(nc, t, bank[6], 5)
            output(CHUNKS - 1, "bank_clear", 2 * CHUNKS - 2)
            stay_awake(nc, t, bank[6], 8)

        @block.scalar
        def _(act):
            def exponent(n, pi):
                act.wait_ge(s("shifted"), n + 1)
                nc.scalar.activation(prob[pi][:, :], prob[pi][:, :], ACT.Exp).then_inc(s("exp_ready"), 1)

            def probs_out(n):
                act.wait_ge(s("pT_done"), n + 1)
                nc.scalar.activation(probT[:, :, :].rearrange("p g q -> p (g q)"), pT_b[:, 0:PAIRS * SEQ], ACT.Identity)
                nc.scalar.activation(probclsT[:, :], pT_b[0:HEADS, PAIRS * SEQ:(PAIRS + 1) * SEQ],
                                     ACT.Identity).then_inc(s("probT_ready"), 1)

            def keys_out(c):
                for m in range(DK):
                    act.wait_ge(s("k_done"), 2 * c + m + 1)
                    if m == 0 and isinstance(c, int) and c == 1:
                        act.wait_ge(s("kblk_first"), 2)
                    elif m == 0 and not (isinstance(c, int) and c == 0):
                        act.wait_ge(s("kblk_ready"), c - 1)
                    nc.scalar.activation(kT[:, m].rearrange("p b k -> p (b k)"), proj_b[m][0:DP, 0:CT], ACT.Identity,
                                         bias=bias[:, m, 2:3]).then_inc(s("k_ready"), 1)

            def values_lo(c, par, q, first):
                act.wait_ge(s("v_done"), 2 * c + q + 1)
                if not first:
                    act.wait_ge(s("av_done"), 4 * c + 2 * q - 6)
                src = v_b[0:64].rearrange("p i (g e d) -> p i g e d", g=PAIRS, e=2)[:, :, :, 0, :]
                nc.scalar.activation(vblk[par][0:64, 2 * q:2 * q + 2, :, 0:HD], src,
                                     ACT.Identity).then_inc(s("v_ready_lo"), 1)

            def attn_out(n, i, c):
                act.wait_ge(s("aT_done"), n + 1)
                if i == 0 and not (isinstance(c, int) and c == 0):
                    act.wait_ge(s("o_done"), 2 * c)
                for m in range(DK):
                    last = nc.scalar.activation(attnT[:, m, i * SEQ:(i + 1) * SEQ], aT_b[:, m, :], ACT.Identity,
                                                bias=bias[:, m, 3:4])
                last.then_inc(s("attnT_ready"), 1)

            def step(c, par, prev=True, more=True, fresh=False):
                for i in range(GI):
                    exponent(4 * c + i, i % 2)
                    probs_out(4 * c + i)
                    if i > 0:
                        attn_out(4 * c + i - 1, i - 1, c)
                    elif prev:
                        attn_out(4 * c - 1, GI - 1, c - 1)
                    if more:
                        if i == 0:
                            keys_out(c + 1)
                        for v in VALUES_AT[i]:
                            values_lo(c + 1, 1 - par, v, fresh)

            for m in range(DK):
                src = xnT[:, m, 0:CT].rearrange("p (b i) -> p b i", i=SEQ)[:, :, 1:SEQ]
                for e in range(2):
                    last = nc.scalar.activation(xs[0][:, m, :, e, :], src, ACT.Identity)
            last.then_inc(s("xs_ready"), 1)
            nc.scalar.activation(t["d_hi0"], t["d_raw0"], ACT.Identity)
            keys_out(0)
            nc.scalar.activation(t["gu_hi0"], t["gu_raw0"], ACT.Identity).then_inc(s("expert_hi"), 1)
            act.wait_ge(s("blocks_clear"), 1)
            for q in range(2):
                values_lo(0, 0, q, True)
            step(0, 0, prev=False, fresh=True)
            with act.Fori(0, (CHUNKS - 2) // 2) as it:
                for p in range(2):
                    step(it * 2 + 1 + p, (1 + p) % 2)
            step(CHUNKS - 1, 1, more=False)
            attn_out(IMGS - 1, GI - 1, CHUNKS - 1)

        @block.vector
        def _(dve):
            def shift(c, i, pi):
                n = 4 * c + i
                dve.wait_ge(s("scores_done"), n + 1)
                patch = score_b[:, :, 0:HH * PATCHES].rearrange("p m (h k) -> p m h k", h=HH)
                cls = score_b[:, :, HH * PATCHES:]
                nc.vector.tensor_reduce(top[:, :, :], patch, AX.X, ALU.max).then_inc(s("patch_top"), 1)
                dve.wait_ge(s("patch_top"), n + 1)
                nc.vector.tensor_tensor(top[:, :, :], top[:, :, :], cls, ALU.max).then_inc(s("top_ready"), 1)
                dve.wait_ge(s("top_ready"), n + 1)
                if not (isinstance(c, int) and 4 * c + i < 2):
                    dve.wait_ge(s("pT_done"), n - 1)
                nc.vector.tensor_tensor(prob[pi][:, PAIRS * 128:].rearrange("p (m h) -> p m h", m=DK), cls,
                                        top[:, :, :], ALU.subtract)
                nc.vector.tensor_tensor(
                    prob[pi][:, 0:PAIRS * 128].rearrange("p (m h k) -> p m h k", m=DK, h=HH), patch,
                    top[:, :, :].unsqueeze(3).broadcast_to([SEQ, DK, HH, PATCHES]),
                    ALU.subtract).then_inc(s("shifted"), 1)

            def queries_out(c, par):
                for m in range(DK):
                    dve.wait_ge(s("q_done"), 2 * c + m + 1)
                    if m == 0 and not (isinstance(c, int) and c < 2):
                        dve.wait_ge(s("scores_done"), 4 * c - 4)
                    nc.vector.tensor_scalar(qT[par][:, m, :], proj_b[m][0:DP, 0:CT], bias[:, m, 1:2], HD ** -0.5,
                                            ALU.add, ALU.mult).then_inc(s("q_ready"), 1)

            def values_hi(c, par, q, first):
                dve.wait_ge(s("v_done"), 2 * c + q + 1)
                if not first:
                    dve.wait_ge(s("av_done"), 4 * c + 2 * q - 6)
                src = v_b[64:128].rearrange("p i (g e d) -> p i g e d", g=PAIRS, e=2)[:, :, :, 1, :]
                nc.vector.tensor_copy(vblk[par][64:128, 2 * q:2 * q + 2, :, HD + 1:VW - 1],
                                      src).then_inc(s("v_ready_hi"), 1)

            def attend(n):
                dve.wait_ge(s("av_done"), n + 1)
                av = av_b.rearrange("p (h d) -> p h d", h=HEADS)
                nc.vector.reciprocal(rsum[:, :], av[:, :, HD]).then_inc(s("rsum_ready"), 1)
                dve.wait_ge(s("rsum_ready"), n + 1)
                nc.vector.tensor_tensor(attn[:, :, :], av[:, :, 0:HD],
                                        rsum[:, :].unsqueeze(2).broadcast_to([SEQ, HEADS, HD]),
                                        ALU.mult).then_inc(s("attn_ready"), 1)

            def residual(c):
                for m in range(DK):
                    dve.wait_ge(s("o_done"), 2 * c + m + 1)
                    nc.vector.scalar_tensor_tensor(span(hT, m, c), proj_b[m][0:DP, 0:CT], bias[:, m, 4:5],
                                                   span(hT, m, c), ALU.add, ALU.add).then_inc(s("bank_clear"), 1)

            def step(c, par, prev=True, more=True, fresh=False):
                for i in range(GI):
                    if i < GI - 1:
                        shift(c, i + 1, (i + 1) % 2)
                    elif more:
                        shift(c + 1, 0, 0)
                    if more:
                        if i == 2:
                            queries_out(c + 1, 1 - par)
                        for v in VALUES_AT[i]:
                            values_hi(c + 1, 1 - par, v, fresh)
                    if i == 1 and prev:
                        residual(c - 1)
                    attend(4 * c + i)

            nc.vector.memset(vcls[:, :], 0.0).then_inc(s("vcls_zero"), 1)
            dve.wait_ge(s("vcls_done"), 1)
            dve.wait_ge(s("vcls_zero"), 1)
            vc = vcls[:, :].rearrange("p (h d) -> p h d", h=HEADS)
            nc.vector.tensor_tensor(vc[:, :, 0:HD], v_b[0:HEADS, 0, :].rearrange("p (h d) -> p h d", h=HEADS),
                                    t["clsmask"][:, :].unsqueeze(2).broadcast_to([HEADS, HEADS, HD]), ALU.mult)
            nc.vector.tensor_copy(vc[:, :, HD], t["clsmask"][:, :]).then_inc(s("vcls_ready"), 1)
            dve.wait_ge(s("k_ready"), 1)
            key_block(nc.vector, 0, 0).then_inc(s("kblk_first"), 1)
            queries_out(0, 0)
            dve.wait_ge(s("blocks_clear"), 1)
            for q in range(2):
                values_hi(0, 0, q, True)
            shift(0, 0, 0)
            step(0, 0, prev=False, fresh=True)
            with dve.Fori(0, (CHUNKS - 2) // 2) as it:
                for p in range(2):
                    step(it * 2 + 1 + p, (1 + p) % 2)
            step(CHUNKS - 1, 1, more=False)
            residual(CHUNKS - 1)

        @block.gpsimd
        def _(pool):
            def copy_chunk(c, par):
                if not (isinstance(c, int) and c < 2):
                    pool.wait_ge(s("v_done"), 2 * c - 2)
                for m in range(DK):
                    src = xnT[:, m, bass.ds(c * CT, CT)].rearrange("p (b i) -> p b i", i=SEQ)[:, :, 1:SEQ]
                    last = nc.gpsimd.tensor_copy(xs[par][:, m],
                                                 src.unsqueeze(2).broadcast_to([DP, GI, 2, PATCHES]))
                last.then_inc(s("xs_ready"), 1)

            def key_blocks(c, par):
                pool.wait_ge(s("k_ready"), 2 * c + 2)
                if not (isinstance(c, int) and c < 2):
                    pool.wait_ge(s("scores_done"), 4 * c - 4)
                for m in range(DK):
                    last = key_block(nc.gpsimd, par, m)
                last.then_inc(s("kblk_ready"), 1)

            for v in vblk:
                last = nc.gpsimd.memset(v[:, :, :, :], 0.0)
            last.then_inc(s("zeroed"), 1)
            pool.wait_ge(s("zeroed"), 1)
            for v in vblk:
                nc.gpsimd.memset(v[0:64, :, :, HD:HD + 1], 1.0)
                last = nc.gpsimd.memset(v[64:128, :, :, VW - 1:VW], 1.0)
            last.then_inc(s("blocks_clear"), 1)
            pool.wait_ge(s("blocks_clear"), 1)
            pool.wait_ge(s("k_ready"), 2)
            key_block(nc.gpsimd, 0, 1).then_inc(s("kblk_first"), 1)
            copy_chunk(1, 1)
            key_blocks(1, 1)
            with pool.Fori(0, (CHUNKS - 2) // 2) as it:
                for p in range(2):
                    copy_chunk(it * 2 + 2 + p, p)
                    key_blocks(it * 2 + 2 + p, p)
            pool.wait_ge(s("expert_hi"), 1)
            nc.gpsimd.tensor_tensor(t["gu_lo0"], t["gu_raw0"], t["gu_hi0"].bitcast(FP32), ALU.subtract)
            nc.gpsimd.tensor_tensor(t["d_lo0"], t["d_raw0"], t["d_hi0"].bitcast(FP32), ALU.subtract)


def table_stage(nc, t, a, table):
    with ExitStack() as ctx:
        def sb(name, shape, dt=FP32):
            return ctx.enter_context(nc.sbuf_tensor("c_" + name, shape, dt))

        s = Sems(nc, ctx, "c")
        hT, xnT, bank, bias, ident, rows = t["hT"], t["xnT"], t["bank"], t["bias"], t["ident"], t["rows"]
        xc = [sb(f"xc{p}", [DP, DK, NT]) for p in range(2)]
        sq = sb("sq", [DP, DK, NT])
        std = sb("std", [DP, NT])
        rstd = sb("rstd", [DP, NT])
        xn = [sb(f"xn{p}", [DP, DK, NT]) for p in range(2)]
        mean_b = [bank[p][0:DP, 0:NT] for p in range(2)]
        var_b = [bank[2 + p][0:DP, 0:NT] for p in range(2)]
        row_b = [[bank[4 + 2 * p + j][0:TT] for j in range(NJ)] for p in range(2)]
        block = ctx.enter_context(nc.Block())

        def least(c, n):
            return isinstance(c, int) and c < n

        def chunks(eng, step):
            for c in range(2):
                step(c, c, 2)
            with eng.Fori(1, NARROW // 2 - 1) as it:
                for p in range(2):
                    step(it * 2 + p, p, 2)
            for c in range(NARROW - 2, NARROW):
                step(c, c % 2, NARROW - 1 - c)

        @block.tensor
        def _(pe):
            def mean(c, p):
                if not least(c, 2):
                    pe.wait_ge(s("xc_ready"), c - 1)
                for m in range(DK):
                    last = nc.tensor.matmul(mean_b[p], t["avg"], hT[:, m, bass.ds(c * NT, NT)], start=(m == 0),
                                            stop=(m == DK - 1))
                last.then_inc(s("mean_done"), 1)

            def var(c, p):
                pe.wait_ge(s("sq_ready"), c + 1)
                if not least(c, 2):
                    pe.wait_ge(s("std_ready"), c - 1)
                for m in range(DK):
                    last = nc.tensor.matmul(var_b[p], t["avg"], sq[:, m, :], start=(m == 0), stop=(m == DK - 1))
                last.then_inc(s("var_done"), 1)

            def tiles(c, p):
                pe.wait_ge(s("xn_ready"), c + 1)
                if not least(c, 2):
                    pe.wait_ge(s("row_ready"), NJ * (c - 1))
                for j in range(NJ):
                    tokens = slice(j * TT, (j + 1) * TT)
                    for k in range(DK):
                        nc.tensor.matmul(row_b[p][j][:, D:D + E], xn[p][:, k, tokens], t["gate_w"][:, k, :],
                                         start=(k == 0), stop=(k == DK - 1))
                    for k in range(DK):
                        last = nc.tensor.transpose(row_b[p][j][:, k * DP:(k + 1) * DP], xn[p][:, k, tokens],
                                                   ident[0:DP, 0:DP])
                    last.then_inc(s("tile_done"), 1)

            mean(0, 0)
            mean(1, 1)
            stay_awake(nc, t, bank[7], 6)
            var(0, 0)

            def step(c, p, ahead):
                if ahead > 1:
                    mean(c + 2, p)
                if ahead > 0:
                    var(c + 1, 1 - p)
                tiles(c, p)

            chunks(pe, step)
            stay_awake(nc, t, bank[0], 12)

        @block.scalar
        def _(act):
            def square(c, p):
                act.wait_ge(s("xc_ready"), c + 1)
                if not least(c, 1):
                    act.wait_ge(s("var_done"), c)
                nc.scalar.activation(sq[:, :, :], xc[p][:, :, :], ACT.Square).then_inc(s("sq_ready"), 1)

            def deviation(c, p):
                act.wait_ge(s("var_done"), c + 1)
                if not least(c, 1):
                    act.wait_ge(s("rstd_ready"), c)
                nc.scalar.activation(std[:, :], var_b[p], ACT.Sqrt, bias=bias[:, 0, 6:7]).then_inc(s("std_ready"), 1)

            def copy_rows(c, p):
                for j in range(NJ):
                    act.wait_ge(s("tile_done"), NJ * c + j + 1)
                    row = rows[:, c * NJ + j, :] if isinstance(c, int) else rows[:, bass.ds(c * NJ + j, 1), :].rearrange(
                        "p o r -> p (o r)")
                    nc.scalar.activation(row[:, 0:D], row_b[p][j][:, 0:D], ACT.Identity)
                    nc.scalar.activation(row[:, D:TURN], row_b[p][j][:, MAIN:D], ACT.Identity)
                    nc.scalar.activation(row[:, TURN:ROW], row_b[p][j][:, D:D + E],
                                         ACT.Identity).then_inc(s("row_ready"), 1)

            def step(c, p, ahead):
                if ahead > 0:
                    square(c + 1, 1 - p)
                if not least(c, 1):
                    copy_rows(c - 1, 1 - p)
                if ahead > 0:
                    deviation(c + 1, 1 - p)

            square(0, 0)
            deviation(0, 0)
            chunks(act, step)
            copy_rows(NARROW - 1, 1)
            act.wait_ge(s("row_ready"), TILES)
            nc.scalar.activation(rows[:, :, TURN:ROW], rows[:, :, TURN:ROW], ACT.Sigmoid).then_inc(s("score_ready"), 1)

        @block.vector
        def _(dve):
            def centre(c, p):
                dve.wait_ge(s("mean_done"), c + 1)
                if not least(c, 2):
                    dve.wait_ge(s("xn_ready"), c - 1)
                nc.vector.tensor_tensor(xc[p][:, :, :], hT[:, :, bass.ds(c * NT, NT)],
                                        mean_b[p].unsqueeze(1).broadcast_to([DP, DK, NT]),
                                        ALU.subtract).then_inc(s("xc_ready"), 1)

            def normalise(c, p):
                dve.wait_ge(s("std_ready"), c + 1)
                if not least(c, 1):
                    dve.wait_ge(s("xn_ready"), c)
                nc.vector.reciprocal(rstd[:, :], std[:, :]).then_inc(s("rstd_ready"), 1)
                dve.wait_ge(s("rstd_ready"), c + 1)
                if not least(c, 2):
                    dve.wait_ge(s("tile_done"), NJ * (c - 1))
                    dve.wait_ge(s("kept"), c - 1)
                nc.vector.tensor_tensor(xn[p][:, :, :], xc[p][:, :, :],
                                        rstd[:, :].unsqueeze(1).broadcast_to([DP, DK, NT]),
                                        ALU.mult).then_inc(s("xn_ready"), 1)

            def step(c, p, ahead):
                if ahead > 0:
                    centre(c + 1, 1 - p)
                normalise(c, p)

            centre(0, 0)
            chunks(dve, step)

        @block.gpsimd
        def _(pool):
            def keep(c, p, ahead):
                pool.wait_ge(s("xn_ready"), c + 1)
                nc.gpsimd.tensor_copy(xnT[:, :, bass.ds(c * NT, NT)], xn[p][:, :, :]).then_inc(s("kept"), 1)

            chunks(pool, keep)

        @block.sync
        def _(sp):
            sp.wait_ge(s("score_ready"), 1)
            sp.dma_start(table.rearrange("(i t) r -> t i r", t=TT), rows).then_inc(t["table_out"], 16)


def shared_stage(nc, t, a, out):
    with ExitStack() as ctx:
        def sb(name, shape, dt=FP32):
            return ctx.enter_context(nc.sbuf_tensor("d_" + name, shape, dt))

        s = Sems(nc, ctx, "d")
        hT, xnT, bank, ident, rows, limit = t["hT"], t["xnT"], t["bank"], t["ident"], t["rows"], t["limit"]
        wgu, wd = t["shared_gu"], t["shared_d"]
        hc = [sb(f"hc{p}", [DP, DK, WT]) for p in range(2)]
        gate = [sb(f"gate{p}", [128, WT]) for p in range(2)]
        hid = sb("hid", [128, FST, WT])
        base = [sb(f"base{p}", [TT, D]) for p in range(2)]
        reach = sb("reach", [TT, TILES, E], FP16)
        part = sb("part", [TT, E], FP16)
        back = sb("back", [TT, E], U32)
        gate_b, up_b = bank[0:2], bank[2:4]
        down_b = bank[4:6]
        count_b = bank[6][0:TT, 0:E]
        score = rows[:, :, TURN:ROW]
        block = ctx.enter_context(nc.Block())

        def first(c):
            return isinstance(c, int) and c == 0

        @block.sync
        def _(sp):
            def store(c, js):
                for j in js:
                    sp.wait_ge(s("base_ready"), 4 * c + j + 1)
                    sp.dma_start(out[bass.ds((c * WJ + j) * TT, TT), :], base[j % 2][:, :]).then_inc(s(f"base_out{j % 2}"), 16)

            store(0, range(WJ))
            with sp.Fori(1, WIDE) as c:
                store(c, range(WJ))
            for p in range(2):
                sp.wait_ge(s(f"base_out{p}"), 16 * TILES // 2)
            sp.wait_ge(t["table_out"], 16)

        @block.tensor
        def _(pe):
            def gate_up(c, f, n):
                for g, b, read in ((0, gate_b, "gate_ready"), (1, up_b, "hid_ready")):
                    if not (isinstance(n, int) and n < 2):
                        pe.wait_ge(s(read), n - 1)
                    for k in range(DK):
                        last = nc.tensor.matmul(b[f % 2][:, 0:WT], wgu[:, g, k, f * 128:(f + 1) * 128],
                                                xnT[:, k, bass.ds(c * WT, WT)], start=(k == 0), stop=(k == DK - 1))
                    last.then_inc(s("gate_done" if g == 0 else "up_done"), 1)

            def down(c, par, j):
                if j == 0:
                    pe.wait_ge(s("hid_ready"), 3 * c + 3)
                    pe.wait_ge(s("hc_ready"), c + 1)
                if not (first(c) and j < 2):
                    pe.wait_ge(s("base_ready"), 4 * c + j - 1)
                b = down_b[j % 2][0:TT, 0:D]
                for f in range(FST):
                    nc.tensor.matmul(b, hid[:, f, j * TT:(j + 1) * TT], wd[:, f, :], start=(f == 0), stop=False,
                                     skip_group_check=True)
                for k in range(DK):
                    last = nc.tensor.matmul(b[:, k * DP:(k + 1) * DP], hc[par][:, k, j * TT:(j + 1) * TT],
                                            ident[0:DP, 0:DP], start=False, stop=(k == DK - 1), skip_group_check=True)
                last.then_inc(s("down_done"), 1)

            def count(n):
                pe.wait_ge(s("part_ready"), n + 1)
                nc.tensor.matmul(count_b, t["ones"][0:TT, 0:TT], part[:, :], start=True,
                                 stop=True).then_inc(s("counted"), 1)

            def chunk(c, par):
                for q in range(STEPS):
                    if q < FST:
                        gate_up(c, q, c * FST + q)
                    elif q < STEPS - 1:
                        down(c, par, q - FST)
                    else:
                        for j in range(STEPS - 1 - FST, WJ):
                            down(c, par, j)
                    count(c * STEPS + q)

            chunk(0, 0)
            with pe.Fori(0, (WIDE - 1) // 2) as it:
                for p in range(2):
                    chunk(it * 2 + 1 + p, 1 - p)

        @block.scalar
        def _(act):
            def chunk(c):
                for f in range(FST):
                    n = c * FST + f
                    act.wait_ge(s("gate_done"), n + 1)
                    if not (isinstance(n, int) and n < 2):
                        act.wait_ge(s("hid_ready"), n - 1)
                    nc.scalar.activation(gate[f % 2][:, :], gate_b[f % 2][:, 0:WT], ACT.Silu).then_inc(s("gate_ready"), 1)
                for j in range(WJ):
                    act.wait_ge(s("down_done"), 4 * c + j + 1)
                    if not (first(c) and j < 2):
                        act.wait_ge(s(f"base_out{j % 2}"), 16 * (2 * c + j // 2))
                    nc.scalar.activation(base[j % 2][:, :], down_b[j % 2][0:TT, 0:D],
                                         ACT.Identity).then_inc(s("base_ready"), 1)

            chunk(0)
            with act.Fori(1, WIDE) as c:
                chunk(c)

        @block.vector
        def _(dve):
            def reached(n):
                nc.vector.tensor_tensor(reach[:, :, :], score, limit.bitcast(FP32).unsqueeze(1).broadcast_to([TT, TILES, E]),
                                        ALU.is_ge).then_inc(s("reach_ready"), 1)
                dve.wait_ge(s("reach_ready"), n + 1)
                if not (isinstance(n, int) and n == 0):
                    dve.wait_ge(s("counted"), n)
                with nc.allow_low_precision(reason="counts up to TILES are exact"):
                    nc.vector.tensor_reduce(part[:, :], reach[:, :, :].rearrange("p i e -> p e i"), AX.X,
                                            ALU.add).then_inc(s("part_ready"), 1)

            def settle(n):
                dve.wait_ge(s("counted"), n + 1)
                nc.vector.tensor_scalar(back[:, :], count_b, float(CAP), t["bitf"][:, bass.ds(n, 1)], ALU.is_lt,
                                        ALU.mult).then_inc(s("back_ready"), 1)
                dve.wait_ge(s("back_ready"), n + 1)
                nc.vector.scalar_tensor_tensor(limit, back[:, :], t["bitu"][:, bass.ds(n, 1)], limit, ALU.bitwise_or,
                                               ALU.bitwise_xor).then_inc(s("limit_ready"), 1)
                dve.wait_ge(s("limit_ready"), n + 2)

            def hidden(c, f):
                n = c * FST + f
                dve.wait_ge(s("gate_ready"), n + 1)
                dve.wait_ge(s("up_done"), n + 1)
                if f == 0 and not first(c):
                    dve.wait_ge(s("down_done"), 4 * c)
                nc.vector.tensor_tensor(hid[:, f, :], gate[f % 2][:, :], up_b[f % 2][:, 0:WT],
                                        ALU.mult).then_inc(s("hid_ready"), 1)

            def chunk(c):
                for q in range(STEPS):
                    reached(c * STEPS + q)
                    if q < FST:
                        hidden(c, q)
                    settle(c * STEPS + q)

            nc.vector.memset(limit, 1 << (BITS - 1)).then_inc(s("limit_ready"), 1)
            dve.wait_ge(s("limit_ready"), 1)
            chunk(0)
            with dve.Fori(1, WIDE) as c:
                chunk(c)

        @block.gpsimd
        def _(pool):
            def chunk(c, par):
                if not (isinstance(c, int) and c < 2):
                    pool.wait_ge(s("down_done"), 4 * c - 4)
                nc.gpsimd.tensor_copy(hc[par][:, :, :], hT[:, :, bass.ds(c * WT, WT)]).then_inc(s("hc_ready"), 1)

            chunk(0, 0)
            chunk(1, 1)
            chunk(2, 0)
            with pool.Fori(1, (WIDE - 1) // 2) as it:
                for p in range(2):
                    chunk(it * 2 + 1 + p, 1 - p)


def slot_stage(nc, t, a):
    with ExitStack() as ctx:
        def sb(name, shape, dt=FP32):
            return ctx.enter_context(nc.sbuf_tensor("e_" + name, shape, dt))

        s = Sems(nc, ctx, "e")
        bank, rows, limit = t["bank"], t["rows"], t["limit"]
        N = E * TILES
        above = sb("above", [TT, N], FP16)
        equal = sb("equal", [TT, N], FP16)
        run = [sb(f"run{i}", [TT, N], FP16) for i in range(2)]
        room = sb("room", [TT, E])
        rank = sb("rank", [TT, N])
        fits = sb("fits", [TT, N])
        slot = sb("slot", [TT, N])
        third = sb("third", [TT, N])
        third2 = sb("third2", [TT, N])
        above_b, equal_b, total_b = bank[0][0:TT, 0:N], bank[1][0:TT, 0:N], bank[2][0:TT, 0:E]
        score = rows[:, :, TURN:ROW].rearrange("p i e -> p e i")
        lim = limit.bitcast(FP32).unsqueeze(2).broadcast_to([TT, E, TILES])
        block = ctx.enter_context(nc.Block())

        def by_expert(x):
            return x.rearrange("p (e i) -> p e i", e=E)

        @block.vector
        def _(dve):
            done = [0]

            def then(ins):
                done[0] += 1
                ins.then_inc(s("step"), 1)
                dve.wait_ge(s("step"), done[0])

            nc.vector.tensor_tensor(by_expert(above[:, :]), score, lim, ALU.is_gt)
            then(nc.vector.tensor_tensor(by_expert(equal[:, :]), score, lim, ALU.is_equal))
            for m, r in ((above, run[0]), (equal, run[1])):
                last = nc.vector.tensor_tensor_scan(r[:, :], t["restart"], m[:, :], 0.0, ALU.mult, ALU.add)
            last.then_inc(s("run_ready"), 1)
            dve.wait_ge(s("ranked"), 1)
            then(nc.vector.tensor_scalar(room[:, :], total_b, -1.0, float(CAP), ALU.mult, ALU.add))
            then(nc.vector.tensor_copy(rank[:, :], equal_b))
            room_bc = room[:, :].unsqueeze(2).broadcast_to([TT, E, TILES])
            then(nc.vector.tensor_tensor(by_expert(fits[:, :]), by_expert(rank[:, :]), room_bc, ALU.is_lt))
            then(nc.vector.tensor_tensor(fits[:, :], fits[:, :], equal[:, :], ALU.mult))
            then(nc.vector.tensor_tensor(fits[:, :], fits[:, :], above[:, :], ALU.add))
            then(nc.vector.tensor_tensor(by_expert(rank[:, :]), by_expert(rank[:, :]), room_bc, ALU.min))
            then(nc.vector.tensor_tensor(slot[:, :], above_b, rank[:, :], ALU.add))
            then(nc.vector.scalar_tensor_tensor(slot[:, :], slot[:, :], 1.0, fits[:, :], ALU.add, ALU.mult))
            then(nc.vector.tensor_scalar(slot[:, :], slot[:, :], -1.0, None, ALU.add))
            then(nc.vector.tensor_scalar(third[:, :], slot[:, :], float(SLOTP), None, ALU.is_ge))
            then(nc.vector.tensor_scalar(third2[:, :], slot[:, :], float(2 * SLOTP), None, ALU.is_ge))
            then(nc.vector.tensor_tensor(third[:, :], third[:, :], third2[:, :], ALU.add))
            then(nc.vector.scalar_tensor_tensor(t["slotp"], third[:, :], -float(SLOTP), slot[:, :], ALU.mult, ALU.add))
            for b in range(3):
                last = nc.vector.scalar_tensor_tensor(
                    t["slotid"][:, :, :, b], by_expert(third[:, :]), float(b),
                    t["ids"].unsqueeze(1).broadcast_to([TT, E, TILES]), ALU.is_equal, ALU.mult)
            then(last)

        @block.tensor
        def _(pe):
            stay_awake(nc, t, bank[3], 12)
            pe.wait_ge(s("run_ready"), 1)
            for m, r, b in ((above, run[0], above_b), (equal, run[1], equal_b)):
                nc.tensor.matmul(b, t["ones"][0:TT, 0:TT], r[:, :], start=True, stop=False)
                nc.tensor.matmul(b, t["before"], m[:, :], start=False, stop=True)
            nc.tensor.matmul(total_b, t["ones"][0:TT, 0:TT], by_expert(run[0][:, :])[:, :, TILES - 1], start=True,
                             stop=True).then_inc(s("ranked"), 1)
            stay_awake(nc, t, bank[3], 32)


def expert_stage(nc, t, a, table, out):
    with ExitStack() as ctx:
        def sb(name, shape, dt=FP32):
            return ctx.enter_context(nc.sbuf_tensor("f_" + name, shape, dt))

        s = Sems(nc, ctx, "f")
        bank, ident = t["bank"], t["ident"]
        raw, hi, lo = ([(t[f"gu_{kind}{q}"], t[f"d_{kind}{q}"]) for q in range(2)] for kind in ("raw", "hi", "lo"))
        hot = [sb(f"hot{p}", [TT, TILES, SLOTP], FP16) for p in range(2)]
        slotid = [sb(f"slotid{p}", [TT, TILES, 3], FP16) for p in range(2)]
        listed = sb("listed", [3, SLOTP])
        ids = [sb(f"ids{p}", [SLOTP, 3], U32) for p in range(2)]
        ids_out = [sb(f"ids_out{p}", [SLOTP, 3], U32) for p in range(2)]
        got = [sb(f"got{p}", [SLOTP, 3, ROW]) for p in range(2)]
        score = [sb(f"score{p}", [SLOTP, 3]) for p in range(2)]
        x_hi = sb("x_hi", [128, CAP], FP32R)
        x_lo = sb("x_lo", [128, CAP], FP32R)
        x_tail = sb("x_tail", [128, CAP], FP32R)
        gate = [sb(f"gate{p}", [128, CAP]) for p in range(2)]
        hid = [sb(f"hid{p}", [128, CAP]) for p in range(2)]
        hid_hi = sb("hid_hi", [128, FET, CAP], FP32R)
        hid_lo = sb("hid_lo", [128, FET, CAP], FP32R)
        y = [sb(f"y{p}", [SLOTP, 3, D]) for p in range(2)]
        gate_b, up_b = bank[0:2], bank[2:4]
        x_b = [b[:, 0:CAP] for b in bank[4:6]]
        down_b = [bank[6][:, 0:D], bank[7][:, 0:D], bank[4][:, 0:D]]
        list_b = bank[5][0:3, 272:272 + SLOTP]
        ids_b = bank[5][0:SLOTP, 480:483]
        block = ctx.enter_context(nc.Block())

        def least(e, n):
            return isinstance(e, int) and e < n

        def loads_of(e, p):
            return 8 * (e - p) + 16

        def experts(eng, body):
            for e in range(2):
                body(e, e, 3)
            with eng.Fori(1, E // 2 - 2) as it:
                for p in range(2):
                    body(it * 2 + p, p, 3)
            for e in range(E - 4, E):
                body(e, e % 2, min(3, E - 1 - e))

        @block.sync
        def _(sp):
            def load(e, p):
                sp.wait_ge(s("gu_split"), 4 * (e - 2)) if not least(e, 3) else None
                sp.dma_start(raw[p][0], a["expert_gu"][e]).then_inc(s(f"gu_loaded{p}"), 16)
                sp.wait_ge(s("d_split"), 2 * (e - 2)) if not least(e, 3) else None
                sp.dma_start(raw[p][1], a["expert_d"][e]).then_inc(s(f"d_loaded{p}"), 16)

            load(2, 0)
            load(3, 1)
            with sp.Fori(2, E // 2) as it:
                for p in range(2):
                    load(it * 2 + p, p)

        @block.tensor
        def _(pe):
            def list_tokens(e, p):
                pe.wait_ge(s("hot_ready"), e + 1)
                if not least(e, 1):
                    pe.wait_ge(s("ids_ready"), e)
                for i in range(TILES):
                    last = nc.tensor.matmul(list_b, slotid[p][:, i, :], hot[p][:, i, :], start=(i == 0),
                                            stop=(i == TILES - 1), skip_group_check=True)
                last.then_inc(s("listed"), 1)

            def flip_ids(e):
                pe.wait_ge(s("list_ready"), e + 1)
                nc.tensor.matmul(ids_b, listed[:, :], ident[0:3, 0:3], start=True, stop=True).then_inc(s("ids_done"), 1)

            def flip_rows(e, p, listed):
                pe.wait_ge(s("ids_ready"), listed)
                pe.wait_ge(s(f"got{p}"), 24 * (e - p) + 48)
                if not least(e, 2):
                    pe.wait_ge(s("y_ready"), 3 * e - 3)
                for k in range(2):
                    for b in range(3):
                        n = THIRDS[b]
                        last = nc.tensor.transpose(x_b[k][:, b * SLOTP:b * SLOTP + n],
                                                   got[p][0:n, b, k * MAIN:(k + 1) * MAIN], ident[0:n, 0:n])
                    last.then_inc(s("x_done"), 1)

            def gate_up(e, p, two):
                pe.wait_ge(s("x_ready"), 2 * e + 2)
                if not least(e, 1):
                    pe.wait_ge(s("gu_split"), 4 * e)
                wh, wl = hi[p][0], lo[p][0]
                for f in range(FET):
                    n = e * FET + f
                    w = slice(f * 128, (f + 1) * 128)
                    for g, b, read in ((0, gate_b, "gate_ready"), (1, up_b, "hid_ready")):
                        if not least(n, 2):
                            pe.wait_ge(s(read), n - 1)
                        b = b[f % 2][:, 0:CAP]
                        passes = ((wh[:, 0, g, w], x_hi[:, :]), (wl[:, 0, g, w], x_hi[:, :]), (wh[:, 0, g, w], x_lo[:, :]),
                                  (wh[:, 1, g, w], x_tail[:, :]), (wl[0:TAIL, 1, g, w], x_tail[0:TAIL, :]))
                        for i, (wt, xt) in enumerate(passes):
                            last = nc.tensor.matmul(b, wt, xt, start=(i == 0), stop=(i == len(passes) - 1),
                                                    skip_group_check=True)
                        last.then_inc(s("gate_done" if g == 0 else "up_done"), 1)
                    if two and f == 0:
                        list_tokens(e + 2, p)
                    if two and f == 3:
                        flip_ids(e + 2)

            def down(e, p, one):
                if not least(e, 1):
                    pe.wait_ge(s("d_split"), 2 * e)
                wh, wl = hi[p][1], lo[p][1]
                early, late = range(FET - 2), range(FET - 2, FET)
                for b, fs in ((0, early), (1, early), (0, late), (1, late), (2, range(FET))):
                    n = THIRDS[b]
                    slots = slice(b * SLOTP, b * SLOTP + n)
                    if fs[0] == 0 and not one:
                        pe.wait_ge(s("y_ready"), 3 * e - 2 + b)
                    if b == 2 and one:
                        pe.wait_ge(s("x_ready"), 2 * e + 4)
                    for f in fs:
                        if b == 0:
                            pe.wait_ge(s("hid_split"), FET * e + f + 1)
                        for i, (xt, wt) in enumerate(((hid_hi, wh), (hid_hi, wl), (hid_lo, wh))):
                            last = nc.tensor.matmul(down_b[b][0:n, :], xt[:, f, slots], wt[:, f, :],
                                                    start=(f == 0 and i == 0), stop=(f == FET - 1 and i == 2),
                                                    skip_group_check=True)
                    if fs[-1] == FET - 1:
                        last.then_inc(s("down_done"), 1)

            def body(e, p, after):
                gate_up(e, p, after >= 2)
                if after:
                    flip_rows(e + 1, 1 - p, e + 3 if after >= 2 else E)
                down(e, p, after > 0)

            for q in range(2):
                stay_awake(nc, t, bank[7], 6)
                list_tokens(q, q)
                flip_ids(q)
            stay_awake(nc, t, bank[7], 20)
            flip_rows(0, 0, 2)
            stay_awake(nc, t, bank[7], 8)
            experts(pe, body)

        @block.scalar
        def _(act):
            def round_hidden(n, f):
                act.wait_ge(s("hid_ready"), n + 1)
                nc.scalar.activation(hid_hi[:, f, :], hid[f % 2][:, :], ACT.Identity).then_inc(s("hid_rounded"), 1)

            def round_weights(e, p, j):
                if j < 4:
                    if j == 0:
                        if not least(e, 2):
                            act.wait_ge(s(f"gu_loaded{p}"), loads_of(e, p) - 16)
                            act.wait_ge(s("up_done"), FET * (e - 1))
                    part = (slice(None), j // 2, j % 2, slice(None))
                    nc.scalar.activation(hi[p][0][part], raw[p][0][part], ACT.Identity).then_inc(s("gu_rounded"), 1)
                else:
                    if j == 4 and not least(e, 2):
                        act.wait_ge(s(f"d_loaded{p}"), loads_of(e, p) - 16)
                        act.wait_ge(s("down_done"), 3 * (e - 1))
                    part = (slice(None), slice((j - 4) * 3, (j - 3) * 3), slice(None))
                    nc.scalar.activation(hi[p][1][part], raw[p][1][part], ACT.Identity).then_inc(s("d_rounded"), 1)

            def round_rows(e):
                for k, dst in enumerate((x_hi, x_tail)):
                    act.wait_ge(s("x_done"), 2 * e + k + 1)
                    if k == 0 and not least(e, 1):
                        act.wait_ge(s("up_done"), FET * e)
                    nc.scalar.activation(dst[:, :], x_b[k], ACT.Identity).then_inc(s("x_rounded"), 1)

            def body(e, p, after):
                for f in range(FET):
                    n = e * FET + f
                    act.wait_ge(s("gate_done"), n + 1)
                    if not least(n, 2):
                        act.wait_ge(s("hid_ready"), n - 1)
                    nc.scalar.activation(gate[f % 2][:, :], gate_b[f % 2][:, 0:CAP], ACT.Silu).then_inc(s("gate_ready"), 1)
                    if f > 0:
                        if f == 1 and not least(e, 1):
                            act.wait_ge(s("down_done"), 3 * e)
                        round_hidden(n - 1, f - 1)
                    if after and 0 < f < 4:
                        round_weights(e + 1, 1 - p, f)
                round_hidden(e * FET + FET - 1, FET - 1)
                if after:
                    round_rows(e + 1)
                    for j in (4, 5):
                        round_weights(e + 1, 1 - p, j)
                if not least(e, 2):
                    act.wait_ge(s(f"added{p}"), 24 * (e - p))
                act.wait_ge(s("score_kept"), e + 1)
                for b in range(3):
                    act.wait_ge(s("down_done"), 3 * e + b + 1)
                    if b == 2 and after >= 2:
                        round_weights(e + 2, p, 0)
                    n = THIRDS[b]
                    nc.scalar.activation(y[p][0:n, b, :], down_b[b][0:n, :], ACT.Identity,
                                         scale=score[p][0:n, b:b + 1]).then_inc(s("y_ready"), 1)

            round_rows(0)
            round_weights(1, 1, 0)
            experts(act, body)

        @block.vector
        def _(dve):
            def one_hot(e, p):
                if not least(e, 2):
                    dve.wait_ge(s("listed"), e - 1)
                nc.vector.tensor_copy(slotid[p][:, :, :], t["slotid"][:, bass.ds(e, 1)].rearrange("p o i b -> p (o i) b"))
                col = t["slotp"][:, bass.ds(e * TILES, TILES)]
                nc.vector.tensor_tensor(hot[p][:, :, :], t["iota"].unsqueeze(1).broadcast_to([TT, TILES, SLOTP]),
                                        col.unsqueeze(2).broadcast_to([TT, TILES, SLOTP]),
                                        ALU.is_equal).then_inc(s("hot_ready"), 1)

            def keep_list(e):
                dve.wait_ge(s("listed"), e + 1)
                nc.vector.tensor_copy(listed[:, :], list_b).then_inc(s("list_ready"), 1)

            def token_ids(e, p):
                dve.wait_ge(s("ids_done"), e + 1)
                if not least(e, 2):
                    dve.wait_ge(s(f"got{p}"), 24 * (e - p))
                nc.vector.tensor_scalar(ids[p][:, :], ids_b, float(IDMID), None, ALU.add).then_inc(s("ids_ready"), 1)

            def keep_score(e, p):
                dve.wait_ge(s(f"got{p}"), 24 * (e - p) + 48)
                if not least(e, 2):
                    dve.wait_ge(s("y_ready"), 3 * e - 3)
                    dve.wait_ge(s(f"added{p}"), 24 * (e - p))
                nc.vector.tensor_copy(ids_out[p][:, :], ids[p][:, :])
                nc.vector.tensor_copy(score[p][:, 0:2],
                                      got[p][:, 0:2, bass.ds(e + TURN, 1)].rearrange("p b o -> p (b o)"))
                nc.vector.tensor_copy(score[p][0:THIRDS[2], 2:3],
                                      got[p][0:THIRDS[2], 2, bass.ds(e + TURN, 1)]).then_inc(s("score_kept"), 1)

            def split_rows(e):
                dve.wait_ge(s("x_rounded"), 2 * e + 1)
                nc.vector.tensor_tensor(x_lo[:, :], x_b[0], x_hi[:, :].bitcast(FP32),
                                        ALU.subtract).then_inc(s("x_ready"), 1)
                dve.wait_ge(s("x_rounded"), 2 * e + 2)
                nc.vector.tensor_tensor(x_tail[TAIL:, :], x_b[1][TAIL:, :], x_tail[TAIL:, :].bitcast(FP32),
                                        ALU.subtract).then_inc(s("x_ready"), 1)

            def split_weights(e, p, j):
                dve.wait_ge(s("gu_rounded"), 4 * e - 3 + j)
                part = (slice(0, 128 if j < 2 else TAIL), j // 2, j % 2, slice(None))
                nc.vector.tensor_tensor(lo[p][0][part], raw[p][0][part], hi[p][0][part].bitcast(FP32),
                                        ALU.subtract).then_inc(s("gu_split"), 1)

            def split_hidden(n, f):
                dve.wait_ge(s("hid_rounded"), n + 1)
                nc.vector.tensor_tensor(hid_lo[:, f, :], hid[f % 2][:, :], hid_hi[:, f, :].bitcast(FP32),
                                        ALU.subtract).then_inc(s("hid_split"), 1)

            def body(e, p, after):
                for f in range(FET):
                    n = e * FET + f
                    dve.wait_ge(s("gate_ready"), n + 1)
                    dve.wait_ge(s("up_done"), n + 1)
                    if not least(n, 2):
                        dve.wait_ge(s("hid_split"), n - 1)
                    nc.vector.tensor_tensor(hid[f % 2][:, :], gate[f % 2][:, :], up_b[f % 2][:, 0:CAP],
                                            ALU.mult).then_inc(s("hid_ready"), 1)
                    if f > 0:
                        split_hidden(n - 1, f - 1)
                    if after and f == 1:
                        split_weights(e + 1, 1 - p, 1)
                    if f == 1 and after >= 2:
                        keep_list(e + 2)
                    if f == 3 and after >= 2:
                        token_ids(e + 2, p)
                split_hidden(e * FET + FET - 1, FET - 1)
                if after:
                    split_rows(e + 1)
                    for j in (2, 3):
                        split_weights(e + 1, 1 - p, j)
                if after == 3:
                    one_hot(e + 3, 1 - p)
                if after:
                    keep_score(e + 1, 1 - p)
                if after >= 2:
                    split_weights(e + 2, p, 0)

            one_hot(0, 0)
            one_hot(1, 1)
            keep_list(0)
            token_ids(0, 0)
            one_hot(2, 0)
            keep_list(1)
            token_ids(1, 1)
            keep_score(0, 0)
            split_rows(0)
            split_weights(1, 1, 0)
            experts(dve, body)

        @block.gpsimd
        def _(pool):
            def gather(e, p):
                pool.wait_ge(s("ids_ready"), e + 1)
                if not least(e, 2):
                    pool.wait_ge(s("score_kept"), e - 1)
                    pool.wait_ge(s("x_done"), 2 * (e - 1))
                pool.sem_inc(s("gathers"), 1)
                for b in range(3):
                    n = THIRDS[b]
                    nc.gpsimd.indirect_dma_start(
                        out=got[p][0:n, b, :], out_offset=None, in_=table,
                        in_offset=bass.IndirectOffsetOnAxis(ap=ids[p][0:n, b:b + 1], axis=0)).then_inc(s(f"got{p}"), 16)

            def add(e, p):
                pool.wait_ge(s("y_ready"), 3 * e + 3)
                if not least(e, 1):
                    pool.wait_ge(s(f"added{1 - p}"), 24 * (e - p) + 48 * p)
                pool.sem_inc(s("adds"), 1)
                for b in range(3):
                    n = THIRDS[b]
                    nc.gpsimd.indirect_dma_start(
                        out=out, out_offset=bass.IndirectOffsetOnAxis(ap=ids_out[p][0:n, b:b + 1], axis=0),
                        in_=y[p][0:n, b, :], in_offset=None, compute_op=ALU.add).then_inc(s(f"added{p}"), 16)

            def split_down(e, p):
                for j in range(2):
                    pool.wait_ge(s("d_rounded"), 2 * e - 1 + j)
                    part = (slice(None), slice(j * 3, (j + 1) * 3), slice(None))
                    nc.gpsimd.tensor_tensor(lo[p][1][part], raw[p][1][part], hi[p][1][part].bitcast(FP32),
                                            ALU.subtract).then_inc(s("d_split"), 1)

            def body(e, p, after):
                if after >= 2:
                    gather(e + 2, p)
                if after:
                    split_down(e + 1, 1 - p)
                add(e, p)

            gather(0, 0)
            gather(1, 1)
            experts(pool, body)
            for p in range(2):
                pool.wait_ge(s(f"added{p}"), 16 * 3 * E // 2)


def tower(nc, a, table, out):
    with ExitStack() as ctx:
        def sb(ctx, name, shape, dt=FP32):
            return ctx.enter_context(nc.sbuf_tensor(name, shape, dt))[tuple(slice(None) for _ in shape)]

        def const(ctx, *names):
            for name in names:
                t[name] = sb(ctx, "s_" + name, list(a[name].shape), a[name].dtype)

        psum = ctx.enter_context(nc.psum_tensor("psum", [128, 8 * 512], FP32))
        t = {
            "psum": psum,
            "table_out": ctx.enter_context(nc.semaphore("table_out")),
            "bank": [psum[:, 512 * i:512 * (i + 1)] for i in range(8)],
            "slotp": sb(ctx, "slotp", [TT, E * TILES], FP16),
            "slotid": sb(ctx, "slotid", [TT, E, TILES, 3], FP16),
        }
        const(ctx, "ident", "iota", "ones")
        for q in range(2):
            t[f"gu_raw{q}"] = sb(ctx, f"gu_raw{q}", [128, 2, 2, FE])
            t[f"d_raw{q}"] = sb(ctx, f"d_raw{q}", [128, FET, D])

        def parts(ctx, q):
            for kind in ("hi", "lo"):
                t[f"gu_{kind}{q}"] = sb(ctx, f"gu_{kind}{q}", [128, 2, 2, FE], FP32R)
                t[f"d_{kind}{q}"] = sb(ctx, f"d_{kind}{q}", [128, FET, D], FP32R)

        parts(ctx, 0)
        with ExitStack() as dense:
            t["hT"] = sb(dense, "hT", [DP, DK, TOK])
            t["xnT"] = sb(dense, "xnT", [DP, DK, TOK])
            t["limit"] = sb(dense, "limit", [TT, E], U32)
            const(dense, "bias", "avg", "headmask", "clsmask", "attn_w", "gate_w", "shared_gu", "shared_d", "bitf",
                  "bitu", "before", "ids", "restart")
            embed_stage(nc, t, a)
            attention_stage(nc, t, a)
            t["rows"] = sb(dense, "rows", [TT, TILES, ROW])
            table_stage(nc, t, a, table)
            shared_stage(nc, t, a, out)
            slot_stage(nc, t, a)
        parts(ctx, 1)
        expert_stage(nc, t, a, table, out)


def layouts(x, cls_tok, L0_tok_w, L0_tok_b, L0_attn_wq, L0_attn_bq, L0_attn_wk, L0_attn_bk, L0_attn_wv, L0_attn_bv,
            L0_attn_ww, L0_attn_bw, L0_ffn_gate_weight, L0_ffn_Wg, L0_ffn_Wu, L0_ffn_Wd, L0_ffn_Ws_g, L0_ffn_Ws_u,
            L0_ffn_Ws_d):
    import numpy as np

    def halves(m):
        return np.asarray(m).T.reshape(DK, DP, -1).transpose(1, 0, 2)

    def turned(m):
        m = np.asarray(m).transpose(0, 2, 1)
        return np.stack([m[:, :MAIN], np.concatenate([m[:, MAIN:], m[:, MAIN:]], 1)], 2)

    def blocks(m):
        return np.asarray(m).T.reshape(-1, 128, D).transpose(1, 0, 2)

    P = 32
    patches = np.asarray(x).reshape(CHUNKS, GI, 8, P, 8, P).transpose(0, 3, 5, 1, 2, 4)
    patches = patches.reshape(CHUNKS, PK, 128, CP).transpose(0, 2, 1, 3)
    bias = np.zeros((DP, DK, 8), np.float32)
    for n, v in enumerate((L0_tok_b, L0_attn_bq, L0_attn_bk, L0_attn_bv, L0_attn_bw, cls_tok)):
        bias[:, :, n] = np.asarray(v).reshape(DK, DP).T
    bias[:, :, 6] = EPS
    at = np.arange(128)
    bits = [1 << (BITS - 1 - n) for n in range(BITS)] + [0]
    restart = np.ones((TT, E, TILES), np.float32)
    restart[:, :, 0] = 0
    tt = np.arange(TT)
    return {
        "patches": patches,
        "tok_w": np.asarray(L0_tok_w).T.reshape(PK, 128, D).transpose(1, 0, 2),
        "bias": bias,
        "attn_w": np.stack([halves(m) for m in (L0_attn_wq, L0_attn_wk, L0_attn_wv, L0_attn_ww)], 1),
        "gate_w": halves(L0_ffn_gate_weight),
        "shared_gu": np.stack([halves(L0_ffn_Ws_g), halves(L0_ffn_Ws_u)], 1),
        "shared_d": blocks(L0_ffn_Ws_d),
        "expert_gu": np.stack([turned(m) for m in (L0_ffn_Wg, L0_ffn_Wu)], 3),
        "expert_d": np.asarray(L0_ffn_Wd).transpose(0, 2, 1).reshape(E, FET, 128, D).transpose(0, 2, 1, 3),
        "avg": np.full((DP, DP), 1 / D, np.float32),
        "ident": np.eye(128, dtype=np.float32),
        "headmask": (np.arange(DP)[:, None] // HD == np.arange(HH)).astype(np.float32),
        "clsmask": np.eye(HEADS, dtype=np.float32),
        "ones": np.ones((128, 128), np.float16),
        "before": -(tt[:, None] >= tt[None, :]).astype(np.float16),
        "iota": np.tile(np.arange(SLOTP, dtype=np.float16), (TT, 1)),
        "ids": (np.arange(TILES)[None, :] * TT + tt[:, None] - IDMID).astype(np.float16),
        "restart": restart.reshape(TT, -1),
        "bitf": np.tile(np.array(bits[:-1], np.float32), (TT, 1)),
        "bitu": np.tile(np.array(bits[1:], np.uint32), (TT, 1)),
    }


def kernel(**inputs):
    import numpy as np
    import concourse.bacc as bacc
    from concourse.bass_utils import run_bass_kernel_spmd

    nc = bacc.Bacc("TRN2", target_bir_lowering=False, num_devices=1)
    arrays, a = {}, {}
    for name, v in layouts(**inputs).items():
        arrays[name + "_in"] = v = np.ascontiguousarray(v)
        a[name] = nc.dram_tensor(name + "_in", v.shape, mybir.dt.from_np(v.dtype), kind="ExternalInput").ap()
    table = nc.dram_tensor("table", (TOK, ROW), FP32, kind="Internal").ap()
    out = nc.dram_tensor("y_out", (TOK, D), FP32, kind="ExternalOutput").ap()
    tower(nc, a, table, out)
    r = run_bass_kernel_spmd(nc, [arrays], core_ids=[0])
    return r.results[0]["y_out"].reshape(IMGS, SEQ, D)
```

```python
import concourse.bass as bass
from concourse import mybir
from contextlib import ExitStack

FP32 = mybir.dt.float32
FP32R = mybir.dt.float32r
FP16 = mybir.dt.float16
U32 = mybir.dt.uint32
ALU = mybir.AluOpType
ACT = mybir.ActivationFunctionType
AX = mybir.AxisListType

IMGS = 32
PATCHES = 64
SEQ = PATCHES + 1
D = 192
DP = 96
DK = D // DP
PIX = 1024
PK = PIX // 128
TOK = IMGS * SEQ
HEADS = 12
HD = D // HEADS
HH = HEADS // DK
PAIRS = HEADS // 2
GI = 4
CHUNKS = IMGS // GI
CT = GI * SEQ
CP = GI * PATCHES
TT = 104
TILES = TOK // TT
WJ = 4
WT = WJ * TT
WIDE = TOK // WT
NJ = 2
NT = NJ * TT
NARROW = TOK // NT
E = 16
TOPK = 2
CAP = -(-TOK * TOPK // E)
SLOTP = -(-CAP // 3)
THIRDS = [SLOTP, SLOTP, CAP - 2 * SLOTP]
FE = 768
FET = FE // 128
FS = 384
FST = FS // 128
MAIN = 128
TAIL = D - MAIN
TURN = MAIN + 2 * TAIL
ROW = TURN + E
BITS = 30
STEPS = BITS // WIDE
IDMID = 1040
EPS = 1e-5
CROWS = 2 * 32 + HEADS
VW = 2 * (HD + 1)


class Sems:

    def __init__(self, nc, ctx, stage):
        self.made, self.nc, self.ctx, self.stage = {}, nc, ctx, stage

    def __call__(self, name):
        if name not in self.made:
            self.made[name] = self.ctx.enter_context(self.nc.semaphore(f"{self.stage}_{name}"))
        return self.made[name]


def stay_awake(nc, t, bank, n):
    for _ in range(n):
        nc.tensor.matmul(bank[:, 0:512], t["ones"], t["ones"].unsqueeze(1).broadcast_to([128, 4, 128]), start=True,
                         stop=True)


def embed_stage(nc, t, a):
    with ExitStack() as ctx:
        def sb(name, shape, dt=FP32):
            return ctx.enter_context(nc.sbuf_tensor("a_" + name, shape, dt))

        s = Sems(nc, ctx, "a")
        hT, xnT, bank, bias = t["hT"], t["xnT"], t["bank"], t["bias"]
        raw = [sb(f"raw{p}", [128, PK, CP]) for p in range(2)]
        xh = [sb(f"xh{p}", [128, PK, CP], FP32R) for p in range(2)]
        xl = [sb(f"xl{p}", [128, PK, CP], FP32R) for p in range(2)]
        tok_w = sb("tok_w", [128, PK, D])
        tok_hi = sb("tok_hi", [128, PK, D], FP32R)
        tok_lo = sb("tok_lo", [128, PK, D], FP32R)
        xc = sb("xc", [DP, DK, CT])
        sq = sb("sq", [DP, DK, CT])
        std = sb("std", [DP, CT])
        rstd = sb("rstd", [DP, CT])
        QK = PK // 2
        emb = [bank[2 * p:2 * p + 2] for p in range(2)]
        mean_b, var_b = bank[4], bank[5]
        block = ctx.enter_context(nc.Block())

        def half(q):
            return (slice(None), slice(q * QK, (q + 1) * QK))

        def cols(x, c):
            return x[:, :, bass.ds(c * CT, CT)]

        @block.sync
        def _(sp):
            sp.dma_start(tok_w[:, :, :], a["tok_w"]).then_inc(s("tok_w"), 16)

            def load(c, p):
                for q in range(2):
                    if isinstance(c, int) and c == 2:
                        sp.wait_ge(s("split_first"), q + 1)
                    elif not (isinstance(c, int) and c < 2):
                        sp.wait_ge(s("split"), 2 * c - 5 + q)
                    sp.dma_start(raw[p][half(q)], a["patches"][c][half(q)]).then_inc(s(f"loaded{p}{q}"), 16)

            load(0, 0)
            sp.dma_start(bias[:, :, :], a["bias"]).then_inc(s("consts"), 16)
            sp.dma_start(t["avg"][:, :], a["avg"]).then_inc(s("consts"), 16)
            sp.dma_start(t["ones"], a["ones"]).then_inc(s("consts"), 16)
            for c in range(1, 4):
                load(c, c % 2)
            with sp.Fori(2, CHUNKS // 2) as it:
                for p in range(2):
                    load(it * 2 + p, p)
            later = ("ident", "headmask", "clsmask", "attn_w", "gate_w", "shared_gu", "shared_d", "before",
                     "iota", "ids", "restart", "bitf", "bitu")
            for name in later:
                sp.dma_start(t[name], a[name]).then_inc(s("later"), 16)
            for e in range(2):
                sp.dma_start(t[f"gu_raw{e}"], a["expert_gu"][e]).then_inc(s("experts"), 16)
                sp.dma_start(t[f"d_raw{e}"], a["expert_d"][e]).then_inc(s("experts"), 16)
            sp.wait_ge(s("later"), 16 * len(later))
            sp.wait_ge(s("experts"), 16 * 4)

        @block.tensor
        def _(pe):
            pe.wait_ge(s("tok_split"), 2)
            pe.wait_ge(s("consts"), 48)

            def embed(c, par, m):
                start = isinstance(c, int) and c == 0
                if m == 0 and not start:
                    pe.wait_ge(s("split"), 2 * c)
                out, rows = emb[par][m][0:DP, 0:CP], slice(m * DP, (m + 1) * DP)
                for k in range(PK):
                    if start and m == 0 and k % QK == 0:
                        pe.wait_ge(s("rounded"), k // QK + 1)
                    nc.tensor.matmul(out, tok_hi[:, k, rows], xh[par][:, k, :], start=(k == 0), stop=False)
                    nc.tensor.matmul(out, tok_lo[:, k, rows], xh[par][:, k, :], start=False, stop=False)
                for k in range(PK):
                    if start and m == 0 and k % QK == 0:
                        pe.wait_ge(s("split_first"), k // QK + 1)
                    last = nc.tensor.matmul(out, tok_hi[:, k, rows], xl[par][:, k, :], start=False, stop=(k == PK - 1))
                last.then_inc(s("emb_done"), 1)

            def mean(c):
                pe.wait_ge(s("h_ready"), 2 * c + 2)
                if not isinstance(c, int) or c > 0:
                    pe.wait_ge(s("xc_ready"), c)
                for m in range(DK):
                    last = nc.tensor.matmul(mean_b[0:DP, 0:CT], t["avg"][:, :], hT[:, m, bass.ds(c * CT, CT)],
                                            start=(m == 0), stop=(m == DK - 1))
                last.then_inc(s("mean_done"), 1)

            def var(c):
                pe.wait_ge(s("sq_ready"), c + 1)
                for m in range(DK):
                    last = nc.tensor.matmul(var_b[0:DP, 0:CT], t["avg"][:, :], sq[:, m, :],
                                            start=(m == 0), stop=(m == DK - 1))
                last.then_inc(s("var_done"), 1)

            def step(c, par):
                embed(c + 1, 1 - par, 0)
                mean(c)
                embed(c + 1, 1 - par, 1)
                var(c)

            embed(0, 0, 0)
            embed(0, 0, 1)
            with pe.Fori(0, (CHUNKS - 2) // 2) as it:
                for p in range(2):
                    step(it * 2 + p, p)
            step(CHUNKS - 2, 0)
            mean(CHUNKS - 1)
            stay_awake(nc, t, bank[6], 12)
            var(CHUNKS - 1)
            stay_awake(nc, t, bank[6], 13)

        @block.scalar
        def _(act):
            act.wait_ge(s("tok_w"), 16)
            nc.scalar.activation(tok_hi[:, :, :], tok_w[:, :, :], ACT.Identity).then_inc(s("tok_split"), 1)
            for q in range(2):
                act.wait_ge(s(f"loaded0{q}"), 16)
                nc.scalar.activation(xh[0][half(q)], raw[0][half(q)], ACT.Identity).then_inc(s("rounded"), 1)
            act.wait_ge(s("consts"), 48)

            def embedded(c, par):
                for m in range(DK):
                    act.wait_ge(s("emb_done"), 2 * c + m + 1)
                    dst = hT[:, m, bass.ds(c * CT, CT)].rearrange("p (b i) -> p b i", i=SEQ)[:, :, 1:SEQ]
                    src = emb[par][m][0:DP, 0:CP].rearrange("p (b i) -> p b i", i=PATCHES)
                    nc.scalar.activation(dst, src, ACT.Identity, bias=bias[:, m, 0:1]).then_inc(s("h_ready"), 1)

            def squares(c):
                act.wait_ge(s("xc_ready"), c + 1)
                nc.scalar.activation(sq[:, :, :], xc[:, :, :], ACT.Square).then_inc(s("sq_ready"), 1)

            def deviation(c):
                act.wait_ge(s("var_done"), c + 1)
                if not isinstance(c, int) or c > 0:
                    act.wait_ge(s("rstd_ready"), c)
                nc.scalar.activation(std[:, :], var_b[0:DP, 0:CT], ACT.Sqrt,
                                     bias=bias[:, 0, 6:7]).then_inc(s("std_ready"), 1)

            def round_patches(c, p):
                for q in range(2):
                    act.wait_ge(s(f"loaded{p}{q}"), 8 * (c - p) + 16)
                    if q == 0 and not (isinstance(c, int) and c < 2):
                        act.wait_ge(s("emb_done"), 2 * c - 2)
                    nc.scalar.activation(xh[p][half(q)], raw[p][half(q)], ACT.Identity).then_inc(s("rounded"), 1)

            round_patches(1, 1)
            embedded(0, 0)
            with act.Fori(0, (CHUNKS - 2) // 2) as it:
                for p in range(2):
                    round_patches(it * 2 + p + 2, p)
                    squares(it * 2 + p)
                    embedded(it * 2 + p + 1, 1 - p)
                    deviation(it * 2 + p)
            squares(CHUNKS - 2)
            embedded(CHUNKS - 1, 1)
            deviation(CHUNKS - 2)
            squares(CHUNKS - 1)
            deviation(CHUNKS - 1)

        @block.vector
        def _(dve):
            dve.wait_ge(s("tok_split"), 1)
            nc.vector.tensor_tensor(tok_lo[:, :, :], tok_w[:, :, :], tok_hi[:, :, :].bitcast(FP32),
                                    ALU.subtract).then_inc(s("tok_split"), 1)
            for q in range(2):
                dve.wait_ge(s("rounded"), q + 1)
                nc.vector.tensor_tensor(xl[0][half(q)], raw[0][half(q)], xh[0][half(q)].bitcast(FP32),
                                        ALU.subtract).then_inc(s("split_first"), 1)
            dve.wait_ge(s("consts"), 48)

            def centre(c):
                dve.wait_ge(s("mean_done"), c + 1)
                if not isinstance(c, int) or c > 0:
                    dve.wait_ge(s("xn_ready"), c)
                nc.vector.tensor_tensor(xc[:, :, :], cols(hT, c),
                                        mean_b[0:DP, 0:CT].unsqueeze(1).broadcast_to([DP, DK, CT]),
                                        ALU.subtract).then_inc(s("xc_ready"), 1)

            def normalise(c):
                dve.wait_ge(s("std_ready"), c + 1)
                nc.vector.reciprocal(rstd[:, :], std[:, :]).then_inc(s("rstd_ready"), 1)
                dve.wait_ge(s("rstd_ready"), c + 1)
                nc.vector.tensor_tensor(cols(xnT, c), xc[:, :, :],
                                        rstd[:, :].unsqueeze(1).broadcast_to([DP, DK, CT]),
                                        ALU.mult).then_inc(s("xn_ready"), 1)

            with dve.Fori(0, CHUNKS) as c:
                centre(c)
                normalise(c)

        @block.gpsimd
        def _(pool):
            pool.wait_ge(s("consts"), 48)
            for m in range(DK):
                dst = hT[:, m, :].rearrange("p (b i) -> p b i", i=SEQ)[:, :, 0]
                last = nc.gpsimd.tensor_copy(dst, bias[:, m, 5:6].broadcast_to([DP, IMGS]))
                last.then_inc(s("cls_written"), 1)

            def split_patches(c, p):
                for q in range(2):
                    pool.wait_ge(s("rounded"), 2 * c + q + 1)
                    nc.gpsimd.tensor_tensor(xl[p][half(q)], raw[p][half(q)], xh[p][half(q)].bitcast(FP32),
                                            ALU.subtract).then_inc(s("split"), 1)

            split_patches(1, 1)
            with pool.Fori(1, CHUNKS // 2) as it:
                for p in range(2):
                    split_patches(it * 2 + p, p)


def attention_stage(nc, t, a):
    with ExitStack() as ctx:
        def sb(name, shape, dt=FP32):
            return ctx.enter_context(nc.sbuf_tensor("b_" + name, shape, dt))

        s = Sems(nc, ctx, "b")
        hT, xnT, bank, bias, ident, w = t["hT"], t["xnT"], t["bank"], t["bias"], t["ident"], t["attn_w"]
        WQ, WK, WV, WO = range(4)
        xs = [sb(f"xs{p}", [DP, DK, GI, 2, PATCHES]) for p in range(2)]
        qT = [sb(f"qT{p}", [DP, DK, CT]) for p in range(2)]
        kT = sb("kT", [DP, DK, GI, SEQ])
        kblk = [sb(f"kblk{p}", [DP, DK, GI, HH * SEQ]) for p in range(2)]
        vblk = [sb(f"vblk{p}", [128, GI, PAIRS, VW]) for p in range(2)]
        vcls_raw = sb("vcls_raw", [CROWS, PAIRS * VW])
        vcls = sb("vcls", [CROWS, PAIRS * VW], FP32R)
        prob = [sb(f"prob{p}", [SEQ, HEADS * PATCHES + 3 * 32]) for p in range(2)]
        top = sb("top", [SEQ, DK, HH])
        probT = sb("probT", [128, PAIRS, SEQ])
        probclsT = sb("probclsT", [CROWS, SEQ], FP32R)
        rsum = sb("rsum", [SEQ, HEADS])
        attn = sb("attn", [SEQ, HEADS, HD])
        attnT = sb("attnT", [DP, DK, CT])
        proj_b = bank[0:2]
        score_b = t["psum"][0:SEQ, 2 * 512:4 * 512].rearrange("p (m n) -> p m n", m=2)[:, :, 0:HH * SEQ]
        pT_b = bank[4]
        cT_b = bank[4][0:CROWS, PAIRS * SEQ:(PAIRS + 1) * SEQ]
        av_b = bank[5][0:SEQ, 0:PAIRS * VW]
        v_b = bank[6][:, 0:2 * D].rearrange("p (i d) -> p i d", i=2)
        aT_b = bank[7][0:DP, 0:DK * SEQ].rearrange("p (m i) -> p m i", m=DK)
        VALUES_AT = [[], [], [0], [1]]
        block = ctx.enter_context(nc.Block())

        def span(x, m, c):
            return x[:, m, bass.ds(c * CT, CT)]

        def class_probs(pi):
            return prob[pi][:, PAIRS * 128:].rearrange("p (r c) -> p r c", c=32)[:, :, 0:HEADS]

        def key_block(eng, par, m):
            eng.tensor_tensor(
                kblk[par][:, m, :, 0:HH * PATCHES].rearrange("p b (h k) -> p b h k", h=HH),
                kT[:, m, :, 1:SEQ].unsqueeze(2).broadcast_to([DP, GI, HH, PATCHES]),
                t["headmask"].unsqueeze(1).unsqueeze(3).broadcast_to([DP, GI, HH, PATCHES]), ALU.mult)
            return eng.tensor_tensor(
                kblk[par][:, m, :, HH * PATCHES:], kT[:, m, :, 0].unsqueeze(2).broadcast_to([DP, GI, HH]),
                t["headmask"].unsqueeze(1).broadcast_to([DP, GI, HH]), ALU.mult)

        @block.tensor
        def _(pe):
            def keys(c, par):
                for m in range(DK):
                    if m == 0 and not (isinstance(c, int) and c == 0):
                        pe.wait_ge(s("q_ready"), 2 * c)
                    for k in range(DK):
                        last = nc.tensor.matmul(proj_b[m][0:DP, 0:CT], w[:, WK, k, m * DP:(m + 1) * DP],
                                                span(xnT, k, c), start=(k == 0), stop=(k == DK - 1))
                    last.then_inc(s("k_done"), 1)

            def queries(c, par):
                for m in range(DK):
                    if isinstance(c, int) and c < 2:
                        pe.wait_ge(s("k_ready"), 2 * c + m + 1)
                    else:
                        pe.wait_ge(s("bank_clear"), 2 * c - 3 + m)
                    for k in range(DK):
                        last = nc.tensor.matmul(proj_b[m][0:DP, 0:CT], w[:, WQ, k, m * DP:(m + 1) * DP],
                                                span(xnT, k, c), start=(k == 0), stop=(k == DK - 1))
                    last.then_inc(s("q_done"), 1)

            def values(c, par, q):
                if q == 0:
                    pe.wait_ge(s("xs_ready"), c + 1)
                if not (isinstance(c, int) and c == 0 and q == 0):
                    pe.wait_ge(s("v_ready_lo"), 2 * c + q)
                    pe.wait_ge(s("v_ready_hi"), 2 * c + q)
                for i in range(2):
                    for k in range(DK):
                        tok = xs[par][:, k, 2 * q + i].rearrange("p e n -> p (e n)")
                        last = nc.tensor.matmul(v_b[:, i, :], tok, w[:, WV, k, :], start=(k == 0), stop=(k == DK - 1))
                last.then_inc(s("v_done"), 1)

            def scores(c, par, i):
                if i == 0:
                    pe.wait_ge(s("q_ready"), 2 * c + 2)
                    if isinstance(c, int) and c == 0:
                        pe.wait_ge(s("kblk_first"), 2)
                    else:
                        pe.wait_ge(s("kblk_ready"), c)
                if not (isinstance(c, int) and c == 0 and i == 0):
                    pe.wait_ge(s("shifted"), 4 * c + i)
                for m in range(DK):
                    last = nc.tensor.matmul(score_b[:, m, :], qT[par][:, m, i * SEQ:(i + 1) * SEQ],
                                            kblk[par][:, m, i, :], start=True, stop=True)
                last.then_inc(s("scores_done"), 1)

            def flip_probs(c, i, pi):
                pe.wait_ge(s("exp_ready"), 4 * c + i + 1)
                if not (isinstance(c, int) and c == 0 and i == 0):
                    pe.wait_ge(s("probT_ready"), 4 * c + i)
                for g in range(PAIRS):
                    nc.tensor.transpose(pT_b[:, g * SEQ:(g + 1) * SEQ], prob[pi][:, g * 128:(g + 1) * 128],
                                        ident[0:SEQ, 0:SEQ])
                nc.tensor.transpose(cT_b, prob[pi][:, PAIRS * 128:PAIRS * 128 + CROWS],
                                    ident[0:SEQ, 0:SEQ]).then_inc(s("pT_done"), 1)

            def weigh(c, par, i):
                pe.wait_ge(s("probT_ready"), 4 * c + i + 1)
                if i % 2 == 0:
                    pe.wait_ge(s("v_ready_lo"), 2 * c + i // 2 + 1)
                    pe.wait_ge(s("v_ready_hi"), 2 * c + i // 2 + 1)
                if not (isinstance(c, int) and c == 0 and i == 0):
                    pe.wait_ge(s("attn_ready"), 4 * c + i)
                for g in range(PAIRS):
                    nc.tensor.matmul(av_b[:, g * VW:(g + 1) * VW], probT[:, g, :], vblk[par][:, i, g, :],
                                     start=(g == 0), stop=False, skip_group_check=True)
                pe.wait_ge(s("probcls_ready"), 4 * c + i + 1)
                nc.tensor.matmul(av_b, probclsT[:, :], vcls[:, :], start=False, stop=True,
                                 skip_group_check=True).then_inc(s("av_done"), 1)

            def flip_attn(n, i, c):
                pe.wait_ge(s("attn_ready"), n + 1)
                if not (isinstance(n, int) and n == 0):
                    pe.wait_ge(s("attnT_ready"), n)
                rows = attn[:, :, :].rearrange("p h d -> p (h d)")
                for m in range(DK):
                    last = nc.tensor.transpose(aT_b[:, m, :], rows[:, m * DP:(m + 1) * DP],
                                               ident[0:SEQ, 0:SEQ])
                last.then_inc(s("aT_done"), 1)

            def output(c, last_use, value):
                pe.wait_ge(s("attnT_ready"), 4 * c + 4)
                pe.wait_ge(s(last_use), value)
                for m in range(DK):
                    for k in range(DK):
                        last = nc.tensor.matmul(proj_b[m][0:DP, 0:CT], w[:, WO, k, m * DP:(m + 1) * DP],
                                                attnT[:, k, :], start=(k == 0), stop=(k == DK - 1))
                    last.then_inc(s("o_done"), 1)

            def step(c, par, prev=True, more=True):
                for i in range(GI):
                    if i < GI - 1:
                        scores(c, par, i + 1)
                    elif more:
                        scores(c + 1, 1 - par, 0)
                    flip_probs(c, i, i % 2)
                    if i > 0:
                        flip_attn(4 * c + i - 1, i - 1, c)
                    elif prev:
                        flip_attn(4 * c - 1, GI - 1, c - 1)
                    if more:
                        if i == 0:
                            keys(c + 1, 1 - par)
                        elif i == 2:
                            queries(c + 1, 1 - par)
                        for v in VALUES_AT[i]:
                            values(c + 1, 1 - par, v)
                    if i == 1 and prev:
                        if more:
                            output(c - 1, "k_ready", 2 * c + 4)
                        else:
                            output(c - 1, "q_ready", 2 * c + 2)
                    if (i != 1 and not more) or (i == 1 and not prev):
                        stay_awake(nc, t, bank[6], 5)
                    weigh(c, par, i)

            keys(0, 0)
            for k in range(DK):
                last = nc.tensor.matmul(v_b[0:CROWS, 0, :], xnT[:, k, 0:1].broadcast_to([DP, CROWS]),
                                        w[:, WV, k, :], start=(k == 0), stop=(k == DK - 1))
            last.then_inc(s("vcls_done"), 1)
            queries(0, 0)
            pe.wait_ge(s("vcls_ready"), 1)
            for q in range(2):
                values(0, 0, q)
            stay_awake(nc, t, bank[7], 4)
            scores(0, 0, 0)
            stay_awake(nc, t, bank[7], 10)
            step(0, 0, prev=False)
            with pe.Fori(0, (CHUNKS - 2) // 2) as it:
                for p in range(2):
                    step(it * 2 + 1 + p, (1 + p) % 2)
            step(CHUNKS - 1, 1, more=False)
            stay_awake(nc, t, bank[6], 4)
            flip_attn(IMGS - 1, GI - 1, CHUNKS - 1)
            stay_awake(nc, t, bank[6], 5)
            output(CHUNKS - 1, "bank_clear", 2 * CHUNKS - 2)
            stay_awake(nc, t, bank[6], 8)

        @block.scalar
        def _(act):
            def exponent(n, pi):
                act.wait_ge(s("shifted"), n + 1)
                patch, cls = prob[pi][:, 0:PAIRS * 128], class_probs(pi)
                nc.scalar.activation(patch, patch, ACT.Exp)
                nc.scalar.activation(cls, cls, ACT.Exp).then_inc(s("exp_ready"), 1)

            def probs_out(n):
                act.wait_ge(s("pT_done"), n + 1)
                nc.scalar.activation(probT[:, :, :].rearrange("p g q -> p (g q)"), pT_b[:, 0:PAIRS * SEQ], ACT.Identity)
                nc.scalar.activation(probclsT[:, :], cT_b, ACT.Identity).then_inc(s("probT_ready"), 1)

            def keys_out(c):
                for m in range(DK):
                    act.wait_ge(s("k_done"), 2 * c + m + 1)
                    if m == 0 and isinstance(c, int) and c == 1:
                        act.wait_ge(s("kblk_first"), 2)
                    elif m == 0 and not (isinstance(c, int) and c == 0):
                        act.wait_ge(s("kblk_ready"), c - 1)
                    nc.scalar.activation(kT[:, m].rearrange("p b k -> p (b k)"), proj_b[m][0:DP, 0:CT], ACT.Identity,
                                         bias=bias[:, m, 2:3]).then_inc(s("k_ready"), 1)

            def values_lo(c, par, q, first):
                act.wait_ge(s("v_done"), 2 * c + q + 1)
                if not first:
                    act.wait_ge(s("av_done"), 4 * c + 2 * q - 6)
                src = v_b[0:64].rearrange("p i (g e d) -> p i g e d", g=PAIRS, e=2)[:, :, :, 0, :]
                nc.scalar.activation(vblk[par][0:64, 2 * q:2 * q + 2, :, 0:HD], src,
                                     ACT.Identity).then_inc(s("v_ready_lo"), 1)

            def attn_out(n, i, c):
                act.wait_ge(s("aT_done"), n + 1)
                if i == 0 and not (isinstance(c, int) and c == 0):
                    act.wait_ge(s("o_done"), 2 * c)
                for m in range(DK):
                    last = nc.scalar.activation(attnT[:, m, i * SEQ:(i + 1) * SEQ], aT_b[:, m, :], ACT.Identity,
                                                bias=bias[:, m, 3:4])
                last.then_inc(s("attnT_ready"), 1)

            def step(c, par, prev=True, more=True, fresh=False):
                for i in range(GI):
                    exponent(4 * c + i, i % 2)
                    probs_out(4 * c + i)
                    if i > 0:
                        attn_out(4 * c + i - 1, i - 1, c)
                    elif prev:
                        attn_out(4 * c - 1, GI - 1, c - 1)
                    if more:
                        if i == 0:
                            keys_out(c + 1)
                        for v in VALUES_AT[i]:
                            values_lo(c + 1, 1 - par, v, fresh)

            for m in range(DK):
                src = xnT[:, m, 0:CT].rearrange("p (b i) -> p b i", i=SEQ)[:, :, 1:SEQ]
                for e in range(2):
                    last = nc.scalar.activation(xs[0][:, m, :, e, :], src, ACT.Identity)
            last.then_inc(s("xs_ready"), 1)
            nc.scalar.activation(t["d_hi0"], t["d_raw0"], ACT.Identity)
            keys_out(0)
            act.wait_ge(s("blocks_clear"), 1)
            for q in range(2):
                values_lo(0, 0, q, True)
            nc.scalar.activation(t["gu_hi0"], t["gu_raw0"], ACT.Identity).then_inc(s("expert_hi"), 1)
            step(0, 0, prev=False, fresh=True)
            with act.Fori(0, (CHUNKS - 2) // 2) as it:
                for p in range(2):
                    step(it * 2 + 1 + p, (1 + p) % 2)
            step(CHUNKS - 1, 1, more=False)
            attn_out(IMGS - 1, GI - 1, CHUNKS - 1)

        @block.vector
        def _(dve):
            def shift(c, i, pi):
                n = 4 * c + i
                dve.wait_ge(s("scores_done"), n + 1)
                patch = score_b[:, :, 0:HH * PATCHES].rearrange("p m (h k) -> p m h k", h=HH)
                cls = score_b[:, :, HH * PATCHES:]
                nc.vector.tensor_reduce(top[:, :, :], patch, AX.X, ALU.max).then_inc(s("patch_top"), 1)
                dve.wait_ge(s("patch_top"), n + 1)
                nc.vector.tensor_tensor(top[:, :, :], top[:, :, :], cls, ALU.max).then_inc(s("top_ready"), 1)
                dve.wait_ge(s("top_ready"), n + 1)
                if not (isinstance(c, int) and 4 * c + i < 2):
                    dve.wait_ge(s("pT_done"), n - 1)
                nc.vector.tensor_tensor(class_probs(pi).rearrange("p r (m h) -> p r m h", m=DK),
                                        cls.unsqueeze(1).broadcast_to([SEQ, 3, DK, HH]),
                                        top[:, :, :].unsqueeze(1).broadcast_to([SEQ, 3, DK, HH]), ALU.subtract)
                nc.vector.tensor_tensor(
                    prob[pi][:, 0:PAIRS * 128].rearrange("p (m h k) -> p m h k", m=DK, h=HH), patch,
                    top[:, :, :].unsqueeze(3).broadcast_to([SEQ, DK, HH, PATCHES]),
                    ALU.subtract).then_inc(s("shifted"), 1)

            def class_rest(n):
                dve.wait_ge(s("probT_ready"), n + 1)
                mid = slice(32, 32 + HEADS)
                nc.vector.tensor_tensor(probclsT[mid, :], cT_b[mid, :], probclsT[mid, :].bitcast(FP32),
                                        ALU.subtract).then_inc(s("probcls_ready"), 1)

            def queries_out(c, par):
                for m in range(DK):
                    dve.wait_ge(s("q_done"), 2 * c + m + 1)
                    if m == 0 and not (isinstance(c, int) and c < 2):
                        dve.wait_ge(s("scores_done"), 4 * c - 4)
                    nc.vector.tensor_scalar(qT[par][:, m, :], proj_b[m][0:DP, 0:CT], bias[:, m, 1:2], HD ** -0.5,
                                            ALU.add, ALU.mult).then_inc(s("q_ready"), 1)

            def values_hi(c, par, q, first):
                dve.wait_ge(s("v_done"), 2 * c + q + 1)
                if not first:
                    dve.wait_ge(s("av_done"), 4 * c + 2 * q - 6)
                src = v_b[64:128].rearrange("p i (g e d) -> p i g e d", g=PAIRS, e=2)[:, :, :, 1, :]
                nc.vector.tensor_copy(vblk[par][64:128, 2 * q:2 * q + 2, :, HD + 1:VW - 1],
                                      src).then_inc(s("v_ready_hi"), 1)

            def attend(n):
                dve.wait_ge(s("av_done"), n + 1)
                av = av_b.rearrange("p (h d) -> p h d", h=HEADS)
                nc.vector.reciprocal(rsum[:, :], av[:, :, HD]).then_inc(s("rsum_ready"), 1)
                dve.wait_ge(s("rsum_ready"), n + 1)
                nc.vector.tensor_tensor(attn[:, :, :], av[:, :, 0:HD],
                                        rsum[:, :].unsqueeze(2).broadcast_to([SEQ, HEADS, HD]),
                                        ALU.mult).then_inc(s("attn_ready"), 1)

            def residual(c):
                for m in range(DK):
                    dve.wait_ge(s("o_done"), 2 * c + m + 1)
                    nc.vector.scalar_tensor_tensor(span(hT, m, c), proj_b[m][0:DP, 0:CT], bias[:, m, 4:5],
                                                   span(hT, m, c), ALU.add, ALU.add).then_inc(s("bank_clear"), 1)

            def step(c, par, prev=True, more=True, fresh=False):
                for i in range(GI):
                    if i < GI - 1:
                        shift(c, i + 1, (i + 1) % 2)
                    elif more:
                        shift(c + 1, 0, 0)
                    class_rest(4 * c + i)
                    if more:
                        if i == 2:
                            queries_out(c + 1, 1 - par)
                        for v in VALUES_AT[i]:
                            values_hi(c + 1, 1 - par, v, fresh)
                    if i == 1 and prev:
                        residual(c - 1)
                    attend(4 * c + i)

            dve.wait_ge(s("vcls_done"), 1)
            vc = vcls_raw[:, :].rearrange("p (h d) -> p h d", h=HEADS)
            nc.vector.tensor_tensor(vc[:, :, 0:HD], v_b[0:CROWS, 0, :].rearrange("p (h d) -> p h d", h=HEADS),
                                    t["clsmask"][:, :].unsqueeze(2).broadcast_to([CROWS, HEADS, HD]), ALU.mult)
            nc.vector.tensor_copy(vc[:, :, HD], t["clsmask"][:, :]).then_inc(s("vcls_raw"), 1)
            dve.wait_ge(s("vcls_raw"), 1)
            nc.vector.tensor_copy(vcls[:, :], vcls_raw[:, :]).then_inc(s("vcls_rounded"), 1)
            dve.wait_ge(s("vcls_rounded"), 1)
            low = slice(64, CROWS)
            nc.vector.tensor_tensor(vcls[low, :], vcls_raw[low, :], vcls[low, :].bitcast(FP32),
                                    ALU.subtract).then_inc(s("vcls_ready"), 1)
            dve.wait_ge(s("k_ready"), 1)
            key_block(nc.vector, 0, 0).then_inc(s("kblk_first"), 1)
            queries_out(0, 0)
            dve.wait_ge(s("blocks_clear"), 1)
            for q in range(2):
                values_hi(0, 0, q, True)
            shift(0, 0, 0)
            step(0, 0, prev=False, fresh=True)
            with dve.Fori(0, (CHUNKS - 2) // 2) as it:
                for p in range(2):
                    step(it * 2 + 1 + p, (1 + p) % 2)
            step(CHUNKS - 1, 1, more=False)
            residual(CHUNKS - 1)

        @block.gpsimd
        def _(pool):
            def copy_chunk(c, par):
                if not (isinstance(c, int) and c < 2):
                    pool.wait_ge(s("v_done"), 2 * c - 2)
                for m in range(DK):
                    src = xnT[:, m, bass.ds(c * CT, CT)].rearrange("p (b i) -> p b i", i=SEQ)[:, :, 1:SEQ]
                    last = nc.gpsimd.tensor_copy(xs[par][:, m],
                                                 src.unsqueeze(2).broadcast_to([DP, GI, 2, PATCHES]))
                last.then_inc(s("xs_ready"), 1)

            def key_blocks(c, par):
                pool.wait_ge(s("k_ready"), 2 * c + 2)
                if not (isinstance(c, int) and c < 2):
                    pool.wait_ge(s("scores_done"), 4 * c - 4)
                for m in range(DK):
                    last = key_block(nc.gpsimd, par, m)
                last.then_inc(s("kblk_ready"), 1)

            for v in vblk:
                last = nc.gpsimd.memset(v[:, :, :, :], 0.0)
            for p in prob:
                last = nc.gpsimd.memset(p[:, PAIRS * 128:], 0.0)
            last.then_inc(s("zeroed"), 1)
            pool.wait_ge(s("zeroed"), 1)
            for v in vblk:
                nc.gpsimd.memset(v[0:64, :, :, HD:HD + 1], 1.0)
                last = nc.gpsimd.memset(v[64:128, :, :, VW - 1:VW], 1.0)
            last.then_inc(s("blocks_clear"), 1)
            pool.wait_ge(s("blocks_clear"), 1)
            pool.wait_ge(s("k_ready"), 2)
            key_block(nc.gpsimd, 0, 1).then_inc(s("kblk_first"), 1)
            copy_chunk(1, 1)
            key_blocks(1, 1)
            with pool.Fori(0, (CHUNKS - 2) // 2) as it:
                for p in range(2):
                    copy_chunk(it * 2 + 2 + p, p)
                    key_blocks(it * 2 + 2 + p, p)
            pool.wait_ge(s("expert_hi"), 1)
            nc.gpsimd.tensor_tensor(t["gu_lo0"], t["gu_raw0"], t["gu_hi0"].bitcast(FP32), ALU.subtract)
            nc.gpsimd.tensor_tensor(t["d_lo0"], t["d_raw0"], t["d_hi0"].bitcast(FP32), ALU.subtract)


def table_stage(nc, t, a, table):
    with ExitStack() as ctx:
        def sb(name, shape, dt=FP32):
            return ctx.enter_context(nc.sbuf_tensor("c_" + name, shape, dt))

        s = Sems(nc, ctx, "c")
        hT, bank, bias, ident, rows = t["hT"], t["bank"], t["bias"], t["ident"], t["rows"]
        xc = [sb(f"xc{p}", [DP, DK, NT]) for p in range(2)]
        sq = sb("sq", [DP, DK, NT])
        std = sb("std", [DP, NT])
        rstd = sb("rstd", [DP, NT])
        xn = [sb(f"xn{p}", [DP, DK, NT]) for p in range(2)]
        mean_b = [bank[p][0:DP, 0:NT] for p in range(2)]
        var_b = [bank[2 + p][0:DP, 0:NT] for p in range(2)]
        row_b = [[bank[4 + 2 * p + j][0:TT] for j in range(NJ)] for p in range(2)]
        block = ctx.enter_context(nc.Block())

        EARLY = NJ * (NARROW - 2)

        def least(c, n):
            return isinstance(c, int) and c < n

        def chunks(eng, step):
            for c in range(2):
                step(c, c, 2)
            with eng.Fori(1, NARROW // 2 - 1) as it:
                for p in range(2):
                    step(it * 2 + p, p, 2)
            for c in range(NARROW - 2, NARROW):
                step(c, c % 2, NARROW - 1 - c)

        @block.tensor
        def _(pe):
            def mean(c, p):
                if not least(c, 2):
                    pe.wait_ge(s("xc_ready"), c - 1)
                for m in range(DK):
                    last = nc.tensor.matmul(mean_b[p], t["avg"], hT[:, m, bass.ds(c * NT, NT)], start=(m == 0),
                                            stop=(m == DK - 1))
                last.then_inc(s("mean_done"), 1)

            def var(c, p):
                pe.wait_ge(s("sq_ready"), c + 1)
                if not least(c, 2):
                    pe.wait_ge(s("std_ready"), c - 1)
                for m in range(DK):
                    last = nc.tensor.matmul(var_b[p], t["avg"], sq[:, m, :], start=(m == 0), stop=(m == DK - 1))
                last.then_inc(s("var_done"), 1)

            def tiles(c, p):
                pe.wait_ge(s("xn_ready"), c + 1)
                if not least(c, 2):
                    pe.wait_ge(s("row_ready"), NJ * (c - 1))
                for j in range(NJ):
                    tokens = slice(j * TT, (j + 1) * TT)
                    for k in range(DK):
                        nc.tensor.matmul(row_b[p][j][:, D:D + E], xn[p][:, k, tokens], t["gate_w"][:, k, :],
                                         start=(k == 0), stop=(k == DK - 1))
                    for k in range(DK):
                        last = nc.tensor.transpose(row_b[p][j][:, k * DP:(k + 1) * DP], xn[p][:, k, tokens],
                                                   ident[0:DP, 0:DP])
                    last.then_inc(s("tile_done"), 1)

            mean(0, 0)
            mean(1, 1)
            stay_awake(nc, t, bank[7], 8)
            var(0, 0)
            stay_awake(nc, t, bank[7], 8)

            def step(c, p, ahead):
                if ahead > 1:
                    mean(c + 2, p)
                if ahead == 1:
                    stay_awake(nc, t, bank[0], 3)
                if ahead > 0:
                    var(c + 1, 1 - p)
                if ahead < 2:
                    stay_awake(nc, t, bank[0], 3 if ahead else 6)
                tiles(c, p)

            chunks(pe, step)
            stay_awake(nc, t, bank[0], 7)

        @block.scalar
        def _(act):
            def square(c, p):
                act.wait_ge(s("xc_ready"), c + 1)
                if not least(c, 1):
                    act.wait_ge(s("var_done"), c)
                nc.scalar.activation(sq[:, :, :], xc[p][:, :, :], ACT.Square).then_inc(s("sq_ready"), 1)

            def deviation(c, p):
                act.wait_ge(s("var_done"), c + 1)
                if not least(c, 1):
                    act.wait_ge(s("rstd_ready"), c)
                nc.scalar.activation(std[:, :], var_b[p], ACT.Sqrt, bias=bias[:, 0, 6:7]).then_inc(s("std_ready"), 1)

            def copy_rows(c, p):
                for j in range(NJ):
                    act.wait_ge(s("tile_done"), NJ * c + j + 1)
                    row = rows[:, c * NJ + j, :] if isinstance(c, int) else rows[:, bass.ds(c * NJ + j, 1), :].rearrange(
                        "p o r -> p (o r)")
                    nc.scalar.activation(row[:, 0:D], row_b[p][j][:, 0:D], ACT.Identity)
                    nc.scalar.activation(row[:, D:TURN], row_b[p][j][:, MAIN:D], ACT.Identity)
                    nc.scalar.activation(row[:, TURN:ROW], row_b[p][j][:, D:D + E],
                                         ACT.Identity).then_inc(s("row_ready"), 1)

            def scores(start, stop):
                act.wait_ge(s("row_ready"), stop)
                nc.scalar.activation(rows[:, start:stop, TURN:ROW], rows[:, start:stop, TURN:ROW],
                                     ACT.Sigmoid).then_inc(s("score_ready"), 1)

            def step(c, p, ahead):
                if ahead > 0:
                    square(c + 1, 1 - p)
                if not least(c, 1):
                    copy_rows(c - 1, 1 - p)
                if ahead > 0:
                    deviation(c + 1, 1 - p)
                act.wait_ge(s("xn_ready"), c + 1)
                nc.scalar.activation(t["xn_hi"][:, :, bass.ds(c * NT, NT)], xn[p][:, :, :],
                                     ACT.Identity).then_inc(s("rounded"), 1)
                if ahead == 1:
                    scores(0, EARLY)

            nc.scalar.activation(t["shared_hi"], t["shared_gu"], ACT.Identity).then_inc(s("shared_hi"), 1)
            square(0, 0)
            deviation(0, 0)
            chunks(act, step)
            copy_rows(NARROW - 1, 1)
            scores(EARLY, TILES)

        @block.vector
        def _(dve):
            def centre(c, p):
                dve.wait_ge(s("mean_done"), c + 1)
                if not least(c, 2):
                    dve.wait_ge(s("xn_ready"), c - 1)
                nc.vector.tensor_tensor(xc[p][:, :, :], hT[:, :, bass.ds(c * NT, NT)],
                                        mean_b[p].unsqueeze(1).broadcast_to([DP, DK, NT]),
                                        ALU.subtract).then_inc(s("xc_ready"), 1)

            def normalise(c, p):
                dve.wait_ge(s("std_ready"), c + 1)
                if not least(c, 1):
                    dve.wait_ge(s("xn_ready"), c)
                nc.vector.reciprocal(rstd[:, :], std[:, :]).then_inc(s("rstd_ready"), 1)
                dve.wait_ge(s("rstd_ready"), c + 1)
                if not least(c, 2):
                    dve.wait_ge(s("tile_done"), NJ * (c - 1))
                    dve.wait_ge(s("kept"), c - 1)
                nc.vector.tensor_tensor(xn[p][:, :, :], xc[p][:, :, :],
                                        rstd[:, :].unsqueeze(1).broadcast_to([DP, DK, NT]),
                                        ALU.mult).then_inc(s("xn_ready"), 1)

            def step(c, p, ahead):
                if ahead > 0:
                    centre(c + 1, 1 - p)
                normalise(c, p)

            centre(0, 0)
            chunks(dve, step)

        @block.gpsimd
        def _(pool):
            def rest(c, p, ahead):
                pool.wait_ge(s("rounded"), c + 1)
                cols = (slice(None), slice(None), bass.ds(c * NT, NT))
                nc.gpsimd.tensor_tensor(t["xn_lo"][cols], xn[p][:, :, :], t["xn_hi"][cols].bitcast(FP32),
                                        ALU.subtract).then_inc(s("kept"), 1)

            pool.wait_ge(s("shared_hi"), 1)
            nc.gpsimd.tensor_tensor(t["shared_lo"], t["shared_gu"], t["shared_hi"].bitcast(FP32), ALU.subtract)
            chunks(pool, rest)

        @block.sync
        def _(sp):
            sp.wait_ge(s("score_ready"), 2)
            sp.dma_start(table.rearrange("(i t) r -> t i r", t=TT), rows).then_inc(t["table_out"], 16)


def shared_stage(nc, t, a, out):
    with ExitStack() as ctx:
        def sb(name, shape, dt=FP32):
            return ctx.enter_context(nc.sbuf_tensor("d_" + name, shape, dt))

        s = Sems(nc, ctx, "d")
        hT, bank, ident, rows, limit = t["hT"], t["bank"], t["ident"], t["rows"], t["limit"]
        wh, wl, xh, xl, wd = t["shared_hi"], t["shared_lo"], t["xn_hi"], t["xn_lo"], t["shared_d"]
        hc = [sb(f"hc{p}", [DP, DK, WT]) for p in range(2)]
        gate = [sb(f"gate{p}", [128, WT]) for p in range(2)]
        up = [sb(f"up{p}", [128, WT]) for p in range(2)]
        hid = sb("hid", [128, FST, WT])
        base = [sb(f"base{p}", [TT, D]) for p in range(2)]
        reach = sb("reach", [TT, TILES, E], FP16)
        part = sb("part", [TT, E], FP16)
        back = sb("back", [TT, E], U32)
        gate_b, up_b = bank[0:2], bank[2:4]
        down_b = bank[4:6]
        count_b = bank[6][0:TT, 0:E]
        score = rows[:, :, TURN:ROW]
        block = ctx.enter_context(nc.Block())

        def first(c):
            return isinstance(c, int) and c == 0

        @block.sync
        def _(sp):
            def store(c, js):
                for j in js:
                    sp.wait_ge(s("base_ready"), 4 * c + j + 1)
                    sp.dma_start(out[bass.ds((c * WJ + j) * TT, TT), :], base[j % 2][:, :]).then_inc(t["base_out"][j % 2], 16)

            store(0, range(WJ))
            with sp.Fori(1, WIDE) as c:
                store(c, range(WJ))

        @block.tensor
        def _(pe):
            def gate_up(c, f, g, k):
                n = c * FST + f
                b, read, done = ((gate_b, "gate_ready", "gate_done"), (up_b, "up_ready", "up_done"))[g]
                if k == 0 and not (isinstance(n, int) and n < 2):
                    pe.wait_ge(s(read), n - 1)
                tile = slice(f * 128, (f + 1) * 128)
                for i, (wt, x) in enumerate(((wh, xh), (wl, xh), (wh, xl))):
                    last = nc.tensor.matmul(b[f % 2][:, 0:WT], wt[:, g, k, tile], x[:, k, bass.ds(c * WT, WT)],
                                            start=(k == 0 and i == 0), stop=(k == DK - 1 and i == 2))
                if k == DK - 1:
                    last.then_inc(s(done), 1)

            def down(c, par, j, step=None):
                if j == 0:
                    pe.wait_ge(s("hc_ready"), c + 1)
                if not (first(c) and j < 2):
                    pe.wait_ge(s("base_ready"), 4 * c + j - 1)
                b = down_b[j % 2][0:TT, 0:D]
                for k in range(DK):
                    nc.tensor.matmul(b[:, k * DP:(k + 1) * DP], hc[par][:, k, j * TT:(j + 1) * TT],
                                     ident[0:DP, 0:DP], start=(k == 0), stop=False, skip_group_check=True)
                for f in range(FST):
                    if f == FST - 1 and step is not None:
                        count(step)
                    if j == 0:
                        pe.wait_ge(s("hid_ready"), 3 * c + f + 1)
                    last = nc.tensor.matmul(b, hid[:, f, j * TT:(j + 1) * TT], wd[:, f, :], start=False,
                                            stop=(f == FST - 1), skip_group_check=True)
                last.then_inc(s("down_done"), 1)

            def count(n):
                pe.wait_ge(s("part_ready"), n + 1)
                nc.tensor.matmul(count_b, t["ones"][0:TT, 0:TT], part[:, :], start=True,
                                 stop=True).then_inc(s("counted"), 1)

            GU_AT = (4, 7, 10)

            def chunk(c, par):
                q = c * STEPS
                halves = [(f, g, k) for f in range(FST) for g in range(2) for k in range(DK)]
                for n, (f, g, k) in enumerate(halves):
                    gate_up(c, f, g, k)
                    if n + 1 in GU_AT:
                        count(q + GU_AT.index(n + 1))
                down(c, par, 0, q + 3)
                down(c, par, 1)
                count(q + 4)
                down(c, par, 2)
                down(c, par, 3, q + 5)

            chunk(0, 0)
            with pe.Fori(0, (WIDE - 1) // 2) as it:
                for p in range(2):
                    chunk(it * 2 + 1 + p, 1 - p)

        @block.scalar
        def _(act):
            def chunk(c):
                for f in range(FST):
                    n = c * FST + f
                    act.wait_ge(s("gate_done"), n + 1)
                    if not (isinstance(n, int) and n < 2):
                        act.wait_ge(s("hid_ready"), n - 1)
                    nc.scalar.activation(gate[f % 2][:, :], gate_b[f % 2][:, 0:WT], ACT.Silu).then_inc(s("gate_ready"), 1)
                    act.wait_ge(s("up_done"), n + 1)
                    nc.scalar.activation(up[f % 2][:, :], up_b[f % 2][:, 0:WT], ACT.Identity).then_inc(s("up_ready"), 1)
                for j in range(WJ):
                    act.wait_ge(s("down_done"), 4 * c + j + 1)
                    if not (first(c) and j < 2):
                        act.wait_ge(t["base_out"][j % 2], 16 * (2 * c + j // 2))
                    nc.scalar.activation(base[j % 2][:, :], down_b[j % 2][0:TT, 0:D],
                                         ACT.Identity).then_inc(s("base_ready"), 1)

            chunk(0)
            with act.Fori(1, WIDE) as c:
                chunk(c)

        @block.vector
        def _(dve):
            def reached(n):
                nc.vector.tensor_tensor(reach[:, :, :], score, limit.bitcast(FP32).unsqueeze(1).broadcast_to([TT, TILES, E]),
                                        ALU.is_ge).then_inc(s("reach_ready"), 1)
                dve.wait_ge(s("reach_ready"), n + 1)
                if not (isinstance(n, int) and n == 0):
                    dve.wait_ge(s("counted"), n)
                with nc.allow_low_precision(reason="counts up to TILES are exact"):
                    nc.vector.tensor_reduce(part[:, :], reach[:, :, :].rearrange("p i e -> p e i"), AX.X,
                                            ALU.add).then_inc(s("part_ready"), 1)

            def settle(n):
                dve.wait_ge(s("counted"), n + 1)
                nc.vector.tensor_scalar(back[:, :], count_b, float(CAP), t["bitf"][:, bass.ds(n, 1)], ALU.is_lt,
                                        ALU.mult).then_inc(s("back_ready"), 1)
                dve.wait_ge(s("back_ready"), n + 1)
                nc.vector.scalar_tensor_tensor(limit, back[:, :], t["bitu"][:, bass.ds(n, 1)], limit, ALU.bitwise_or,
                                               ALU.bitwise_xor).then_inc(s("limit_ready"), 1)
                dve.wait_ge(s("limit_ready"), n + 2)

            def chunk(c):
                for q in range(STEPS):
                    reached(c * STEPS + q)
                    settle(c * STEPS + q)

            nc.vector.memset(limit, 1 << (BITS - 1)).then_inc(s("limit_ready"), 1)
            dve.wait_ge(s("limit_ready"), 1)
            chunk(0)
            with dve.Fori(1, WIDE) as c:
                chunk(c)

        @block.gpsimd
        def _(pool):
            def copy_chunk(c, par):
                if not (isinstance(c, int) and c < 2):
                    pool.wait_ge(s("down_done"), 4 * c - 4)
                nc.gpsimd.tensor_copy(hc[par][:, :, :], hT[:, :, bass.ds(c * WT, WT)]).then_inc(s("hc_ready"), 1)

            def hidden(c):
                for f in range(FST):
                    n = c * FST + f
                    pool.wait_ge(s("gate_ready"), n + 1)
                    pool.wait_ge(s("up_ready"), n + 1)
                    if f == 0 and not first(c):
                        pool.wait_ge(s("down_done"), 4 * c)
                    nc.gpsimd.tensor_tensor(hid[:, f, :], gate[f % 2][:, :], up[f % 2][:, :],
                                            ALU.mult).then_inc(s("hid_ready"), 1)

            copy_chunk(0, 0)
            hidden(0)
            with pool.Fori(0, (WIDE - 1) // 2) as it:
                for p in range(2):
                    copy_chunk(it * 2 + 1 + p, 1 - p)
                    hidden(it * 2 + 1 + p)


def slot_stage(nc, t, a):
    with ExitStack() as ctx:
        def sb(name, shape, dt=FP32):
            return ctx.enter_context(nc.sbuf_tensor("e_" + name, shape, dt))

        s = Sems(nc, ctx, "e")
        bank, rows, limit = t["bank"], t["rows"], t["limit"]
        N = E * TILES
        above = sb("above", [TT, N], FP16)
        equal = sb("equal", [TT, N], FP16)
        run = [sb(f"run{i}", [TT, N], FP16) for i in range(2)]
        room = sb("room", [TT, E])
        rank = sb("rank", [TT, N])
        fits = sb("fits", [TT, N])
        slot = sb("slot", [TT, N])
        third = sb("third", [TT, N])
        third2 = sb("third2", [TT, N])
        above_b, equal_b, total_b = bank[0][0:TT, 0:N], bank[1][0:TT, 0:N], bank[2][0:TT, 0:E]
        score = rows[:, :, TURN:ROW].rearrange("p i e -> p e i")
        lim = limit.bitcast(FP32).unsqueeze(2).broadcast_to([TT, E, TILES])
        block = ctx.enter_context(nc.Block())

        def by_expert(x):
            return x.rearrange("p (e i) -> p e i", e=E)

        @block.sync
        def _(sp):
            sp.wait_ge(t["table_out"], 16)
            for p in range(2):
                sp.wait_ge(t["base_out"][p], 16 * TILES // 2)

        @block.vector
        def _(dve):
            done = [0]

            def then(ins):
                done[0] += 1
                ins.then_inc(s("step"), 1)
                dve.wait_ge(s("step"), done[0])

            nc.vector.tensor_tensor(by_expert(above[:, :]), score, lim, ALU.is_gt)
            then(nc.vector.tensor_tensor(by_expert(equal[:, :]), score, lim, ALU.is_equal))
            for m, r in ((above, run[0]), (equal, run[1])):
                last = nc.vector.tensor_tensor_scan(r[:, :], t["restart"], m[:, :], 0.0, ALU.mult, ALU.add)
            last.then_inc(s("run_ready"), 1)
            dve.wait_ge(s("ranked"), 1)
            then(nc.vector.tensor_scalar(room[:, :], total_b, -1.0, float(CAP), ALU.mult, ALU.add))
            then(nc.vector.tensor_copy(rank[:, :], equal_b))
            room_bc = room[:, :].unsqueeze(2).broadcast_to([TT, E, TILES])
            then(nc.vector.tensor_tensor(by_expert(fits[:, :]), by_expert(rank[:, :]), room_bc, ALU.is_lt))
            then(nc.vector.tensor_tensor(fits[:, :], fits[:, :], equal[:, :], ALU.mult))
            then(nc.vector.tensor_tensor(fits[:, :], fits[:, :], above[:, :], ALU.add))
            then(nc.vector.tensor_tensor(by_expert(rank[:, :]), by_expert(rank[:, :]), room_bc, ALU.min))
            then(nc.vector.tensor_tensor(slot[:, :], above_b, rank[:, :], ALU.add))
            then(nc.vector.scalar_tensor_tensor(slot[:, :], slot[:, :], 1.0, fits[:, :], ALU.add, ALU.mult))
            then(nc.vector.tensor_scalar(slot[:, :], slot[:, :], -1.0, None, ALU.add))
            then(nc.vector.tensor_scalar(third[:, :], slot[:, :], float(SLOTP), None, ALU.is_ge))
            then(nc.vector.tensor_scalar(third2[:, :], slot[:, :], float(2 * SLOTP), None, ALU.is_ge))
            then(nc.vector.tensor_tensor(third[:, :], third[:, :], third2[:, :], ALU.add))
            then(nc.vector.scalar_tensor_tensor(t["slotp"], third[:, :], -float(SLOTP), slot[:, :], ALU.mult, ALU.add))
            for b in range(3):
                last = nc.vector.scalar_tensor_tensor(
                    t["slotid"][:, :, :, b], by_expert(third[:, :]), float(b),
                    t["ids"].unsqueeze(1).broadcast_to([TT, E, TILES]), ALU.is_equal, ALU.mult)
            then(last)

        @block.tensor
        def _(pe):
            stay_awake(nc, t, bank[3], 7)
            pe.wait_ge(s("run_ready"), 1)
            for m, r, b in ((above, run[0], above_b), (equal, run[1], equal_b)):
                nc.tensor.matmul(b, t["ones"][0:TT, 0:TT], r[:, :], start=True, stop=False)
                nc.tensor.matmul(b, t["before"], m[:, :], start=False, stop=True)
            nc.tensor.matmul(total_b, t["ones"][0:TT, 0:TT], by_expert(run[0][:, :])[:, :, TILES - 1], start=True,
                             stop=True).then_inc(s("ranked"), 1)
            stay_awake(nc, t, bank[3], 32)


def expert_stage(nc, t, a, table, out):
    with ExitStack() as ctx:
        def sb(name, shape, dt=FP32):
            return ctx.enter_context(nc.sbuf_tensor("f_" + name, shape, dt))

        s = Sems(nc, ctx, "f")
        bank, ident = t["bank"], t["ident"]
        raw, hi, lo = ([(t[f"gu_{kind}{q}"], t[f"d_{kind}{q}"]) for q in range(2)] for kind in ("raw", "hi", "lo"))
        hot = [sb(f"hot{p}", [TT, TILES, SLOTP], FP16) for p in range(2)]
        slotid = [sb(f"slotid{p}", [TT, TILES, 3], FP16) for p in range(2)]
        listed = sb("listed", [3, SLOTP])
        ids = [sb(f"ids{p}", [SLOTP, 3], U32) for p in range(2)]
        ids_out = [sb(f"ids_out{p}", [SLOTP, 3], U32) for p in range(2)]
        got = [sb(f"got{p}", [SLOTP, 3, ROW]) for p in range(2)]
        score = [sb(f"score{p}", [SLOTP, 3]) for p in range(2)]
        x_hi = sb("x_hi", [128, CAP], FP32R)
        x_lo = sb("x_lo", [128, CAP], FP32R)
        x_tail = sb("x_tail", [128, CAP], FP32R)
        gate = [sb(f"gate{p}", [128, CAP]) for p in range(2)]
        hid = [sb(f"hid{p}", [128, CAP]) for p in range(2)]
        hid_hi = sb("hid_hi", [128, FET, CAP], FP32R)
        hid_lo = sb("hid_lo", [128, FET, CAP], FP32R)
        y = [sb(f"y{p}", [SLOTP, 3, D]) for p in range(2)]
        gate_b, up_b = bank[0:2], bank[2:4]
        x_b = [b[:, 0:CAP] for b in bank[4:6]]
        down_b = [bank[6][:, 0:D], bank[7][:, 0:D], bank[4][:, 0:D]]
        list_b = bank[5][0:3, 272:272 + SLOTP]
        ids_b = bank[5][0:SLOTP, 480:483]
        block = ctx.enter_context(nc.Block())

        def least(e, n):
            return isinstance(e, int) and e < n

        def loads_of(e, p):
            return 8 * (e - p) + 16

        def experts(eng, body):
            for e in range(2):
                body(e, e, 3)
            with eng.Fori(1, E // 2 - 2) as it:
                for p in range(2):
                    body(it * 2 + p, p, 3)
            for e in range(E - 4, E):
                body(e, e % 2, min(3, E - 1 - e))

        @block.sync
        def _(sp):
            def load(e, p):
                sp.wait_ge(s("gu_split"), 4 * (e - 2)) if not least(e, 3) else None
                sp.dma_start(raw[p][0], a["expert_gu"][e]).then_inc(s(f"gu_loaded{p}"), 16)
                sp.wait_ge(s("d_split"), 2 * (e - 2)) if not least(e, 3) else None
                sp.dma_start(raw[p][1], a["expert_d"][e]).then_inc(s(f"d_loaded{p}"), 16)

            load(2, 0)
            load(3, 1)
            with sp.Fori(2, E // 2) as it:
                for p in range(2):
                    load(it * 2 + p, p)

        @block.tensor
        def _(pe):
            def list_tokens(e, p):
                pe.wait_ge(s("hot_ready"), e + 1)
                if not least(e, 1):
                    pe.wait_ge(s("ids_ready"), e)
                for i in range(TILES):
                    last = nc.tensor.matmul(list_b, slotid[p][:, i, :], hot[p][:, i, :], start=(i == 0),
                                            stop=(i == TILES - 1), skip_group_check=True)
                last.then_inc(s("listed"), 1)

            def flip_ids(e):
                pe.wait_ge(s("list_ready"), e + 1)
                nc.tensor.matmul(ids_b, listed[:, :], ident[0:3, 0:3], start=True, stop=True).then_inc(s("ids_done"), 1)

            def flip_rows(e, p, listed):
                pe.wait_ge(s("ids_ready"), listed)
                pe.wait_ge(s(f"got{p}"), 24 * (e - p) + 48)
                if not least(e, 2):
                    pe.wait_ge(s("y_ready"), 3 * e - 3)
                for k in range(2):
                    for b in range(3):
                        n = THIRDS[b]
                        last = nc.tensor.transpose(x_b[k][:, b * SLOTP:b * SLOTP + n],
                                                   got[p][0:n, b, k * MAIN:(k + 1) * MAIN], ident[0:n, 0:n])
                    last.then_inc(s("x_done"), 1)

            def gate_up(e, p, two):
                pe.wait_ge(s("x_ready"), 2 * e + 2)
                if not least(e, 1):
                    pe.wait_ge(s("gu_split"), 4 * e)
                wh, wl = hi[p][0], lo[p][0]
                for f in range(FET):
                    n = e * FET + f
                    w = slice(f * 128, (f + 1) * 128)
                    for g, b, read in ((0, gate_b, "gate_ready"), (1, up_b, "hid_ready")):
                        if not least(n, 2):
                            pe.wait_ge(s(read), n - 1)
                        b = b[f % 2][:, 0:CAP]
                        passes = ((wh[:, 0, g, w], x_hi[:, :]), (wl[:, 0, g, w], x_hi[:, :]), (wh[:, 0, g, w], x_lo[:, :]),
                                  (wh[:, 1, g, w], x_tail[:, :]), (wl[0:TAIL, 1, g, w], x_tail[0:TAIL, :]))
                        for i, (wt, xt) in enumerate(passes):
                            last = nc.tensor.matmul(b, wt, xt, start=(i == 0), stop=(i == len(passes) - 1),
                                                    skip_group_check=True)
                        last.then_inc(s("gate_done" if g == 0 else "up_done"), 1)
                    if two and f == 0:
                        list_tokens(e + 2, p)
                    if two and f == 3:
                        flip_ids(e + 2)

            def down(e, p, one):
                if not least(e, 1):
                    pe.wait_ge(s("d_split"), 2 * e)
                wh, wl = hi[p][1], lo[p][1]
                early, late = range(FET - 2), range(FET - 2, FET)
                for b, fs in ((0, early), (1, early), (0, late), (1, late), (2, range(FET))):
                    n = THIRDS[b]
                    slots = slice(b * SLOTP, b * SLOTP + n)
                    if fs[0] == 0 and not one:
                        pe.wait_ge(s("y_ready"), 3 * e - 2 + b)
                    if b == 2 and one:
                        pe.wait_ge(s("x_ready"), 2 * e + 4)
                    for f in fs:
                        if b == 0:
                            pe.wait_ge(s("hid_split"), FET * e + f + 1)
                        for i, (xt, wt) in enumerate(((hid_hi, wh), (hid_hi, wl), (hid_lo, wh))):
                            last = nc.tensor.matmul(down_b[b][0:n, :], xt[:, f, slots], wt[:, f, :],
                                                    start=(f == 0 and i == 0), stop=(f == FET - 1 and i == 2),
                                                    skip_group_check=True)
                    if fs[-1] == FET - 1:
                        last.then_inc(s("down_done"), 1)

            def body(e, p, after):
                gate_up(e, p, after >= 2)
                if after:
                    flip_rows(e + 1, 1 - p, e + 3 if after >= 2 else E)
                down(e, p, after > 0)

            for q in range(2):
                stay_awake(nc, t, bank[7], 8)
                list_tokens(q, q)
                flip_ids(q)
            stay_awake(nc, t, bank[7], 9)
            flip_rows(0, 0, 2)
            stay_awake(nc, t, bank[7], 6)
            experts(pe, body)

        @block.scalar
        def _(act):
            def round_hidden(n, f):
                act.wait_ge(s("hid_ready"), n + 1)
                nc.scalar.activation(hid_hi[:, f, :], hid[f % 2][:, :], ACT.Identity).then_inc(s("hid_rounded"), 1)

            def round_weights(e, p, j):
                if j < 4:
                    if j == 0:
                        if not least(e, 2):
                            act.wait_ge(s(f"gu_loaded{p}"), loads_of(e, p) - 16)
                            act.wait_ge(s("up_done"), FET * (e - 1))
                    part = (slice(None), j // 2, j % 2, slice(None))
                    nc.scalar.activation(hi[p][0][part], raw[p][0][part], ACT.Identity).then_inc(s("gu_rounded"), 1)
                else:
                    if j == 4 and not least(e, 2):
                        act.wait_ge(s(f"d_loaded{p}"), loads_of(e, p) - 16)
                        act.wait_ge(s("down_done"), 3 * (e - 1))
                    part = (slice(None), slice((j - 4) * 3, (j - 3) * 3), slice(None))
                    nc.scalar.activation(hi[p][1][part], raw[p][1][part], ACT.Identity).then_inc(s("d_rounded"), 1)

            def round_rows(e):
                for k, dst in enumerate((x_hi, x_tail)):
                    act.wait_ge(s("x_done"), 2 * e + k + 1)
                    if k == 0 and not least(e, 1):
                        act.wait_ge(s("up_done"), FET * e)
                    nc.scalar.activation(dst[:, :], x_b[k], ACT.Identity).then_inc(s("x_rounded"), 1)

            def body(e, p, after):
                for f in range(FET):
                    n = e * FET + f
                    act.wait_ge(s("gate_done"), n + 1)
                    if not least(n, 2):
                        act.wait_ge(s("hid_ready"), n - 1)
                    nc.scalar.activation(gate[f % 2][:, :], gate_b[f % 2][:, 0:CAP], ACT.Silu).then_inc(s("gate_ready"), 1)
                    if f > 0:
                        if f == 1 and not least(e, 1):
                            act.wait_ge(s("down_done"), 3 * e)
                        round_hidden(n - 1, f - 1)
                    if after and 0 < f < 4:
                        round_weights(e + 1, 1 - p, f)
                round_hidden(e * FET + FET - 1, FET - 1)
                if after:
                    round_rows(e + 1)
                    for j in (4, 5):
                        round_weights(e + 1, 1 - p, j)
                if not least(e, 2):
                    act.wait_ge(s(f"added{p}"), 24 * (e - p))
                act.wait_ge(s("score_kept"), e + 1)
                for b in range(3):
                    act.wait_ge(s("down_done"), 3 * e + b + 1)
                    if b == 2 and after >= 2:
                        round_weights(e + 2, p, 0)
                    n = THIRDS[b]
                    nc.scalar.activation(y[p][0:n, b, :], down_b[b][0:n, :], ACT.Identity,
                                         scale=score[p][0:n, b:b + 1]).then_inc(s("y_ready"), 1)

            round_rows(0)
            round_weights(1, 1, 0)
            experts(act, body)

        @block.vector
        def _(dve):
            def one_hot(e, p):
                if not least(e, 2):
                    dve.wait_ge(s("listed"), e - 1)
                nc.vector.tensor_copy(slotid[p][:, :, :], t["slotid"][:, bass.ds(e, 1)].rearrange("p o i b -> p (o i) b"))
                col = t["slotp"][:, bass.ds(e * TILES, TILES)]
                nc.vector.tensor_tensor(hot[p][:, :, :], t["iota"].unsqueeze(1).broadcast_to([TT, TILES, SLOTP]),
                                        col.unsqueeze(2).broadcast_to([TT, TILES, SLOTP]),
                                        ALU.is_equal).then_inc(s("hot_ready"), 1)

            def keep_list(e):
                dve.wait_ge(s("listed"), e + 1)
                nc.vector.tensor_copy(listed[:, :], list_b).then_inc(s("list_ready"), 1)

            def token_ids(e, p):
                dve.wait_ge(s("ids_done"), e + 1)
                if not least(e, 2):
                    dve.wait_ge(s(f"got{p}"), 24 * (e - p))
                nc.vector.tensor_scalar(ids[p][:, :], ids_b, float(IDMID), None, ALU.add).then_inc(s("ids_ready"), 1)

            def keep_score(e, p):
                dve.wait_ge(s(f"got{p}"), 24 * (e - p) + 48)
                if not least(e, 2):
                    dve.wait_ge(s("y_ready"), 3 * e - 3)
                    dve.wait_ge(s(f"added{p}"), 24 * (e - p))
                nc.vector.tensor_copy(ids_out[p][:, :], ids[p][:, :])
                nc.vector.tensor_copy(score[p][:, 0:2],
                                      got[p][:, 0:2, bass.ds(e + TURN, 1)].rearrange("p b o -> p (b o)"))
                nc.vector.tensor_copy(score[p][0:THIRDS[2], 2:3],
                                      got[p][0:THIRDS[2], 2, bass.ds(e + TURN, 1)]).then_inc(s("score_kept"), 1)

            def split_rows(e):
                dve.wait_ge(s("x_rounded"), 2 * e + 1)
                nc.vector.tensor_tensor(x_lo[:, :], x_b[0], x_hi[:, :].bitcast(FP32),
                                        ALU.subtract).then_inc(s("x_ready"), 1)
                dve.wait_ge(s("x_rounded"), 2 * e + 2)
                nc.vector.tensor_tensor(x_tail[TAIL:, :], x_b[1][TAIL:, :], x_tail[TAIL:, :].bitcast(FP32),
                                        ALU.subtract).then_inc(s("x_ready"), 1)

            def split_weights(e, p, j):
                dve.wait_ge(s("gu_rounded"), 4 * e - 3 + j)
                part = (slice(0, 128 if j < 2 else TAIL), j // 2, j % 2, slice(None))
                nc.vector.tensor_tensor(lo[p][0][part], raw[p][0][part], hi[p][0][part].bitcast(FP32),
                                        ALU.subtract).then_inc(s("gu_split"), 1)

            def split_hidden(n, f):
                dve.wait_ge(s("hid_rounded"), n + 1)
                nc.vector.tensor_tensor(hid_lo[:, f, :], hid[f % 2][:, :], hid_hi[:, f, :].bitcast(FP32),
                                        ALU.subtract).then_inc(s("hid_split"), 1)

            def body(e, p, after):
                for f in range(FET):
                    n = e * FET + f
                    dve.wait_ge(s("gate_ready"), n + 1)
                    dve.wait_ge(s("up_done"), n + 1)
                    if not least(n, 2):
                        dve.wait_ge(s("hid_split"), n - 1)
                    nc.vector.tensor_tensor(hid[f % 2][:, :], gate[f % 2][:, :], up_b[f % 2][:, 0:CAP],
                                            ALU.mult).then_inc(s("hid_ready"), 1)
                    if f > 0:
                        split_hidden(n - 1, f - 1)
                    if after and f == 1:
                        split_weights(e + 1, 1 - p, 1)
                    if f == 1 and after >= 2:
                        keep_list(e + 2)
                    if f == 3 and after >= 2:
                        token_ids(e + 2, p)
                split_hidden(e * FET + FET - 1, FET - 1)
                if after:
                    split_rows(e + 1)
                    for j in (2, 3):
                        split_weights(e + 1, 1 - p, j)
                if after == 3:
                    one_hot(e + 3, 1 - p)
                if after:
                    keep_score(e + 1, 1 - p)
                if after >= 2:
                    split_weights(e + 2, p, 0)

            one_hot(0, 0)
            keep_list(0)
            token_ids(0, 0)
            one_hot(1, 1)
            keep_list(1)
            token_ids(1, 1)
            one_hot(2, 0)
            keep_score(0, 0)
            split_rows(0)
            split_weights(1, 1, 0)
            experts(dve, body)

        @block.gpsimd
        def _(pool):
            def gather(e, p):
                pool.wait_ge(s("ids_ready"), e + 1)
                if not least(e, 2):
                    pool.wait_ge(s("score_kept"), e - 1)
                    pool.wait_ge(s("x_done"), 2 * (e - 1))
                pool.sem_inc(s("gathers"), 1)
                for b in range(3):
                    n = THIRDS[b]
                    nc.gpsimd.indirect_dma_start(
                        out=got[p][0:n, b, :], out_offset=None, in_=table,
                        in_offset=bass.IndirectOffsetOnAxis(ap=ids[p][0:n, b:b + 1], axis=0)).then_inc(s(f"got{p}"), 16)

            def add(e, p):
                pool.wait_ge(s("y_ready"), 3 * e + 3)
                if not least(e, 1):
                    pool.wait_ge(s(f"added{1 - p}"), 24 * (e - p) + 48 * p)
                pool.sem_inc(s("adds"), 1)
                for b in range(3):
                    n = THIRDS[b]
                    nc.gpsimd.indirect_dma_start(
                        out=out, out_offset=bass.IndirectOffsetOnAxis(ap=ids_out[p][0:n, b:b + 1], axis=0),
                        in_=y[p][0:n, b, :], in_offset=None, compute_op=ALU.add).then_inc(s(f"added{p}"), 16)

            def split_down(e, p):
                for j in range(2):
                    pool.wait_ge(s("d_rounded"), 2 * e - 1 + j)
                    part = (slice(None), slice(j * 3, (j + 1) * 3), slice(None))
                    nc.gpsimd.tensor_tensor(lo[p][1][part], raw[p][1][part], hi[p][1][part].bitcast(FP32),
                                            ALU.subtract).then_inc(s("d_split"), 1)

            def body(e, p, after):
                if after >= 2:
                    gather(e + 2, p)
                if after:
                    split_down(e + 1, 1 - p)
                add(e, p)

            gather(0, 0)
            gather(1, 1)
            experts(pool, body)
            for p in range(2):
                pool.wait_ge(s(f"added{p}"), 16 * 3 * E // 2)


def tower(nc, a, table, out):
    with ExitStack() as ctx:
        def sb(ctx, name, shape, dt=FP32):
            return ctx.enter_context(nc.sbuf_tensor(name, shape, dt))[tuple(slice(None) for _ in shape)]

        def const(ctx, *names):
            for name in names:
                t[name] = sb(ctx, "s_" + name, list(a[name].shape), a[name].dtype)

        psum = ctx.enter_context(nc.psum_tensor("psum", [128, 8 * 512], FP32))
        t = {
            "psum": psum,
            "table_out": ctx.enter_context(nc.semaphore("table_out")),
            "base_out": [ctx.enter_context(nc.semaphore(f"base_out{p}")) for p in range(2)],
            "bank": [psum[:, 512 * i:512 * (i + 1)] for i in range(8)],
            "slotp": sb(ctx, "slotp", [TT, E * TILES], FP16),
            "slotid": sb(ctx, "slotid", [TT, E, TILES, 3], FP16),
        }
        const(ctx, "ident", "iota", "ones")
        for q in range(2):
            t[f"gu_raw{q}"] = sb(ctx, f"gu_raw{q}", [128, 2, 2, FE])
            t[f"d_raw{q}"] = sb(ctx, f"d_raw{q}", [128, FET, D])

        def parts(ctx, q):
            for kind in ("hi", "lo"):
                t[f"gu_{kind}{q}"] = sb(ctx, f"gu_{kind}{q}", [128, 2, 2, FE], FP32R)
                t[f"d_{kind}{q}"] = sb(ctx, f"d_{kind}{q}", [128, FET, D], FP32R)

        parts(ctx, 0)
        with ExitStack() as dense:
            t["hT"] = sb(dense, "hT", [DP, DK, TOK])
            t["xnT"] = sb(dense, "xnT", [DP, DK, TOK])
            t["limit"] = sb(dense, "limit", [TT, E], U32)
            const(dense, "bias", "avg", "headmask", "clsmask", "attn_w", "gate_w", "shared_gu", "shared_d", "bitf",
                  "bitu", "before", "ids", "restart")
            embed_stage(nc, t, a)
            attention_stage(nc, t, a)
            for kind in ("hi", "lo"):
                t["xn_" + kind] = sb(dense, "xn_" + kind, [DP, DK, TOK], FP32R)
                t["shared_" + kind] = sb(dense, "shared_" + kind, [DP, 2, DK, FS], FP32R)
            t["rows"] = sb(dense, "rows", [TT, TILES, ROW])
            table_stage(nc, t, a, table)
            shared_stage(nc, t, a, out)
            slot_stage(nc, t, a)
        parts(ctx, 1)
        expert_stage(nc, t, a, table, out)


def layouts(x, cls_tok, L0_tok_w, L0_tok_b, L0_attn_wq, L0_attn_bq, L0_attn_wk, L0_attn_bk, L0_attn_wv, L0_attn_bv,
            L0_attn_ww, L0_attn_bw, L0_ffn_gate_weight, L0_ffn_Wg, L0_ffn_Wu, L0_ffn_Wd, L0_ffn_Ws_g, L0_ffn_Ws_u,
            L0_ffn_Ws_d):
    import numpy as np

    def halves(m):
        return np.asarray(m).T.reshape(DK, DP, -1).transpose(1, 0, 2)

    def turned(m):
        m = np.asarray(m).transpose(0, 2, 1)
        return np.stack([m[:, :MAIN], np.concatenate([m[:, MAIN:], m[:, MAIN:]], 1)], 2)

    def blocks(m):
        return np.asarray(m).T.reshape(-1, 128, D).transpose(1, 0, 2)

    P = 32
    patches = np.asarray(x).reshape(CHUNKS, GI, 8, P, 8, P).transpose(0, 3, 5, 1, 2, 4)
    patches = patches.reshape(CHUNKS, PK, 128, CP).transpose(0, 2, 1, 3)
    bias = np.zeros((DP, DK, 8), np.float32)
    for n, v in enumerate((L0_tok_b, L0_attn_bq, L0_attn_bk, L0_attn_bv, L0_attn_bw, cls_tok)):
        bias[:, :, n] = np.asarray(v).reshape(DK, DP).T
    bias[:, :, 6] = EPS
    at = np.arange(128)
    bits = [1 << (BITS - 1 - n) for n in range(BITS)] + [0]
    restart = np.ones((TT, E, TILES), np.float32)
    restart[:, :, 0] = 0
    tt = np.arange(TT)
    return {
        "patches": patches,
        "tok_w": np.asarray(L0_tok_w).T.reshape(PK, 128, D).transpose(1, 0, 2),
        "bias": bias,
        "attn_w": np.stack([halves(m) for m in (L0_attn_wq, L0_attn_wk, L0_attn_wv, L0_attn_ww)], 1),
        "gate_w": halves(L0_ffn_gate_weight),
        "shared_gu": np.stack([halves(L0_ffn_Ws_g), halves(L0_ffn_Ws_u)], 1),
        "shared_d": blocks(L0_ffn_Ws_d),
        "expert_gu": np.stack([turned(m) for m in (L0_ffn_Wg, L0_ffn_Wu)], 3),
        "expert_d": np.asarray(L0_ffn_Wd).transpose(0, 2, 1).reshape(E, FET, 128, D).transpose(0, 2, 1, 3),
        "avg": np.full((DP, DP), 1 / D, np.float32),
        "ident": np.eye(128, dtype=np.float32),
        "headmask": (np.arange(DP)[:, None] // HD == np.arange(HH)).astype(np.float32),
        "clsmask": np.concatenate([np.eye(32, HEADS, dtype=np.float32)] * 3)[:CROWS],
        "ones": np.ones((128, 128), np.float16),
        "before": -(tt[:, None] >= tt[None, :]).astype(np.float16),
        "iota": np.tile(np.arange(SLOTP, dtype=np.float16), (TT, 1)),
        "ids": (np.arange(TILES)[None, :] * TT + tt[:, None] - IDMID).astype(np.float16),
        "restart": restart.reshape(TT, -1),
        "bitf": np.tile(np.array(bits[:-1], np.float32), (TT, 1)),
        "bitu": np.tile(np.array(bits[1:], np.uint32), (TT, 1)),
    }


def kernel(**inputs):
    import numpy as np
    import concourse.bacc as bacc
    from concourse.bass_utils import run_bass_kernel_spmd

    nc = bacc.Bacc("TRN2", target_bir_lowering=False, num_devices=1)
    arrays, a = {}, {}
    for name, v in layouts(**inputs).items():
        arrays[name + "_in"] = v = np.ascontiguousarray(v)
        a[name] = nc.dram_tensor(name + "_in", v.shape, mybir.dt.from_np(v.dtype), kind="ExternalInput").ap()
    table = nc.dram_tensor("table", (TOK, ROW), FP32, kind="Internal").ap()
    out = nc.dram_tensor("y_out", (TOK, D), FP32, kind="ExternalOutput").ap()
    tower(nc, a, table, out)
    r = run_bass_kernel_spmd(nc, [arrays], core_ids=[0])
    return r.results[0]["y_out"].reshape(IMGS, SEQ, D)
```
